# Optimizing a Trainium2 kernel written in Bass

```python
import numpy as np
import jax
import jax.numpy as jnp

def _softmax(x, axis=-1):
    return jax.nn.softmax(x, axis=axis)

def _gelu(x):
    return jax.nn.gelu(x, approximate=True)

def _silu(x):
    return jax.nn.silu(x)

def _sigmoid(x):
    return jax.nn.sigmoid(x)

def _layernorm(x, axis=-1, eps=1e-05):
    m = jnp.mean(x, axis=axis, keepdims=True)
    v = jnp.var(x, axis=axis, keepdims=True)
    return (x - m) / jnp.sqrt(v + eps)

def _scatter_add(tgt, idx, src, axis=0):
    return tgt.at[idx].add(src)

def _segment_sum(src, seg, n):
    return jax.ops.segment_sum(src, seg, n)
kernel_name = 'mk_gnn_ffn_d2_gnn_r8_5fb8da'

def setup_inputs(seed: int=0):
    np.random.seed(seed)
    _w = jnp.asarray

    def _rec_inputs():
        import jax
        import jax.numpy as jnp
        _gk = jax.random.key(seed)
        x = -0.0003713 + 1 * jax.random.normal(jax.random.fold_in(_gk, 1), (6250, 256), jnp.float32)
        src = jax.random.randint(jax.random.fold_in(_gk, 2), (100000,), 0, 6250, jnp.int32)
        dst = jax.random.randint(jax.random.fold_in(_gk, 3), (100000,), 0, 6250, jnp.int32)
        _o = jnp.argsort(dst, stable=True)
        src = src[_o]
        dst = dst[_o]
        return (x, src, dst)
    x, src, dst = _rec_inputs()

    def _L0_gnn_setup():
        import jax, jax.numpy as jnp
        import numpy as np
        N, IN_CH, HEADS, OUT_CH, E = (6250, 256, 4, 64, 100000)
        key = jax.random.key(seed)
        k1, k2, k3, k4, k5 = jax.random.split(key, 5)
        x = jax.random.normal(k1, (N, IN_CH), dtype=jnp.float32)
        edge_index = jax.random.randint(k2, (2, E), 0, N, dtype=jnp.int64)
        bw = float(np.sqrt(6.0 / (IN_CH + HEADS * OUT_CH)))
        ba = float(np.sqrt(6.0 / (HEADS + OUT_CH)))
        weight = jax.random.uniform(k3, (IN_CH, HEADS * OUT_CH), jnp.float32, -bw, bw)
        attn_l = jax.random.uniform(k4, (HEADS, OUT_CH), jnp.float32, -ba, ba)
        attn_r = jax.random.uniform(k5, (HEADS, OUT_CH), jnp.float32, -ba, ba)
        return {'x': x, 'edge_index': edge_index, 'weight': weight, 'attn_l': attn_l, 'attn_r': attn_r}
    _L0_gnn_all = _L0_gnn_setup()
    _L0_gnn_in = {k: v for k, v in _L0_gnn_all.items() if k in ('weight', 'attn_l', 'attn_r')}
    del _L0_gnn_all

    def _L0_ffn_setup():
        import jax, jax.numpy as jnp
        import numpy as np
        E, D, H, TOP_K = (6, 256, 256, 2)
        ROUTER_H = D // 2
        key = jax.random.key(seed)
        ks = jax.random.split(key, 12)
        s = 1.0 / np.sqrt(D)
        sh = 1.0 / np.sqrt(H)
        sr = 1.0 / np.sqrt(ROUTER_H)
        return {'features': jax.random.normal(ks[0], (8, 512, D), dtype=jnp.float32), 'router_w1': jax.random.uniform(ks[1], (D, ROUTER_H), jnp.float32, -s, s), 'router_b1': jnp.zeros((ROUTER_H,), jnp.float32), 'router_w2': jax.random.uniform(ks[2], (ROUTER_H, E), jnp.float32, -sr, sr), 'router_b2': jnp.zeros((E,), jnp.float32), 'expert_w1': jax.random.uniform(ks[3], (E, D, H), jnp.float32, -s, s), 'expert_b1': jnp.zeros((E, H), jnp.float32), 'expert_w2': jax.random.uniform(ks[4], (E, H, H), jnp.float32, -sh, sh), 'expert_b2': jnp.zeros((E, H), jnp.float32), 'expert_w3': jax.random.uniform(ks[5], (E, H, D), jnp.float32, -sh, sh), 'expert_b3': jnp.zeros((E, D), jnp.float32)}
    _L0_ffn_all = _L0_ffn_setup()
    _L0_ffn_in = {k: v for k, v in _L0_ffn_all.items() if k in ('router_w1', 'router_b1', 'router_w2', 'router_b2', 'expert_w1', 'expert_b1', 'expert_w2', 'expert_b2', 'expert_w3', 'expert_b3')}
    del _L0_ffn_all

    def _L1_gnn_setup():
        import jax, jax.numpy as jnp
        import numpy as np
        N, E = (6250, 100000)
        IN_C, HEADS, OUT_C = (256, 4, 64)
        NEG_SLOPE = 0.2

        def _gat_forward(x, W, att_src, att_dst, bias, edge_index):
            n = x.shape[0]
            loop = jnp.arange(n, dtype=edge_index.dtype)
            src = jnp.concatenate([edge_index[0], loop])
            dst = jnp.concatenate([edge_index[1], loop])
            h = (x @ W).reshape(n, HEADS, OUT_C)
            a_src = jnp.einsum('nhc,hc->nh', h, att_src)
            a_dst = jnp.einsum('nhc,hc->nh', h, att_dst)
            e = a_src[src] + a_dst[dst]
            e = jnp.where(e > 0, e, NEG_SLOPE * e)
            m = jax.ops.segment_max(e, dst, num_segments=n)
            m = jnp.where(jnp.isfinite(m), m, 0.0)
            ex = jnp.exp(e - m[dst])
            denom = jax.ops.segment_sum(ex, dst, num_segments=n)
            alpha = ex / (denom[dst] + 1e-16)
            msg = alpha[:, :, None] * h[src]
            out = jax.ops.segment_sum(msg, dst, num_segments=n)
            out = out.reshape(n, HEADS * OUT_C) + bias
            return jax.nn.relu(out)
        key = jax.random.key(seed)
        k1, k2, k3, k4, k5, k6 = jax.random.split(key, 6)
        x = jax.random.normal(k1, (N, IN_C), dtype=jnp.float32)
        edge_index = jax.random.randint(k2, (2, E), 0, N, dtype=jnp.int32)
        W = jax.random.normal(k3, (IN_C, HEADS * OUT_C), dtype=jnp.float32) / np.sqrt(IN_C)
        att_src = jax.random.normal(k4, (HEADS, OUT_C), dtype=jnp.float32) / np.sqrt(OUT_C)
        att_dst = jax.random.normal(k5, (HEADS, OUT_C), dtype=jnp.float32) / np.sqrt(OUT_C)
        bias = jax.random.normal(k6, (HEADS * OUT_C,), dtype=jnp.float32) * 0.01
        return {'x': x, 'edge_index': edge_index, 'W': W, 'att_src': att_src, 'att_dst': att_dst, 'bias': bias}
    _L1_gnn_all = _L1_gnn_setup()
    _L1_gnn_in = {k: v for k, v in _L1_gnn_all.items() if k in ('W', 'att_src', 'att_dst', 'bias')}
    del _L1_gnn_all

    def _L1_ffn_setup():
        import jax, jax.numpy as jnp
        import numpy as np
        TOP_K = 2
        key = jax.random.key(seed)
        ks = jax.random.split(key, 4)
        B, L, D, H, E = (8, 512, 256, 1024, 8)
        s = 0.02
        return {'x': jax.random.normal(ks[0], (B, L, D), jnp.float32), 'Wg': jax.random.normal(ks[1], (D, E), jnp.float32) * s, 'bg': jnp.zeros((E,), jnp.float32), 'W1': jax.random.normal(ks[2], (E, D, H), jnp.float32) * s, 'b1': jnp.zeros((E, H), jnp.float32), 'W2': jax.random.normal(ks[3], (E, H, D), jnp.float32) * s, 'b2': jnp.zeros((E, D), jnp.float32)}
    _L1_ffn_all = _L1_ffn_setup()
    _L1_ffn_in = {k: v for k, v in _L1_ffn_all.items() if k in ('Wg', 'bg', 'W1', 'b1', 'W2', 'b2')}
    del _L1_ffn_all
    return {'x': x, 'src': src, 'dst': dst, 'L0_gnn_weight': _L0_gnn_in['weight'], 'L0_gnn_attn_l': _L0_gnn_in['attn_l'], 'L0_gnn_attn_r': _L0_gnn_in['attn_r'], 'L0_ffn_router_w1': _L0_ffn_in['router_w1'], 'L0_ffn_router_b1': _L0_ffn_in['router_b1'], 'L0_ffn_router_w2': _L0_ffn_in['router_w2'], 'L0_ffn_router_b2': _L0_ffn_in['router_b2'], 'L0_ffn_expert_w1': _L0_ffn_in['expert_w1'], 'L0_ffn_expert_b1': _L0_ffn_in['expert_b1'], 'L0_ffn_expert_w2': _L0_ffn_in['expert_w2'], 'L0_ffn_expert_b2': _L0_ffn_in['expert_b2'], 'L0_ffn_expert_w3': _L0_ffn_in['expert_w3'], 'L0_ffn_expert_b3': _L0_ffn_in['expert_b3'], 'L1_gnn_W': _L1_gnn_in['W'], 'L1_gnn_att_src': _L1_gnn_in['att_src'], 'L1_gnn_att_dst': _L1_gnn_in['att_dst'], 'L1_gnn_bias': _L1_gnn_in['bias'], 'L1_ffn_Wg': _L1_ffn_in['Wg'], 'L1_ffn_bg': _L1_ffn_in['bg'], 'L1_ffn_W1': _L1_ffn_in['W1'], 'L1_ffn_b1': _L1_ffn_in['b1'], 'L1_ffn_W2': _L1_ffn_in['W2'], 'L1_ffn_b2': _L1_ffn_in['b2']}

def reference(x, src, dst, L0_gnn_weight, L0_gnn_attn_l, L0_gnn_attn_r, L0_ffn_router_w1, L0_ffn_router_b1, L0_ffn_router_w2, L0_ffn_router_b2, L0_ffn_expert_w1, L0_ffn_expert_b1, L0_ffn_expert_w2, L0_ffn_expert_b2, L0_ffn_expert_w3, L0_ffn_expert_b3, L1_gnn_W, L1_gnn_att_src, L1_gnn_att_dst, L1_gnn_bias, L1_ffn_Wg, L1_ffn_bg, L1_ffn_W1, L1_ffn_b1, L1_ffn_W2, L1_ffn_b2):
    import jax
    import jax.numpy as jnp

    def _L0_gnn_ref(x, edge_index, weight, attn_l, attn_r):
        import jax, jax.numpy as jnp
        import numpy as np
        N, IN_CH, HEADS, OUT_CH, E = (6250, 256, 4, 64, 100000)
        heads, out_ch = attn_l.shape
        n = x.shape[0]
        xt = jnp.matmul(x, weight).reshape(-1, heads, out_ch)
        row, col = (edge_index[0], edge_index[1])
        alpha_l = jnp.einsum('ehd,hd->eh', xt[row], attn_l)
        alpha_r = jnp.einsum('ehd,hd->eh', xt[col], attn_r)
        alpha = jax.nn.softmax(jax.nn.leaky_relu(alpha_l + alpha_r, 0.01), axis=1)
        tmp = jnp.einsum('nh,nhd->nd', alpha[:n], xt[col[:n]])
        out = jnp.broadcast_to(tmp[:, None, :], (n, heads, out_ch))
        return out.reshape(n, heads * out_ch)

    def _L0_ffn_ref(features, router_w1, router_b1, router_w2, router_b2, expert_w1, expert_b1, expert_w2, expert_b2, expert_w3, expert_b3):
        import jax, jax.numpy as jnp
        import numpy as np
        E, D, H, TOP_K = (6, 256, 256, 2)
        ROUTER_H = D // 2
        rh = jax.nn.relu(features @ router_w1 + router_b1)
        expert_logits = jax.nn.softmax(rh @ router_w2 + router_b2, axis=-1)
        top_w, top_i = jax.lax.top_k(expert_logits, TOP_K)
        routing_weights = jax.nn.softmax(top_w, axis=-1)
        h1 = jax.nn.relu(jnp.einsum('bsd,edh->bseh', features, expert_w1) + expert_b1)
        h2 = jax.nn.relu(jnp.einsum('bseh,ehf->bsef', h1, expert_w2) + expert_b2)
        expert_out = jnp.einsum('bsef,efo->bseo', h2, expert_w3) + expert_b3
        sel = jnp.take_along_axis(expert_out, top_i[:, :, :, None], axis=2)
        combined = jnp.sum(sel * routing_weights[..., None], axis=2)
        return combined

    def _L1_gnn_ref(x, edge_index, W, att_src, att_dst, bias):
        import jax, jax.numpy as jnp
        import numpy as np
        N, E = (6250, 100000)
        IN_C, HEADS, OUT_C = (256, 4, 64)
        NEG_SLOPE = 0.2

        def _gat_forward(x, W, att_src, att_dst, bias, edge_index):
            n = x.shape[0]
            loop = jnp.arange(n, dtype=edge_index.dtype)
            src = jnp.concatenate([edge_index[0], loop])
            dst = jnp.concatenate([edge_index[1], loop])
            h = (x @ W).reshape(n, HEADS, OUT_C)
            a_src = jnp.einsum('nhc,hc->nh', h, att_src)
            a_dst = jnp.einsum('nhc,hc->nh', h, att_dst)
            e = a_src[src] + a_dst[dst]
            e = jnp.where(e > 0, e, NEG_SLOPE * e)
            m = jax.ops.segment_max(e, dst, num_segments=n)
            m = jnp.where(jnp.isfinite(m), m, 0.0)
            ex = jnp.exp(e - m[dst])
            denom = jax.ops.segment_sum(ex, dst, num_segments=n)
            alpha = ex / (denom[dst] + 1e-16)
            msg = alpha[:, :, None] * h[src]
            out = jax.ops.segment_sum(msg, dst, num_segments=n)
            out = out.reshape(n, HEADS * OUT_C) + bias
            return jax.nn.relu(out)
        return _gat_forward(x, W, att_src, att_dst, bias, edge_index)

    def _L1_ffn_ref(x, Wg, bg, W1, b1, W2, b2):
        import jax, jax.numpy as jnp
        import numpy as np
        TOP_K = 2
        B, L, D = x.shape
        E = W1.shape[0]
        xf = x.reshape(-1, D)
        gate_logits = xf @ Wg + bg
        top_w, top_i = jax.lax.top_k(gate_logits, TOP_K)
        top_w = jax.nn.softmax(top_w, axis=-1)
        w_dense = jnp.sum(jax.nn.one_hot(top_i, E, dtype=xf.dtype) * top_w[..., None], axis=1)
        out = jnp.zeros_like(xf)
        for e in range(E):
            h = jax.nn.gelu(xf @ W1[e] + b1[e], approximate=False)
            out = out + w_dense[:, e:e + 1] * (h @ W2[e] + b2[e])
        return out.reshape(B, L, D)
    edge_index = jnp.stack([src, dst])
    x = x + _L0_gnn_ref(_layernorm(x, axis=-1), edge_index, L0_gnn_weight, L0_gnn_attn_l, L0_gnn_attn_r)
    x = x + _L0_ffn_ref(_layernorm(x, axis=-1)[None], L0_ffn_router_w1, L0_ffn_router_b1, L0_ffn_router_w2, L0_ffn_router_b2, L0_ffn_expert_w1, L0_ffn_expert_b1, L0_ffn_expert_w2, L0_ffn_expert_b2, L0_ffn_expert_w3, L0_ffn_expert_b3)[0]
    x = x + _L1_gnn_ref(_layernorm(x, axis=-1), edge_index, L1_gnn_W, L1_gnn_att_src, L1_gnn_att_dst, L1_gnn_bias)
    x = x + _L1_ffn_ref(_layernorm(x, axis=-1)[None], L1_ffn_Wg, L1_ffn_bg, L1_ffn_W1, L1_ffn_b1, L1_ffn_W2, L1_ffn_b2)[0]
    return x

_drawn_inputs = setup_inputs


def setup_inputs(seed=0):
    import zlib

    import numpy as np

    out = dict(_drawn_inputs(seed))
    spreads = {'L0_ffn_router_b1': (0.0, 0.1),
     'L0_ffn_router_b2': (0.0, 0.1),
     'L0_ffn_expert_b1': (0.0, 0.587),
     'L0_ffn_expert_b2': (0.0, 0.29),
     'L0_ffn_expert_b3': (0.0, 0.1),
     'L1_ffn_bg': (0.0, 0.1),
     'L1_ffn_b1': (0.0, 0.385),
     'L1_ffn_b2': (0.0, 0.1)}
    factors = {'L1_gnn_bias': 7.234}
    for name, (base, spread) in spreads.items():
        noise = np.random.default_rng([zlib.crc32(name.encode()), seed]).standard_normal(out[name].shape)
        drawn = base * np.exp(spread * noise) if base else spread * noise
        out[name] = jnp.asarray(drawn.astype(out[name].dtype))
    for name, factor in factors.items():
        out[name] = (out[name] * factor).astype(out[name].dtype)
    return out
```

```python
import concourse.bass as bass
from concourse import mybir
from contextlib import ExitStack

F32 = mybir.dt.float32
I32 = mybir.dt.int32
BF16 = mybir.dt.bfloat16
ALU = mybir.AluOpType
ACT = mybir.ActivationFunctionType
AX = mybir.AxisListType

P = 128
NODES, DIM = 6250, 256
EDGES = 100000
HEADS, CH = 4, 64
TILES = -(-NODES // P)
TAIL = NODES - (TILES - 1) * P
BODY = 7
TRIPS = TILES // BODY
assert TRIPS * BODY == TILES
KC = DIM // P
EPS = 1e-5

MT = 256
SUB = MT // P
E0, H0, R0 = 6, 256, 128
E1, H1 = 8, 1024
NT0 = (2 * NODES) // MT + E0
NT1 = (2 * NODES) // MT + E1
NT0 += NT0 % 2
NT1 += NT1 % 2
SLOTS = max(NT0, NT1) * MT

CHUNKS = (6, 6, 5)
OFFS = (0, 6 * P, 12 * P)
SE = sum(CHUNKS) * P
GRAN = 32
NGRAN = EDGES // GRAN
EROWS = 125
ECOLS = EDGES // EROWS
GPR = ECOLS // GRAN
SEG = SE // GRAN
MAXSTEPS = -(-NGRAN // SEG)
HUGE = 1.0e30


class Shared:
    pass


def lift(eng, sems):
    for s in sems:
        eng.sem_inc(s, 1)


def freed(eng, sem, n):
    eng.wait_ge(sem, n + 1)


class Chain:

    def __init__(self, eng, sem, base=0):
        self.eng, self.sem, self.base, self.n = eng, sem, base, 0

    def mark(self, ins):
        self.n += 1
        ins.then_inc(self.sem, 1)

    def settle(self):
        self.eng.wait_ge(self.sem, self.base + self.n)

    def link(self, ins):
        self.mark(ins)
        self.settle()


def gnn_moe(nc, out, x, src, dst, L0_gnn_weight, L0_gnn_attn_l, L0_gnn_attn_r, L0_ffn_router_w1, L0_ffn_router_b1, L0_ffn_router_w2, L0_ffn_router_b2, L0_ffn_expert_w1, L0_ffn_expert_b1, L0_ffn_expert_w2, L0_ffn_expert_b2, L0_ffn_expert_w3, L0_ffn_expert_b3, L1_gnn_W, L1_gnn_att_src, L1_gnn_att_dst, L1_gnn_bias, L1_ffn_Wg, L1_ffn_bg, L1_ffn_W1, L1_ffn_b1, L1_ffn_W2, L1_ffn_b2, upto=99):
    with ExitStack() as whole:
        K = Shared()
        K.nc = nc

        def tools(stack, tag):
            def sb(name, shape, dt=F32):
                return stack.enter_context(nc.sbuf_tensor(f"{tag}_{name}", shape, dt))

            def pb(name, shape, dt=F32):
                return stack.enter_context(nc.psum_tensor(f"{tag}_{name}", shape, dt))

            used = []

            def sem(name):
                used.append(stack.enter_context(nc.semaphore(f"{tag}_{name}")))
                return used[-1]

            def clear():
                with nc.Block() as block:
                    @block.gpsimd
                    def _(gp):
                        for s in used:
                            gp.sem_clear(s)

            stack.callback(clear)
            return sb, pb, sem

        K.tools = tools
        sb, pb, sem = tools(whole, "g")

        def dram(name, shape, dt=F32):
            return nc.dram_tensor(name, shape, dt, kind="Internal").ap()

        K.T0 = dram("xt_ar", [TILES * P, DIM + 4])
        K.AL = dram("al", [TILES * P, 4])
        K.T1 = dram("h_as", [TILES * P, DIM + 4])
        K.XS = dram("slot_rows", [SLOTS + 2 * P, DIM])
        K.YS = dram("slot_out", [SLOTS + 2 * P, DIM])
        K.SRCP = dram("src_padded", [EDGES + SE], I32)
        K.DSTP = dram("dst_padded", [EDGES + SE])
        K.GR = dram("granule_range", [2, NGRAN])
        K.RT = dram("tile_range", [TILES, 2])

        K.X = sb("x", [P, TILES, DIM])
        K.Y = sb("y", [P, TILES, DIM])
        K.ident = sb("ident", [P, P])
        K.iota = sb("iota", [P, 512])
        K.pid = sb("pid", [P, 1])
        K.valid = sb("valid", [P, 1])
        K.vdump = sb("vdump", [P, 2])
        K.vneg = sb("vneg", [P, 1])
        K.eps = sb("eps", [P, 1])
        K.tri = sb("tri", [P, P], BF16)
        K.ones = sb("ones", [P, P], BF16)
        K.onesf = sb("onesf", [P, TILES])
        K.LG = sb("logits", [P, TILES, 8])
        K.POS = sb("slot_of", [P, TILES, 2], I32)
        K.WT = sb("weight_of", [P, TILES, 2])
        K.TE = sb("expert_of", [P, max(NT0, NT1)], I32)
        K.ET = sb("edge_steps", [1, TILES, 3], I32)
        K.AD = sb("as_ad", [P, TILES, 8])

        K.dstI = sb("dst_first", [P, TILES], I32)
        K.srcI = sb("src_first", [P, TILES], I32)

        setup(K, x, src, dst)
        edge_ranges(K)
        project(K, "a0", None, gat_weights=(L0_gnn_weight, L0_gnn_attn_r, L0_gnn_attn_l))
        if upto > 0:
            project(K, "a1", "attn0", router=(L0_ffn_router_w1, L0_ffn_router_b1, L0_ffn_router_w2, L0_ffn_router_b2))
        if upto > 1:
            route(K, "r0", E0, NT0, True)
            experts(K, "e0", E0, NT0, L0_ffn_expert_w1, L0_ffn_expert_b1, H0, ACT.Relu,
                    L0_ffn_expert_w2, L0_ffn_expert_b2, L0_ffn_expert_w3, L0_ffn_expert_b3)
        if upto > 2:
            project(K, "b0", "combine", gat_weights=(L1_gnn_W, L1_gnn_att_src, L1_gnn_att_dst))
        if upto > 3:
            attention(K, L1_gnn_bias)
        if upto > 4:
            project(K, "b1", None, gate=(L1_ffn_Wg, L1_ffn_bg))
            route(K, "r1", E1, NT1, False)
            experts(K, "e1", E1, NT1, L1_ffn_W1, L1_ffn_b1, H1, ACT.Gelu, None, None, L1_ffn_W2, L1_ffn_b2)
        finish(K, out, upto > 4)


def setup(K, x, src, dst):
    nc = K.nc
    with ExitStack() as stack:
        sb, pb, sem = K.tools(stack, "s")
        zero = sb("zero", [P, DIM])
        dload = sb("dload", [EROWS, ECOLS], I32)
        dflt = sb("dflt", [EROWS, ECOLS])
        rng = sb("rng", [EROWS, 2, GPR])
        padf = sb("padf", [P, SE // P])
        padi = sb("padi", [P, SE // P], I32)
        made = sem("made")
        loaded = sem("loaded")
        dst_in = sem("dst_in")
        ready = sem("ready")
        stored = sem("stored")
        with nc.Block() as block:
            @block.gpsimd
            def _(gp):
                for n, (t, pat) in enumerate(((K.iota, [[1, 512]]), (K.pid, [[1, 1]]))):
                    nc.gpsimd.iota(t[:, :], pattern=pat, base=0, channel_multiplier=n,
                                   allow_small_or_imprecise_dtypes=True).then_inc(made, 1)
                nc.gpsimd.memset(K.ident[:, :], 0.0).then_inc(made, 1)
                nc.gpsimd.memset(K.ones[:, :], 1.0).then_inc(made, 1)
                gp.wait_ge(made, 4)
                nc.gpsimd.affine_select(out=K.ident[:, :], in_=K.ident[:, :], compare_op=ALU.not_equal, fill=1.0,
                                        base=0, pattern=[[-1, P]], channel_multiplier=1).then_inc(made, 1)
                nc.gpsimd.affine_select(out=K.tri[:, :], in_=K.ones[:, :], compare_op=ALU.is_gt, fill=0.0,
                                        base=0, pattern=[[1, P]], channel_multiplier=-1).then_inc(made, 1)

            @block.vector
            def _(v):
                ch = Chain(v, ready)
                ch.mark(nc.vector.memset(K.X[:, TILES - 1, :], 0.0))
                ch.mark(nc.vector.memset(zero[:, :], 0.0))
                ch.mark(nc.vector.memset(padf[:, :], -1.0))
                ch.mark(nc.vector.memset(padi[:, :], 0))
                ch.mark(nc.vector.memset(K.dstI[:, TILES - 1:TILES], 0))
                ch.mark(nc.vector.memset(K.srcI[:, TILES - 1:TILES], 0))
                ch.mark(nc.vector.memset(K.eps[:, :], EPS))
                ch.mark(nc.vector.memset(K.onesf[:, :], 1.0))
                v.wait_ge(made, 6)
                ch.link(nc.vector.tensor_scalar(K.valid[:, :], K.pid[:, :], float(TAIL), None, ALU.is_lt))
                ch.link(nc.vector.tensor_scalar(K.vneg[:, :], K.valid[:, :], -1.0, HUGE, ALU.add, ALU.mult))
                for k in range(2):
                    ch.link(nc.vector.tensor_scalar(K.vdump[:, k:k + 1], K.valid[:, :], -1.0, -1.0, ALU.add, ALU.mult))
                    ch.link(nc.vector.scalar_tensor_tensor(K.vdump[:, k:k + 1], K.pid[:, :], float(SLOTS + k * P),
                                                           K.vdump[:, k:k + 1], ALU.add, ALU.mult))
                v.wait_ge(dst_in, 16)
                ch.link(nc.vector.tensor_copy(dflt[:, :], dload[:, :]))
                gv = dflt[:, :].rearrange("p (g e) -> p g e", e=GRAN)
                ch.mark(nc.vector.tensor_reduce(rng[:, 0, :], gv, AX.X, ALU.min))
                ch.mark(nc.vector.tensor_reduce(rng[:, 1, :], gv, AX.X, ALU.max))
                assert ch.n == 17

            @block.sync
            def _(sp):
                sp.dma_start(dload[:, :], dst.rearrange("(p e) -> p e", p=EROWS)).then_inc(dst_in, 16)
                full = (TILES - 1) * P
                for g in range(6):
                    sp.dma_start(K.X[:, 8 * g:8 * g + 8, :],
                                 x[8 * g * P:8 * (g + 1) * P, :].rearrange("(t p) d -> p t d", p=P)).then_inc(loaded, 16)
                sp.wait_ge(ready, 6)
                sp.dma_start(K.X[0:TAIL, TILES - 1, :], x[full:NODES, :]).then_inc(loaded, 16)
                for t, s in ((K.dstI, dst), (K.srcI, src)):
                    sp.dma_start(t[:, 0:TILES - 1], s[0:full].rearrange("(t p) -> p t", p=P),
                                 allow_slow_non_contiguous=True).then_inc(loaded, 16)
                    sp.dma_start(t[0:TAIL, TILES - 1:TILES], s[full:NODES].rearrange("(p o) -> p o", o=1)).then_inc(loaded, 16)
                sp.wait_ge(loaded, 16 * 11)

            @block.scalar
            def _(act):
                act.dma_start(K.SRCP[0:EDGES].rearrange("(p e) -> p e", p=EROWS),
                              src.rearrange("(p e) -> p e", p=EROWS)).then_inc(stored, 16)
                act.wait_ge(ready, 6)
                act.dma_start(K.SRCP[EDGES:EDGES + SE].rearrange("(p e) -> p e", p=P), padi[:, :]).then_inc(stored, 16)
                act.dma_start(K.DSTP[EDGES:EDGES + SE].rearrange("(p e) -> p e", p=P), padf[:, :]).then_inc(stored, 16)
                rows = (SLOTS + 2 * P) // P
                act.dma_start(K.XS.rearrange("(p r) d -> p r d", p=P),
                              zero[:, :].rearrange("p (o d) -> p o d", o=1).to_broadcast([P, rows, DIM])).then_inc(stored, 16)
                least = min(NT0, NT1) * MT
                act.dma_start(K.YS[least:SLOTS + 2 * P, :].rearrange("(p r) d -> p r d", p=P),
                              zero[:, :].rearrange("p (o d) -> p o d", o=1).to_broadcast([P, (SLOTS - least) // P + 2, DIM])).then_inc(stored, 16)
                act.wait_ge(ready, 15)
                act.dma_start(K.DSTP[0:EDGES].rearrange("(p e) -> p e", p=EROWS), dflt[:, :]).then_inc(stored, 16)
                act.wait_ge(ready, 17)
                for k in range(2):
                    act.dma_start(K.GR[k, :].rearrange("(p g) -> p g", p=EROWS), rng[:, k, :]).then_inc(stored, 16)
                act.wait_ge(stored, 16 * 8)


def edge_ranges(K):
    nc = K.nc
    with ExitStack() as stack:
        sb, pb, sem = K.tools(stack, "er")
        lo = sb("lo", [TILES, NGRAN])
        hi = sb("hi", [TILES, NGRAN])
        idx = sb("idx", [TILES, NGRAN])
        first = sb("first", [TILES, 1])
        last = sb("last", [TILES, 1])
        span = sb("span", [TILES, 2])
        cnt = sb("cnt", [TILES, 1])
        cmp = sb("cmp", [TILES, MAXSTEPS])
        row = sb("row", [1, TILES, 2])
        inc = sb("inc", [1, TILES])
        ranges_in = sem("ranges_in")
        index_made = sem("index_made")
        step = sem("step")
        span_out = sem("span_out")
        row_in = sem("row_in")
        with nc.Block() as block:
            @block.sync
            def _(sp):
                sp.dma_start(lo[:, :], K.GR[0:1, :].rearrange("o g -> (o g)").partition_broadcast(TILES)).then_inc(ranges_in, 16)
                sp.dma_start(hi[:, :], K.GR[1:2, :].rearrange("o g -> (o g)").partition_broadcast(TILES)).then_inc(ranges_in, 16)
                sp.wait_ge(step, 13)
                sp.dma_start(K.RT[:, :], span[:, :]).then_inc(span_out, 16)
                sp.wait_ge(span_out, 16)
                sp.dma_start(row[0:1, :, :], K.RT.rearrange("(o t) k -> o t k", o=1)).then_inc(row_in, 16)
                sp.wait_ge(row_in, 16)

            @block.gpsimd
            def _(gp):
                nc.gpsimd.iota(idx[:, :], pattern=[[1, NGRAN]], base=0, channel_multiplier=0,
                               allow_small_or_imprecise_dtypes=True).then_inc(index_made, 1)

            @block.vector
            def _(v):
                ch = Chain(v, step)
                v.wait_ge(ranges_in, 32)
                v.wait_ge(index_made, 1)
                ch.link(nc.vector.tensor_scalar(first[:, :], K.pid[0:TILES, :], float(P), None, ALU.mult))
                ch.link(nc.vector.tensor_scalar(last[:, :], first[:, :], float(P - 1), None, ALU.add))
                ch.link(nc.vector.tensor_scalar(hi[:, :], hi[:, :], first[:, 0:1], None, ALU.is_ge))
                ch.link(nc.vector.scalar_tensor_tensor(hi[:, :], lo[:, :], last[:, 0:1], hi[:, :], ALU.is_le, ALU.mult))
                ch.link(nc.vector.tensor_scalar(lo[:, :], hi[:, :], -2.0 * NGRAN, 2.0 * NGRAN, ALU.mult, ALU.add))
                ch.link(nc.vector.tensor_tensor(lo[:, :], lo[:, :], idx[:, :], ALU.add))
                ch.link(nc.vector.scalar_tensor_tensor(hi[:, :], idx[:, :], 1.0, hi[:, :], ALU.add, ALU.mult))
                ch.link(nc.vector.tensor_reduce(span[:, 0:1], lo[:, :], AX.X, ALU.min))
                ch.link(nc.vector.tensor_reduce(cnt[:, :], hi[:, :], AX.X, ALU.max))
                ch.link(nc.vector.tensor_scalar(span[:, 0:1], span[:, 0:1], float(NGRAN - 1), None, ALU.min))
                ch.link(nc.vector.tensor_scalar(cnt[:, :], cnt[:, :], span[:, 0:1], 1.0, ALU.subtract, ALU.max))
                ch.link(nc.vector.tensor_scalar(cmp[:, :], K.iota[0:TILES, 0:MAXSTEPS], float(SEG), cnt[:, 0:1],
                                                ALU.mult, ALU.is_lt))
                ch.link(nc.vector.tensor_reduce(span[:, 1:2], cmp[:, :], AX.X, ALU.add))
                assert ch.n == 13
                v.wait_ge(row_in, 16)
                ch.link(nc.vector.tensor_tensor_scan(inc[0:1, :], K.onesf[0:1, 0:TILES], row[0:1, :, 1], 0.0, ALU.mult, ALU.add))
                ch.mark(nc.vector.tensor_scalar(K.ET[0:1, :, 0], row[0:1, :, 0], float(GRAN), None, ALU.mult))
                ch.mark(nc.vector.tensor_copy(K.ET[0:1, :, 1], row[0:1, :, 1]))
                ch.mark(nc.vector.tensor_tensor(K.ET[0:1, :, 2], inc[0:1, :], row[0:1, :, 1], ALU.subtract))


def project(K, tag, pre, gat_weights=None, router=None, gate=None):
    nc = K.nc
    with ExitStack() as stack:
        sb, pb, sem = K.tools(stack, tag)
        NC = DIM + 8 if gat_weights else (E0 if router else E1)
        stats = sb("stats", [P, BODY, 6])
        mv = sb("mv", [P, BODY, 2])
        std = sb("std", [P, BODY, 1])
        rstd = sb("rstd", [P, BODY, 1])
        yg = sb("yg", [P, BODY, DIM])
        yT = sb("yT", [P, BODY, KC, P])
        og = sb("og", [P, BODY, NC])
        w = sb("w", [P, KC, R0 if router else NC])
        if gat_weights:
            att = sb("att", [P, 2, DIM])
            prod = sb("prod", [P, 2, DIM])
        else:
            bias = sb("bias", [P, NC])
        if router:
            w2 = sb("w2", [P, NC])
            rb1 = sb("rb1", [P, 1])
            rhT = sb("rhT", [P, BODY, P])
            pR = [pb(f"pR{n}", [P, 512]) for n in range(2)]
        if pre == "attn0":
            rows = sb("rows", [P, BODY, DIM + 4])
            left = sb("left", [P, BODY, 4])
            z = sb("z", [P, BODY, 4])
            z1 = sb("z1", [P, BODY, 1])
            mix = sb("mix", [P, BODY, DIM])
            tmp = sb("tmp", [P, BODY, CH])
        if pre == "combine":
            rows = sb("rows", [P, BODY, 2 * DIM])
        pT = [pb(f"pT{n}", [P, 512]) for n in range(2)]
        pO = [pb(f"pO{n}", [P, 512]) for n in range(2)]

        w_in = sem("w_in")
        w_ready = sem("w_ready")
        gathered = [sem(f"gathered{j}") for j in range(BODY)]
        rows_used = sem("rows_used")
        chain = sem("chain")
        exps_done = sem("exps_done")
        z_ready = sem("z_ready")
        stats_ready = sem("stats_ready")
        std_ready = sem("std_ready")
        y_ready = sem("y_ready")
        y_kept = sem("y_kept")
        pT_ready = sem("pT_ready")
        yT_ready = sem("yT_ready")
        pR_ready = sem("pR_ready")
        rh_ready = sem("rh_ready")
        pO_ready = sem("pO_ready")
        o_ready = sem("o_ready")
        stored = sem("stored")
        gate_sem = sem("passed")
        og_free = sem("og_free")
        lifts = (o_ready, pT_ready, y_kept, pO_ready, yT_ready, rh_ready, og_free)

        n_w = 4 if gat_weights else (4 if router else 2)
        n_tables = (3 if tag == "a0" else 1) if gat_weights else 0

        with nc.Block() as block:
            @block.sync
            def _(sp):
                if gat_weights:
                    wd, first, second = gat_weights
                    for k in range(KC):
                        sp.dma_start(w[:, k, 0:DIM], wd[k * P:(k + 1) * P, :]).then_inc(w_in, 16)
                    for n, a in enumerate((first, second)):
                        sp.dma_start(att[:, n, :], a.rearrange("h c -> (h c)").partition_broadcast(P)).then_inc(w_in, 16)
                elif router:
                    r1, b1, r2, b2 = router
                    sp.dma_start(w[:, :, :], r1.rearrange("(k p) n -> p k n", p=P)).then_inc(w_in, 16)
                    sp.dma_start(rb1[:, :], b1.rearrange("(p o) -> p o", o=1)).then_inc(w_in, 16)
                    sp.dma_start(w2[:, :], r2).then_inc(w_in, 16)
                    sp.dma_start(bias[:, :], b2.partition_broadcast(P)).then_inc(w_in, 16)
                else:
                    wg, bg = gate
                    sp.dma_start(w[:, :, :], wg.rearrange("(k p) n -> p k n", p=P)).then_inc(w_in, 16)
                    sp.dma_start(bias[:, :], bg.partition_broadcast(P)).then_inc(w_in, 16)
                if gat_weights:
                    with sp.Fori(0, TRIPS) as i:
                        r0 = sp.snap(i * (BODY * P))
                        n_st = sp.snap((i + 1) * (32 if tag == "a0" else 16))
                        freed(sp, o_ready, i * BODY + BODY)
                        if tag == "a0":
                            sp.dma_start(K.T0[bass.ds(r0, BODY * P), :].rearrange("(t p) c -> p t c", p=P),
                                         og[:, :, 0:DIM + 4]).then_inc(stored, 16)
                            sp.dma_start(K.AL[bass.ds(r0, BODY * P), :].rearrange("(t p) c -> p t c", p=P),
                                         og[:, :, DIM + 4:DIM + 8]).then_inc(stored, 16)
                        else:
                            sp.dma_start(K.T1[bass.ds(r0, BODY * P), :].rearrange("(t p) c -> p t c", p=P),
                                         og[:, :, 0:DIM + 4]).then_inc(stored, 16)
                        sp.wait_ge(stored, n_st)
                        sp.sem_inc(og_free, 1)

            @block.gpsimd
            def _(gp):
                lift(gp, lifts)
                if pre is None:
                    return
                for t in range(TILES):
                    j = t % BODY
                    if t >= BODY:
                        gp.wait_ge(rows_used, t - BODY + 1)
                    if pre == "attn0":
                        gp.indirect_dma_start(rows[:, j, :], None, K.T0,
                                              bass.IndirectOffsetOnAxis(ap=K.dstI[:, t:t + 1], axis=0)).then_inc(gathered[j], 16)
                        gp.indirect_dma_start(left[:, j, :], None, K.AL,
                                              bass.IndirectOffsetOnAxis(ap=K.srcI[:, t:t + 1], axis=0)).then_inc(gathered[j], 16)
                    else:
                        for k in range(2):
                            gp.indirect_dma_start(rows[:, j, k * DIM:(k + 1) * DIM], None, K.YS,
                                                  bass.IndirectOffsetOnAxis(ap=K.POS[:, t, k:k + 1], axis=0)).then_inc(gathered[j], 16)

            @block.vector
            def _(v):
                if gat_weights:
                    ch = Chain(v, w_ready)
                    v.wait_ge(w_in, 16 * n_w)
                    for k in range(KC):
                        ch.link(nc.vector.tensor_tensor(prod[:, :, :], att[:, :, :],
                                                        w[:, k:k + 1, 0:DIM].to_broadcast([P, 2, DIM]), ALU.mult))
                        ch.link(nc.vector.tensor_reduce(w[:, k, DIM:DIM + 8],
                                                        prod[:, :, :].rearrange("p n (h c) -> p (n h) c", h=HEADS),
                                                        AX.X, ALU.add))
                per = {None: 0, "attn0": 6 + 2 * BODY, "combine": BODY}[pre] + BODY + 1
                with v.Fori(0, TRIPS) as i:
                    t0 = i * BODY
                    ch = Chain(v, chain, i * per)
                    if pre == "attn0":
                        for j in range(BODY):
                            v.wait_ge(gathered[j], i * 32 + 32)
                        ch.link(nc.vector.tensor_tensor(z[:, :, :], left[:, :, :], rows[:, :, DIM:DIM + 4], ALU.add))
                        ch.link(nc.vector.scalar_tensor_tensor(z[:, :, :], z[:, :, :], 0.01, z[:, :, :], ALU.mult, ALU.max))
                        ch.link(nc.vector.tensor_reduce(z1[:, :, :], z[:, :, :], AX.X, ALU.max))
                        nc.vector.tensor_tensor(z[:, :, :], z[:, :, :], z1[:, :, :].to_broadcast([P, BODY, 4]),
                                                ALU.subtract).then_inc(z_ready, 1)
                        v.wait_ge(exps_done, i + 1)
                        ch.link(nc.vector.tensor_reduce(z1[:, :, :], z[:, :, :], AX.X, ALU.add))
                        ch.link(nc.vector.reciprocal(z1[:, :, :], z1[:, :, :]))
                        ch.link(nc.vector.tensor_tensor(z[:, :, :], z[:, :, :], z1[:, :, :].to_broadcast([P, BODY, 4]), ALU.mult))
                        for j in range(BODY):
                            ch.mark(nc.vector.tensor_tensor(
                                mix[:, j, :].rearrange("p (h c) -> p h c", h=HEADS),
                                rows[:, j, 0:DIM].rearrange("p (h c) -> p h c", h=HEADS),
                                z[:, j, :].rearrange("p (h o) -> p h o", o=1).to_broadcast([P, HEADS, CH]), ALU.mult))
                        ch.settle()
                        for j in range(BODY):
                            ch.mark(nc.vector.tensor_reduce(
                                tmp[:, j, :].rearrange("p (c o) -> p c o", o=1),
                                mix[:, j, :].rearrange("p (h c) -> p c h", h=HEADS), AX.X, ALU.add))
                        ch.settle()
                        for j in range(BODY):
                            Xt = K.X[:, bass.ds(t0 + j, 1), :].rearrange("p o (h c) -> p (o h) c", h=HEADS)
                            nc.vector.tensor_tensor(Xt, Xt, tmp[:, j:j + 1, :].to_broadcast([P, HEADS, CH]),
                                                    ALU.add).then_inc(rows_used, 1)
                        v.wait_ge(rows_used, i * BODY + BODY)
                        v.sem_inc(gate_sem, 1)
                    if pre == "combine":
                        for j in range(BODY):
                            Xt = K.X[:, bass.ds(t0 + j, 1), :].rearrange("p o d -> p (o d)")
                            Wt = K.WT[:, bass.ds(t0 + j, 1), :].rearrange("p o d -> p (o d)")
                            v.wait_ge(gathered[j], i * 32 + 32)
                            ch.mark(nc.vector.scalar_tensor_tensor(Xt, rows[:, j, 0:DIM], Wt[:, 0:1], Xt, ALU.mult, ALU.add))
                        ch.settle()
                        for j in range(BODY):
                            Xt = K.X[:, bass.ds(t0 + j, 1), :].rearrange("p o d -> p (o d)")
                            Wt = K.WT[:, bass.ds(t0 + j, 1), :].rearrange("p o d -> p (o d)")
                            nc.vector.scalar_tensor_tensor(Xt, rows[:, j, DIM:2 * DIM], Wt[:, 1:2], Xt,
                                                           ALU.mult, ALU.add).then_inc(rows_used, 1)
                        v.wait_ge(rows_used, i * BODY + BODY)
                        v.sem_inc(gate_sem, 1)
                    for j in range(BODY):
                        ch.mark(nc.vector.bn_stats(stats[:, j, :], K.X[:, bass.ds(t0 + j, 1), :].rearrange("p o d -> p (o d)")))
                    ch.settle()
                    v.sem_inc(gate_sem, 1)
                    for j in range(BODY):
                        last = nc.vector.bn_aggr(mv[:, j, :], stats[:, j, :])
                    last.then_inc(stats_ready, 1)
                    v.wait_ge(std_ready, i + 1)
                    ch.link(nc.vector.reciprocal(rstd[:, :, :], std[:, :, :]))
                    assert ch.n == per, (ch.n, per)
                    freed(v, pT_ready, i * BODY)
                    if not gat_weights:
                        freed(v, y_kept, i * BODY)
                    for j in range(BODY):
                        nc.vector.tensor_scalar(yg[:, j, :], K.X[:, bass.ds(t0 + j, 1), :].rearrange("p o d -> p (o d)"),
                                                mv[:, j, 0:1], rstd[:, j, :], ALU.subtract, ALU.mult).then_inc(y_ready, 1)
                    if not gat_weights:
                        for j in range(BODY):
                            freed(v, pO_ready, i * BODY + j + 1)
                            nc.vector.tensor_tensor(K.LG[:, bass.ds(t0 + j, 1), 0:NC].rearrange("p o d -> p (o d)"),
                                                    pO[j % 2][:, 0:NC], bias[:, :], ALU.add).then_inc(o_ready, 1)

            @block.scalar
            def _(act):
                with act.Fori(0, TRIPS) as i:
                    t0 = i * BODY
                    if pre == "attn0":
                        act.wait_ge(z_ready, i + 1)
                        nc.scalar.activation(z[:, :, :], z[:, :, :], ACT.Exp).then_inc(exps_done, 1)
                    act.wait_ge(stats_ready, i + 1)
                    nc.scalar.activation(std[:, :, :], mv[:, :, 1:2], ACT.Sqrt, bias=K.eps[:, 0:1]).then_inc(std_ready, 1)

                    def take(j):
                        if gat_weights:
                            freed(act, pO_ready, i * BODY + j + 1)
                            if j == 0:
                                freed(act, og_free, i)
                            if tag != "a0":
                                nc.scalar.activation(K.AD[:, bass.ds(t0 + j, 1), :].rearrange("p o d -> p (o d)"),
                                                     pO[j % 2][:, DIM:DIM + 8], ACT.Copy)
                            nc.scalar.activation(og[:, j, :], pO[j % 2][:, 0:NC], ACT.Copy).then_inc(o_ready, 1)

                    def hidden(j):
                        act.wait_ge(pR_ready, i * BODY + j + 1)
                        nc.scalar.activation(rhT[:, j, :], pR[j % 2][:, 0:P], ACT.Relu, bias=rb1[:, 0:1]).then_inc(rh_ready, 1)

                    freed(act, pO_ready, i * BODY)
                    for j in range(BODY):
                        freed(act, pT_ready, i * BODY + j + 1)
                        nc.scalar.activation(yT[:, j, :, :].rearrange("p k m -> p (k m)"), pT[j % 2][:, 0:KC * P],
                                             ACT.Copy).then_inc(yT_ready, 1)
                        if not gat_weights:
                            nc.scalar.activation(K.Y[:, bass.ds(t0 + j, 1), :].rearrange("p o d -> p (o d)"), yg[:, j, :],
                                                 ACT.Copy).then_inc(y_kept, 1)
                        if router:
                            if j:
                                hidden(j - 1)
                        elif j:
                            take(j - 1)
                    if router:
                        hidden(BODY - 1)
                    else:
                        take(BODY - 1)

            @block.tensor
            def _(pe):
                with pe.Fori(0, TRIPS) as i:
                    def transpose(j):
                        pe.wait_ge(y_ready, i * BODY + j + 1)
                        freed(pe, yT_ready, i * BODY + max(0, j - 1))
                        for k in range(KC):
                            last = nc.tensor.transpose(pT[j % 2][:, k * P:(k + 1) * P], yg[:, j, k * P:(k + 1) * P], K.ident[:, :])
                        last.then_inc(pT_ready, 1)

                    def multiply(j):
                        freed(pe, yT_ready, i * BODY + j + 1)
                        if router:
                            freed(pe, rh_ready, i * BODY + max(0, j - 1))
                            for k in range(KC):
                                last = nc.tensor.matmul(pR[j % 2][:, 0:P], w[:, k, :], yT[:, j, k, :], start=(k == 0), stop=(k == KC - 1))
                            last.then_inc(pR_ready, 1)
                        else:
                            freed(pe, o_ready, i * BODY + max(0, j - 1))
                            for k in range(KC):
                                last = nc.tensor.matmul(pO[j % 2][:, 0:NC], yT[:, j, k, :], w[:, k, :], start=(k == 0), stop=(k == KC - 1))
                            last.then_inc(pO_ready, 1)

                    def second(j):
                        freed(pe, rh_ready, i * BODY + j + 1)
                        freed(pe, o_ready, i * BODY + max(0, j - 1))
                        nc.tensor.matmul(pO[j % 2][:, 0:NC], rhT[:, j, :], w2[:, :], start=True, stop=True).then_inc(pO_ready, 1)

                    if gat_weights:
                        pe.wait_ge(w_ready, 2 * KC)
                    else:
                        pe.wait_ge(w_in, 16 * n_w)
                    for j in range(BODY + 2):
                        if j < BODY:
                            transpose(j)
                        if 1 <= j <= BODY:
                            multiply(j - 1)
                        if router and j >= 2:
                            second(j - 2)


def route(K, tag, E, NT, softmax_first):
    nc = K.nc
    TE = TILES * E
    MAXT = -(-NODES // MT)
    with ExitStack() as stack:
        sb, pb, sem = K.tools(stack, tag)
        p = sb("p", [P, TILES, E])
        c = sb("c", [P, TILES, E])
        M = [sb(f"M{k}", [P, TILES, E]) for k in range(2)]
        m = [sb(f"m{k}", [P, TILES, 1]) for k in range(2)]
        r = sb("r", [P, TILES, 1])
        rev = sb("rev", [P, E])
        Mb = sb("Mb", [P, TE], BF16)
        rank = sb("rank", [P, TILES, E])
        tot = sb("tot", [P, TILES, E])
        inc = sb("inc", [P, TILES, E])
        cmp = sb("cmp", [P, E, MAXT])
        kt = sb("kt", [P, MAXT])
        nt = sb("nt", [P, E])
        end = sb("end", [P, E])
        beg = sb("beg", [P, E])
        pos = sb("pos", [P, TILES, 2])
        cj = sb("cj", [P, NT, E])
        te = sb("te", [P, NT])
        pr = pb("pr", [P, 512])
        pt = pb("pt", [P, 512])
        chain = sem("chain")
        exp_in = sem("exp_in")
        exp_out = sem("exp_out")
        masks = sem("masks")
        ranks = sem("ranks")

        def te_(ap):
            return ap[:, :, :].to_broadcast([P, TILES, E])

        def e_(ap):
            return ap[:, :].rearrange("p (o e) -> p o e", o=1).to_broadcast([P, TILES, E])

        with nc.Block() as block:
            @block.vector
            def _(v):
                ch = Chain(v, chain)
                V = nc.vector
                ch.mark(V.tensor_scalar(rev[:, :], K.iota[:, 0:E], -1.0, float(E), ALU.mult, ALU.add))
                ch.mark(V.tensor_scalar(kt[:, :], K.iota[:, 0:MAXT], float(MT), None, ALU.mult))
                lg = K.LG[:, :, 0:E]
                if softmax_first:
                    ch.link(V.tensor_reduce(r[:, :, :], lg, AX.X, ALU.max))
                    V.tensor_tensor(p[:, :, :], lg, te_(r), ALU.subtract).then_inc(exp_in, 1)
                    v.wait_ge(exp_out, 1)
                    ch.link(V.tensor_reduce(r[:, :, :], p[:, :, :], AX.X, ALU.add))
                    ch.link(V.reciprocal(r[:, :, :], r[:, :, :]))
                    ch.link(V.tensor_tensor(p[:, :, :], p[:, :, :], te_(r), ALU.mult))
                else:
                    ch.link(V.tensor_copy(p[:, :, :], lg))
                for k in range(2):
                    ch.link(V.tensor_reduce(m[k][:, :, :], p[:, :, :], AX.X, ALU.max))
                    ch.link(V.tensor_tensor(c[:, :, :], p[:, :, :], te_(m[k]), ALU.is_equal))
                    ch.link(V.tensor_tensor(c[:, :, :], c[:, :, :], e_(rev), ALU.mult))
                    ch.link(V.tensor_reduce(r[:, :, :], c[:, :, :], AX.X, ALU.max))
                    ch.link(V.tensor_tensor(M[k][:, :, :], c[:, :, :], te_(r), ALU.is_equal))
                    if k == 0:
                        ch.link(V.scalar_tensor_tensor(p[:, :, :], M[0][:, :, :], -HUGE, p[:, :, :], ALU.mult, ALU.add))
                V.tensor_tensor(r[:, :, :], m[1][:, :, :], m[0][:, :, :], ALU.subtract).then_inc(exp_in, 1)
                for k in range(2):
                    ch.link(V.tensor_scalar(M[k][:, TILES - 1, :], M[k][:, TILES - 1, :], K.valid[:, 0:1], None, ALU.mult))
                V.tensor_tensor(Mb[:, :].rearrange("p (t e) -> p t e", e=E), M[0][:, :, :], M[1][:, :, :], ALU.add).then_inc(masks, 1)
                v.wait_ge(exp_out, 2 if softmax_first else 1)
                ch.link(V.tensor_scalar(m[0][:, :, :], r[:, :, :], 1.0, None, ALU.add))
                ch.link(V.reciprocal(K.WT[:, :, 0:1], m[0][:, :, :]))
                ch.link(V.tensor_tensor(K.WT[:, :, 1:2], r[:, :, :], K.WT[:, :, 0:1], ALU.mult))
                v.wait_ge(ranks, 1)
                ch.mark(V.tensor_copy(rank[:, :, :].rearrange("p t e -> p (t e)"), pr[:, 0:TE]))
                ch.link(V.tensor_copy(tot[:, :, :].rearrange("p t e -> p (t e)"), pt[:, 0:TE]))
                for e in range(E):
                    ch.mark(V.tensor_tensor_scan(inc[:, :, e], K.onesf[:, :], tot[:, :, e], 0.0, ALU.mult, ALU.add))
                ch.settle()
                ch.mark(V.tensor_tensor(rank[:, :, :], rank[:, :, :], inc[:, :, :], ALU.add))
                cnt = inc[:, TILES - 1, :].rearrange("p (e o) -> p e o", o=1).to_broadcast([P, E, MAXT])
                ch.link(V.tensor_tensor(cmp[:, :, :], cnt, kt[:, :].rearrange("p (o k) -> p o k", o=1).to_broadcast([P, E, MAXT]), ALU.is_gt))
                ch.mark(V.tensor_tensor(rank[:, :, :], rank[:, :, :], tot[:, :, :], ALU.subtract))
                ch.link(V.tensor_reduce(nt[:, :].rearrange("p (e o) -> p e o", o=1), cmp[:, :, :], AX.X, ALU.add))
                ch.link(V.tensor_tensor_scan(end[:, :], K.onesf[:, 0:E], nt[:, :], 0.0, ALU.mult, ALU.add))
                ch.link(V.tensor_tensor(beg[:, :], end[:, :], nt[:, :], ALU.subtract))
                ch.link(V.tensor_scalar(beg[:, :], beg[:, :], float(MT), None, ALU.mult))
                ch.link(V.tensor_tensor(rank[:, :, :], rank[:, :, :], e_(beg), ALU.add))
                for k in range(2):
                    ch.link(V.tensor_tensor(M[k][:, :, :], M[k][:, :, :], rank[:, :, :], ALU.mult))
                    ch.link(V.tensor_reduce(pos[:, :, k:k + 1], M[k][:, :, :], AX.X, ALU.add))
                ch.link(V.tensor_tensor(pos[:, TILES - 1, :], pos[:, TILES - 1, :], K.vdump[:, :], ALU.add))
                ch.link(V.tensor_copy(K.POS[:, :, :], pos[:, :, :]))
                ch.link(V.tensor_tensor(cj[:, :, :], end[:, :].rearrange("p (o e) -> p o e", o=1).to_broadcast([P, NT, E]),
                                        K.iota[:, 0:NT].rearrange("p (j o) -> p j o", o=1).to_broadcast([P, NT, E]), ALU.is_le))
                ch.link(V.tensor_reduce(te[:, :].rearrange("p (j o) -> p j o", o=1), cj[:, :, :], AX.X, ALU.add))
                ch.link(V.tensor_scalar(te[:, :], te[:, :], float(E - 1), None, ALU.min))
                ch.link(V.tensor_copy(K.TE[:, 0:NT], te[:, :]))

            @block.scalar
            def _(act):
                if softmax_first:
                    act.wait_ge(exp_in, 1)
                    nc.scalar.activation(p[:, :, :], p[:, :, :], ACT.Exp).then_inc(exp_out, 1)
                act.wait_ge(exp_in, 2 if softmax_first else 1)
                nc.scalar.activation(r[:, :, :], r[:, :, :], ACT.Exp).then_inc(exp_out, 1)

            @block.tensor
            def _(pe):
                pe.wait_ge(masks, 1)
                nc.tensor.matmul(pr[:, 0:TE], K.tri[:, :], Mb[:, :], start=True, stop=True)
                nc.tensor.matmul(pt[:, 0:TE], K.ones[:, :], Mb[:, :], start=True, stop=True).then_inc(ranks, 1)


def experts(K, tag, E, NT, wa, ba, H, func, wm, bm, wl, bl):
    nc = K.nc
    HC = H // P
    units = HC + (H // P if wm is not None else 0)
    with ExitStack() as stack:
        sb, pb, sem = K.tools(stack, tag)
        WA = [sb(f"WA{b}", [P, KC, H]) for b in range(2)]
        WL = [sb(f"WL{b}", [P, HC, DIM]) for b in range(2)]
        WM = [sb(f"WM{b}", [P, HC, H]) for b in range(2)] if wm is not None else None
        BA = sb("BA", [P, E * HC])
        BM = sb("BM", [P, E * HC]) if wm is not None else None
        BL = sb("BL", [P, E, DIM])
        xs = [sb(f"xs{b}", [P, SUB, DIM]) for b in range(2)]
        xT = [sb(f"xT{b}", [P, KC, MT]) for b in range(2)]
        hT = [sb(f"hT{b}", [P, HC, MT]) for b in range(2)]
        mT = [sb(f"mT{b}", [P, HC, MT]) for b in range(2)] if wm is not None else None
        ob = [sb(f"ob{b}", [P, SUB, DIM]) for b in range(2)]
        pX = [pb(f"pX{b}", [P, KC, MT]) for b in range(2)]
        pH = [pb(f"pH{n}", [P, 512]) for n in range(4)]
        pO = [pb(f"pO{n}", [P, 512]) for n in range(2)]

        scattered = sem("scattered")
        biases_in = sem("biases_in")
        w_in = [sem(f"w_in{b}") for b in range(2)]
        x_in = [sem(f"x_in{b}") for b in range(2)]
        pX_ready = [sem(f"pX_ready{b}") for b in range(2)]
        xT_ready = sem("xT_ready")
        pH_ready = sem("pH_ready")
        h_ready = sem("h_ready")
        tile_done = [sem(f"tile_done{b}") for b in range(2)]
        half_ready = sem("half_ready")
        o_ready = sem("o_ready")
        stored = [sem(f"stored{b}") for b in range(2)]
        passed = sem("passed")
        ob_free = [sem(f"ob_free{b}") for b in range(2)]
        lifts = (xT_ready, h_ready, o_ready, *pX_ready, *tile_done, *ob_free)
        n_w = 3 if wm is not None else 2

        with nc.Block() as block:
            @block.gpsimd
            def _(gp):
                lift(gp, lifts)
                for t in range(TILES):
                    for k in range(2):
                        gp.indirect_dma_start(K.XS, bass.IndirectOffsetOnAxis(ap=K.POS[:, t, k:k + 1], axis=0),
                                              K.Y[:, t, :], None).then_inc(scattered, 16)
                with gp.Fori(0, NT // 2) as i:
                    for b in range(2):
                        r0 = gp.snap(i * (2 * MT) + b * MT)
                        freed(gp, o_ready, (i * 2 + b + 1) * SUB)
                        gp.sem_inc(passed, 1)
                        gp.dma_start(K.YS[bass.ds(r0, MT), :].rearrange("(s p) d -> p s d", p=P), ob[b][:, :, :]).then_inc(stored[b], 16)
                        gp.wait_ge(stored[b], i * 16 + 16)
                        gp.sem_inc(ob_free[b], 1)

            @block.sync
            def _(sp):
                sp.dma_start(BA[:, :], ba.rearrange("e (c p) -> p (e c)", p=P), allow_slow_non_contiguous=True).then_inc(biases_in, 16)
                sp.dma_start(BL[:, :, :].rearrange("p e d -> p (e d)"), bl.rearrange("e d -> (e d)").partition_broadcast(P)).then_inc(biases_in, 16)
                if wm is not None:
                    sp.dma_start(BM[:, :], bm.rearrange("e (c p) -> p (e c)", p=P), allow_slow_non_contiguous=True).then_inc(biases_in, 16)
                wa_r = wa.rearrange("e k h -> (e k) h")
                wl_r = wl.rearrange("e h d -> (e h) d")
                wm_r = wm.rearrange("e h d -> (e h) d") if wm is not None else None
                with sp.Fori(0, NT // 2) as i:
                    for b in range(2):
                        e = sp.value_load(K.TE[0:1, bass.ds(i * 2 + b, 1)], min_val=0, max_val=E - 1)
                        ra = sp.snap(e * DIM)
                        rl = sp.snap(e * H)
                        r0 = sp.snap(i * (2 * MT) + b * MT)
                        sp.wait_ge(scattered, 16 * 2 * TILES)
                        freed(sp, pX_ready[b], i)
                        sp.dma_start(xs[b][:, :, :], K.XS[bass.ds(r0, MT), :].rearrange("(s p) d -> p s d", p=P)).then_inc(x_in[b], 16)
                        freed(sp, tile_done[b], i)
                        sp.dma_start(WA[b][:, :, :], wa_r[bass.ds(ra, DIM), :].rearrange("(k p) h -> p k h", p=P)).then_inc(w_in[b], 16)
                        sp.dma_start(WL[b][:, :, :], wl_r[bass.ds(rl, H), :].rearrange("(k p) h -> p k h", p=P)).then_inc(w_in[b], 16)
                        if wm is not None:
                            sp.dma_start(WM[b][:, :, :], wm_r[bass.ds(rl, H), :].rearrange("(k p) h -> p k h", p=P)).then_inc(w_in[b], 16)

            @block.tensor
            def _(pe):
                def transpose(i, b):
                    pe.wait_ge(x_in[b], i * 16 + 16)
                    if not isinstance(i, int):
                        freed(pe, xT_ready, i * 2 + b - 1)
                    for s in range(SUB):
                        for k in range(KC):
                            last = nc.tensor.transpose(pX[b][:, k, s * P:(s + 1) * P], xs[b][:, s, k * P:(k + 1) * P], K.ident[:, :])
                    last.then_inc(pX_ready[b], 1)

                def hidden(i, b, W, src, nk, u0):
                    for u in range(HC):
                        freed(pe, h_ready, (i * 2 + b) * units + max(0, u0 + u - 3))
                        for k in range(nk):
                            last = nc.tensor.matmul(pH[(u0 + u) % 4][:, 0:MT], W[b][:, k, u * P:(u + 1) * P], src[b][:, k, :],
                                                    start=(k == 0), stop=(k == nk - 1))
                        last.then_inc(pH_ready, 1)

                def first(i, b):
                    freed(pe, xT_ready, i * 2 + b + 1)
                    pe.wait_ge(w_in[b], (i + 1) * (16 * n_w))
                    hidden(i, b, WA, xT, KC, 0)

                def middle(i, b):
                    if wm is not None:
                        freed(pe, h_ready, (i * 2 + b) * units + HC)
                        hidden(i, b, WM, hT, HC, HC)

                def final(i, b):
                    act_in = mT if wm is not None else hT
                    freed(pe, h_ready, (i * 2 + b + 1) * units)
                    for s in range(SUB):
                        freed(pe, o_ready, (i * 2 + b) * SUB)
                        for k in range(HC):
                            last = nc.tensor.matmul(pO[s][:, 0:DIM], act_in[b][:, k, s * P:(s + 1) * P], WL[b][:, k, :],
                                                    start=(k == 0), stop=(k == HC - 1))
                        last.then_inc(half_ready if s == 0 else tile_done[b], 1)

                pe.wait_ge(biases_in, 16 * n_w)
                transpose(0, 0)
                first(0, 0)
                transpose(0, 1)
                middle(0, 0)
                with pe.Fori(0, NT // 2 - 1) as i:
                    first(i, 1)
                    transpose(i + 1, 0)
                    final(i, 0)
                    middle(i, 1)
                    first(i + 1, 0)
                    transpose(i + 1, 1)
                    final(i, 1)
                    middle(i + 1, 0)
                last = NT // 2 - 1
                first(last, 1)
                final(last, 0)
                middle(last, 1)
                final(last, 1)

            @block.scalar
            def _(act):
                act.wait_ge(biases_in, 16 * n_w)
                with act.Fori(0, NT // 2) as i:
                    for b in range(2):
                        e = act.value_load(K.TE[0:1, bass.ds(i * 2 + b, 1)], min_val=0, max_val=E - 1)
                        freed(act, tile_done[b], i)
                        for u in range(units):
                            act.wait_ge(pH_ready, (i * 2 + b) * units + u + 1)
                            to, bias, c = (hT, BA, u) if u < HC else (mT, BM, u - HC)
                            nc.scalar.activation(to[b][:, c, :], pH[u % 4][:, 0:MT], func,
                                                 bias=bias[:, bass.ds(e * HC + c, 1)]).then_inc(h_ready, 1)

            @block.vector
            def _(v):
                def x_out(i, b):
                    freed(v, pX_ready[b], i + 1)
                    if not isinstance(i, int):
                        v.wait_ge(pH_ready, (i * 2 + b - 2) * units + HC)
                    nc.vector.tensor_copy(xT[b][:, :, :], pX[b][:, :, :]).then_inc(xT_ready, 1)

                def o_out(i, b):
                    e = v.value_load(K.TE[0:1, bass.ds(i * 2 + b, 1) if not isinstance(i, int) else slice(i * 2 + b, i * 2 + b + 1)],
                                     min_val=0, max_val=E - 1)
                    freed(v, ob_free[b], i)
                    for s in range(SUB):
                        if s == 0:
                            v.wait_ge(half_ready, i * 2 + b + 1)
                        else:
                            freed(v, tile_done[b], i + 1)
                        nc.vector.tensor_tensor(ob[b][:, s, :], pO[s][:, 0:DIM],
                                                BL[:, bass.ds(e, 1), :].rearrange("p o d -> p (o d)"), ALU.add).then_inc(o_ready, 1)

                v.wait_ge(biases_in, 16 * n_w)
                x_out(0, 0)
                x_out(0, 1)
                with v.Fori(0, NT // 2 - 1) as i:
                    x_out_next = i + 1
                    o_out(i, 0)
                    x_out(x_out_next, 0)
                    o_out(i, 1)
                    x_out(x_out_next, 1)
                o_out(NT // 2 - 1, 0)
                o_out(NT // 2 - 1, 1)


def attention(K, bias_in):
    nc = K.nc
    J = range(len(CHUNKS))
    with ExitStack() as stack:
        sb, pb, sem = K.tools(stack, "at")
        gm = sb("gm", [P, HEADS])
        gt = sb("gt", [P, HEADS])
        adm = sb("adm", [P, TILES, 8])
        exs = sb("exs", [P, TILES, HEADS])
        pm = sem("pm")
        gm_ready = sem("gm_ready")
        gm_all = sem("gm_all")
        self_z = sem("self_z")
        with nc.Block() as block:
            @block.vector
            def _(v):
                V = nc.vector
                ch = Chain(v, pm)
                AS, ADs = K.AD[:, :, 0:4], K.AD[:, :, 4:8]
                ch.mark(V.tensor_reduce(gm[:, :].rearrange("p (h o) -> p h o", o=1),
                                        K.AD[:, 0:TILES - 1, 0:4].rearrange("p t h -> p h t"), AX.X, ALU.max))
                ch.link(V.tensor_scalar(gt[:, :], K.AD[:, TILES - 1, 0:4], K.vneg[:, 0:1], None, ALU.add))
                V.tensor_tensor(gm[:, :], gm[:, :], gt[:, :], ALU.max).then_inc(gm_ready, 1)
                v.wait_ge(gm_all, 1)
                ch.link(V.tensor_copy(adm[:, :, 0:4], ADs))
                ch.link(V.tensor_tensor(adm[:, :, 4:8], ADs, gt[:, :].rearrange("p (o h) -> p o h", o=1).to_broadcast([P, TILES, HEADS]), ALU.add))
                ch.link(V.scalar_tensor_tensor(adm[:, :, 4:8], adm[:, :, 4:8], 0.2, adm[:, :, 4:8], ALU.mult, ALU.max))
                ch.link(V.tensor_tensor(exs[:, :, :], AS, ADs, ALU.add))
                ch.link(V.scalar_tensor_tensor(exs[:, :, :], exs[:, :, :], 0.2, exs[:, :, :], ALU.mult, ALU.max))
                ch.link(V.tensor_tensor(exs[:, :, :], exs[:, :, :], adm[:, :, 4:8], ALU.subtract))
                V.tensor_scalar(exs[:, :, :], exs[:, :, :], 0.0, None, ALU.min).then_inc(self_z, 1)

            @block.gpsimd
            def _(gp):
                gp.wait_ge(gm_ready, 1)
                nc.gpsimd.partition_all_reduce(gt[:, :], gm[:, :], P, bass.bass_isa.ReduceOp.max).then_inc(gm_all, 1)

            @block.scalar
            def _(act):
                act.wait_ge(self_z, 1)
                nc.scalar.activation(exs[:, :, :], exs[:, :, :], ACT.Exp)

        idx = [sb(f"idx{j}", [P, CHUNKS[j]], I32) for j in J]
        dcol = [sb(f"dcol{j}", [P, CHUNKS[j]]) for j in J]
        drow = [sb(f"drow{j}", [P, CHUNKS[j] * P]) for j in J]
        G = [sb(f"G{j}", [P, CHUNKS[j], DIM + 4]) for j in J]
        OH = [sb(f"OH{j}", [P, CHUNKS[j], P]) for j in J]
        OT = [sb(f"OT{j}", [P, CHUNKS[j], P]) for j in J]
        Z = [sb(f"Z{j}", [P, CHUNKS[j], HEADS]) for j in J]
        own = sb("own", [P, DIM + 4])
        cur = sb("cur", [P, 8])
        TI = sb("TI", [P, P])
        TP = sb("TP", [P, 1])
        ACC = sb("ACC", [P, DIM + 4])
        bias = sb("bias", [P, DIM])
        res = sb("res", [P, DIM])
        rec = sb("rec", [P, HEADS])
        pAd = [pb(f"pAd{j}", [P, 512]) for j in J]
        pAgg = pb("pAgg", [P, 512])

        bias_ld = sem("bias_ld")
        init = sem("init")
        src_in = [sem(f"src_in{j}") for j in J]
        dst_in = [sem(f"dst_in{j}") for j in J]
        gathered = [sem(f"gathered{j}") for j in J]
        onehots = [sem(f"onehots{j}") for j in J]
        agg_done = [sem(f"agg_done{j}") for j in J]
        own_in = sem("own_in")
        own_used = sem("own_used")
        cur_ready = sem("cur_ready")
        ad_ready = sem("ad_ready")
        z_ready = sem("z_ready")
        ex_ready = sem("ex_ready")
        msg_ready = sem("msg_ready")
        acc_done = sem("acc_done")
        chain = sem("chain")
        passed = sem("passed")
        NJ = len(CHUNKS)
        lifts = (own_used, z_ready, acc_done, *agg_done)
        START, STEP, END = 3, 3 * NJ, 5

        def tile_steps(eng, t):
            n = eng.value_load(K.ET[0:1, bass.ds(t, 1), 1:2].rearrange("o a b -> o (a b)"), min_val=1, max_val=MAXSTEPS)
            s0 = eng.value_load(K.ET[0:1, bass.ds(t, 1), 2:3].rearrange("o a b -> o (a b)"), min_val=0, max_val=TILES * MAXSTEPS)
            return n, s0

        with nc.Block() as block:
            @block.sync
            def _(sp):
                sp.dma_start(bias[:, :], bias_in.partition_broadcast(P)).then_inc(bias_ld, 16)
                with sp.Fori(0, TILES) as t:
                    n, s0 = tile_steps(sp, t)
                    base = sp.value_load(K.ET[0:1, bass.ds(t, 1), 0:1].rearrange("o a b -> o (a b)"), min_val=0, max_val=EDGES - GRAN)
                    r0 = sp.snap(t * P)
                    freed(sp, own_used, t)
                    sp.dma_start(own[:, :], K.T1[bass.ds(r0, P), :]).then_inc(own_in, 16)
                    with sp.Fori(0, n) as g:
                        s = sp.snap(s0 + g)
                        e0 = nc.s_assert_within(sp.snap(base + g * SE), 0, EDGES, skip_runtime_bounds_check_because=
                                                "a step begins before its tile's last edge, and SE edges of padding follow the last")
                        at = [sp.snap(e0 + OFFS[j]) for j in J]
                        for j in J:
                            freed(sp, agg_done[j], s)
                            ne = CHUNKS[j] * P
                            sp.dma_start(idx[j][:, :], K.SRCP[bass.ds(at[j], ne)].rearrange("(p c) -> p c", p=P)).then_inc(src_in[j], 16)
                            sp.dma_start(dcol[j][:, :], K.DSTP[bass.ds(at[j], ne)].rearrange("(p c) -> p c", p=P)).then_inc(dst_in[j], 16)
                            sp.dma_start(drow[j][:, :], K.DSTP[bass.ds(at[j], ne)].partition_broadcast(P)).then_inc(dst_in[j], 16)

            @block.gpsimd
            def _(gp):
                lift(gp, lifts)
                with gp.Fori(0, TILES) as t:
                    n, s0 = tile_steps(gp, t)
                    with gp.Fori(0, n) as g:
                        s = gp.snap(s0 + g)
                        for j in J:
                            gp.wait_ge(src_in[j], s * 16 + 16)
                            freed(gp, agg_done[j], s)
                            gp.sem_inc(passed, 1)
                            for c in range(CHUNKS[j]):
                                gp.indirect_dma_start(G[j][:, c, :], None, K.T1,
                                                      bass.IndirectOffsetOnAxis(ap=idx[j][:, c:c + 1], axis=0)).then_inc(gathered[j], 16)

            @block.vector
            def _(v):
                V = nc.vector

                def one_hots(s, j):
                    c = CHUNKS[j]
                    v.wait_ge(dst_in[j], s * 32 + 32)
                    V.tensor_tensor(OH[j][:, :, :], dcol[j][:, :].rearrange("p (c o) -> p c o", o=1).to_broadcast([P, c, P]),
                                    TI[:, :].rearrange("p (o n) -> p o n", o=1).to_broadcast([P, c, P]), ALU.is_equal)
                    V.tensor_scalar(OT[j][:, :, :], drow[j][:, :].rearrange("n (p c) -> n c p", c=c), TP[:, 0:1], None,
                                    ALU.is_equal).then_inc(onehots[j], 1)

                def scores(ch, s, j):
                    c = CHUNKS[j]
                    v.wait_ge(gathered[j], s * (16 * c) + 16 * c)
                    v.wait_ge(ad_ready, s * NJ + j + 1)
                    ad = pAd[j][:, 0:8 * c].rearrange("p (c k) -> p c k", k=8)
                    ch.link(V.tensor_tensor(Z[j][:, :, :], G[j][:, :, DIM:DIM + 4], ad[:, :, 0:4], ALU.add))
                    ch.link(V.scalar_tensor_tensor(Z[j][:, :, :], Z[j][:, :, :], 0.2, Z[j][:, :, :], ALU.mult, ALU.max))
                    ch.link(V.tensor_tensor(Z[j][:, :, :], Z[j][:, :, :], ad[:, :, 4:8], ALU.subtract))
                    V.tensor_scalar(Z[j][:, :, :], Z[j][:, :, :], 0.0, None, ALU.min).then_inc(z_ready, 1)

                def weigh(s, j):
                    c = CHUNKS[j]
                    v.wait_ge(ex_ready, s * NJ + j + 1)
                    rows = G[j][:, :, 0:DIM].rearrange("p c (h k) -> p c h k", h=HEADS)
                    ex = G[j][:, :, DIM:DIM + 4].rearrange("p c (h o) -> p c h o", o=1).to_broadcast([P, c, HEADS, CH])
                    V.tensor_tensor(rows, rows, ex, ALU.mult).then_inc(msg_ready, 1)

                V.tensor_scalar(TI[:, :], K.iota[:, 0:P], -float(P), None, ALU.add).then_inc(init, 1)
                V.tensor_scalar(TP[:, :], K.pid[:, :], -float(P), None, ALU.add).then_inc(init, 1)
                v.wait_ge(init, 2)
                v.wait_ge(bias_ld, 16)
                with v.Fori(0, TILES) as t:
                    n, s0 = tile_steps(v, t)
                    ch = Chain(v, chain, t * (START + END) + s0 * STEP)
                    ex_t = exs[:, bass.ds(t, 1), :].rearrange("p o h -> p (o h)")
                    v.wait_ge(own_in, t * 16 + 16)
                    V.tensor_tensor(ACC[:, 0:DIM].rearrange("p (h k) -> p h k", h=HEADS),
                                    own[:, 0:DIM].rearrange("p (h k) -> p h k", h=HEADS),
                                    ex_t.rearrange("p (h o) -> p h o", o=1).to_broadcast([P, HEADS, CH]), ALU.mult).then_inc(own_used, 1)
                    ch.mark(V.tensor_copy(ACC[:, DIM:DIM + 4], ex_t))
                    ch.mark(V.tensor_scalar(TI[:, :], TI[:, :], float(P), None, ALU.add))
                    ch.mark(V.tensor_scalar(TP[:, :], TP[:, :], float(P), None, ALU.add))
                    V.tensor_copy(cur[:, :], adm[:, bass.ds(t, 1), :].rearrange("p o k -> p (o k)")).then_inc(cur_ready, 1)
                    ch.settle()
                    freed(v, own_used, t + 1)
                    v.sem_inc(passed, 1)
                    assert ch.n == START
                    with v.Fori(0, n) as g:
                        s = v.snap(s0 + g)
                        cs = Chain(v, chain, t * (START + END) + START + s * STEP)
                        one_hots(s, 0)
                        one_hots(s, 1)
                        scores(cs, s, 0)
                        one_hots(s, 2)
                        weigh(s, 0)
                        scores(cs, s, 1)
                        weigh(s, 1)
                        scores(cs, s, 2)
                        weigh(s, 2)
                        freed(v, agg_done[NJ - 1], s + 1)
                        V.tensor_tensor(ACC[:, :], ACC[:, :], pAgg[:, 0:DIM + 4], ALU.add).then_inc(acc_done, 1)
                        freed(v, acc_done, s + 1)
                        assert cs.n == STEP
                    ch = Chain(v, chain, t * (START + END) + START + (s0 + n) * STEP)
                    ch.link(V.tensor_scalar(rec[:, :], ACC[:, DIM:DIM + 4], 1e-30, None, ALU.add))
                    ch.link(V.reciprocal(rec[:, :], rec[:, :]))
                    ch.link(V.tensor_tensor(res[:, :].rearrange("p (h k) -> p h k", h=HEADS),
                                            ACC[:, 0:DIM].rearrange("p (h k) -> p h k", h=HEADS),
                                            rec[:, :].rearrange("p (h o) -> p h o", o=1).to_broadcast([P, HEADS, CH]), ALU.mult))
                    ch.link(V.tensor_tensor(res[:, :], res[:, :], bias[:, :], ALU.add))
                    Xt = K.X[:, bass.ds(t, 1), :].rearrange("p o d -> p (o d)")
                    ch.link(V.scalar_tensor_tensor(Xt, res[:, :], 0.0, Xt, ALU.max, ALU.add))
                    assert ch.n == END

            @block.scalar
            def _(act):
                with act.Fori(0, TILES) as t:
                    n, s0 = tile_steps(act, t)
                    with act.Fori(0, n) as g:
                        s = act.snap(s0 + g)
                        for j in J:
                            freed(act, z_ready, s * NJ + j + 1)
                            nc.scalar.activation(G[j][:, :, DIM:DIM + 4], Z[j][:, :, :], ACT.Exp).then_inc(ex_ready, 1)

            @block.tensor
            def _(pe):
                with pe.Fori(0, TILES) as t:
                    n, s0 = tile_steps(pe, t)
                    pe.wait_ge(cur_ready, t + 1)
                    pe.sem_inc(passed, 1)
                    with pe.Fori(0, n) as g:
                        s = pe.snap(s0 + g)
                        for j in J:
                            pe.wait_ge(onehots[j], s + 1)
                            freed(pe, z_ready, s * NJ)
                            for c in range(CHUNKS[j]):
                                last = nc.tensor.matmul(pAd[j][:, 8 * c:8 * c + 8], OT[j][:, c, :], cur[:, :], start=True, stop=True)
                            last.then_inc(ad_ready, 1)
                        freed(pe, acc_done, s)
                        for j in J:
                            pe.wait_ge(msg_ready, s * NJ + j + 1)
                            for c in range(CHUNKS[j]):
                                last = nc.tensor.matmul(pAgg[:, 0:DIM + 4], OH[j][:, c, :], G[j][:, c, :],
                                                        start=(j == 0 and c == 0), stop=(j == NJ - 1 and c == CHUNKS[j] - 1))
                            last.then_inc(agg_done[j], 1)


def finish(K, out, combine):
    nc = K.nc
    with ExitStack() as stack:
        sb, pb, sem = K.tools(stack, "f")
        rows = sb("rows", [P, BODY, 2 * DIM])
        gathered = [sem(f"gathered{j}") for j in range(BODY)]
        half = sem("half")
        done = sem("done")
        stored = sem("stored")
        with nc.Block() as block:
            @block.gpsimd
            def _(gp):
                for t in range(TILES if combine else 0):
                    j = t % BODY
                    if t >= BODY:
                        gp.wait_ge(done, t - BODY + 1)
                    for k in range(2):
                        gp.indirect_dma_start(rows[:, j, k * DIM:(k + 1) * DIM], None, K.YS,
                                              bass.IndirectOffsetOnAxis(ap=K.POS[:, t, k:k + 1], axis=0)).then_inc(gathered[j], 16)

            @block.vector
            def _(v):
                if not combine:
                    return
                with v.Fori(0, TRIPS) as i:
                    for j in range(BODY):
                        Xt = K.X[:, bass.ds(i * BODY + j, 1), :].rearrange("p o d -> p (o d)")
                        Wt = K.WT[:, bass.ds(i * BODY + j, 1), :].rearrange("p o d -> p (o d)")
                        v.wait_ge(gathered[j], i * 32 + 32)
                        nc.vector.scalar_tensor_tensor(Xt, rows[:, j, 0:DIM], Wt[:, 0:1], Xt, ALU.mult, ALU.add).then_inc(half, 1)
                        v.wait_ge(half, i * BODY + j + 1)
                        nc.vector.scalar_tensor_tensor(Xt, rows[:, j, DIM:2 * DIM], Wt[:, 1:2], Xt, ALU.mult, ALU.add).then_inc(done, 1)

            @block.sync
            def _(sp):
                for i in range(TRIPS):
                    a, b = i * BODY, min((i + 1) * BODY, TILES - 1)
                    if combine:
                        sp.wait_ge(done, (i + 1) * BODY)
                    sp.dma_start(out[a * P:b * P, :].rearrange("(t p) d -> p t d", p=P), K.X[:, a:b, :]).then_inc(stored, 16)
                sp.dma_start(out[(TILES - 1) * P:NODES, :], K.X[0:TAIL, TILES - 1, :]).then_inc(stored, 16)
                sp.wait_ge(stored, 16 * (TRIPS + 1))


_INS = ['x', 'src', 'dst', 'L0_gnn_weight', 'L0_gnn_attn_l', 'L0_gnn_attn_r', 'L0_ffn_router_w1', 'L0_ffn_router_b1',
        'L0_ffn_router_w2', 'L0_ffn_router_b2', 'L0_ffn_expert_w1', 'L0_ffn_expert_b1', 'L0_ffn_expert_w2',
        'L0_ffn_expert_b2', 'L0_ffn_expert_w3', 'L0_ffn_expert_b3', 'L1_gnn_W', 'L1_gnn_att_src', 'L1_gnn_att_dst',
        'L1_gnn_bias', 'L1_ffn_Wg', 'L1_ffn_bg', 'L1_ffn_W1', 'L1_ffn_b1', 'L1_ffn_W2', 'L1_ffn_b2']


def kernel(**inputs):
    import numpy as _np
    import concourse.bacc as _bacc
    from concourse import mybir as _mybir
    from concourse.bass_utils import run_bass_kernel_spmd as _run

    nc = _bacc.Bacc("TRN2", target_bir_lowering=False, num_devices=1)
    arrays, args = {}, {}
    for name in _INS:
        a = _np.ascontiguousarray(inputs[name])
        arrays[f"in_{name}_dram"] = a
        args[name] = nc.dram_tensor(f"in_{name}_dram", a.shape, _mybir.dt.from_np(a.dtype), kind="ExternalInput").ap()
    out = nc.dram_tensor("out_dram", (NODES, DIM), _mybir.dt.float32, kind="ExternalOutput").ap()
    gnn_moe(nc, out, **args)
    r = _run(nc, [arrays], core_ids=[0])
    return r.results[0]["out_dram"]
```

```python
import concourse.bass as bass
from concourse import mybir
from contextlib import ExitStack

F32 = mybir.dt.float32
I32 = mybir.dt.int32
BF16 = mybir.dt.bfloat16
ALU = mybir.AluOpType
ACT = mybir.ActivationFunctionType
AX = mybir.AxisListType

P = 128
NODES, DIM = 6250, 256
EDGES = 100000
HEADS, CH = 4, 64
TILES = -(-NODES // P)
TAIL = NODES - (TILES - 1) * P
BODY = 7
TRIPS = TILES // BODY
assert TRIPS * BODY == TILES
KC = DIM // P
EPS = 1e-5

MT = 256
SUB = MT // P
E0, H0, R0 = 6, 256, 128
E1, H1 = 8, 1024
WIDE = DIM + 1
NODEROWS = TILES * P
MAXT = -(-NODES // MT)
CAP = (MAXT + 1) * MT
NT = (2 * NODES) // MT + E1 + 2
BLANK = max(E0, E1) * CAP
DUMP = BLANK + MT
YDUMP = 2 * NODEROWS

CHUNKS = (6, 6, 5)
OFFS = (0, 6 * P, 12 * P)
SE = sum(CHUNKS) * P
GRAN = 32
NGRAN = EDGES // GRAN
EROWS = 125
ECOLS = EDGES // EROWS
GPR = ECOLS // GRAN
SEG = SE // GRAN
MAXSTEPS = -(-NGRAN // SEG)
HUGE = 1.0e30


class Shared:
    pass


def lift(eng, sems):
    for s in sems:
        eng.sem_inc(s, 1)


def freed(eng, sem, n):
    eng.wait_ge(sem, n + 1)


class Chain:

    def __init__(self, eng, sem, base=0):
        self.eng, self.sem, self.base, self.n = eng, sem, base, 0

    def mark(self, ins):
        self.n += 1
        ins.then_inc(self.sem, 1)

    def settle(self):
        self.eng.wait_ge(self.sem, self.base + self.n)

    def link(self, ins):
        self.mark(ins)
        self.settle()


def gnn_moe(nc, out, x, src, dst, L0_gnn_weight, L0_gnn_attn_l, L0_gnn_attn_r, L0_ffn_router_w1, L0_ffn_router_b1, L0_ffn_router_w2, L0_ffn_router_b2, L0_ffn_expert_w1, L0_ffn_expert_b1, L0_ffn_expert_w2, L0_ffn_expert_b2, L0_ffn_expert_w3, L0_ffn_expert_b3, L1_gnn_W, L1_gnn_att_src, L1_gnn_att_dst, L1_gnn_bias, L1_ffn_Wg, L1_ffn_bg, L1_ffn_W1, L1_ffn_b1, L1_ffn_W2, L1_ffn_b2):
    with ExitStack() as whole:
        K = Shared()
        K.nc = nc

        def tools(stack, tag):
            def sb(name, shape, dt=F32):
                return stack.enter_context(nc.sbuf_tensor(f"{tag}_{name}", shape, dt))

            def pb(name, shape, dt=F32):
                return stack.enter_context(nc.psum_tensor(f"{tag}_{name}", shape, dt))

            used = []

            def sem(name, indirect=False):
                if indirect:
                    return whole.enter_context(nc.semaphore(f"{tag}_{name}"))
                used.append(stack.enter_context(nc.semaphore(f"{tag}_{name}")))
                return used[-1]

            def clear():
                with nc.Block() as block:
                    @block.gpsimd
                    def _(gp):
                        for s in used:
                            gp.sem_clear(s)

            stack.callback(clear)
            return sb, pb, sem

        K.tools = tools
        sb, pb, sem = tools(whole, "g")

        def dram(name, shape, dt=F32):
            return nc.dram_tensor(name, shape, dt, kind="Internal").ap()

        K.T0 = dram("xt_ar", [TILES * P, DIM + 4])
        K.AL = dram("al", [TILES * P, 4])
        K.T1 = dram("h_as", [TILES * P, DIM + 4])
        K.XS = dram("slot_rows", [DUMP + 2 * P, WIDE])
        K.YS = dram("expert_out", [YDUMP + (max(E0, E1) + 1) * MT, DIM])
        K.SRCP = dram("src_padded", [EDGES + SE], I32)
        K.DSTP = dram("dst_padded", [EDGES + SE])
        K.GR = dram("granule_range", [2, NGRAN])
        K.RT = dram("tile_range", [TILES, 2])

        K.X = sb("x", [P, TILES, DIM])
        K.ident = sb("ident", [P, P])
        K.iota = sb("iota", [P, 512])
        K.pid = sb("pid", [P, 1])
        K.valid = sb("valid", [P, 1])
        K.valids = sb("valids", [P, TILES, 1])
        K.dump = sb("dump", [P, TILES, 2])
        K.vneg = sb("vneg", [P, 1])
        K.eps = sb("eps", [P, 1])
        K.tri = sb("tri", [P, P], BF16)
        K.ones = sb("ones", [P, P], BF16)
        K.onesf = sb("onesf", [P, TILES])
        K.POS = sb("slot_of", [P, TILES, 2], I32)
        K.WT = sb("weight_of", [P, TILES, 2])
        K.TE = sb("slot_tiles", [P, NT, 4], I32)
        K.PADS = sb("pads", [P, E1], I32)
        K.LAST = sb("last_pair", [P, 1], I32)
        K.ET = sb("edge_steps", [1, TILES, 3], I32)
        K.AD = sb("as_ad", [P, TILES, 8])

        K.dstI = sb("dst_first", [P, TILES], I32)
        K.srcI = sb("src_first", [P, TILES], I32)

        setup(K, x, src, dst)
        edge_ranges(K)
        project(K, "a0", None, gat_weights=(L0_gnn_weight, L0_gnn_attn_r, L0_gnn_attn_l))
        project(K, "a1", "attn0", router=(L0_ffn_router_w1, L0_ffn_router_b1, L0_ffn_router_w2, L0_ffn_router_b2))
        experts(K, "e0", E0, L0_ffn_expert_w1, L0_ffn_expert_b1, H0, ACT.Relu,
                L0_ffn_expert_w2, L0_ffn_expert_b2, L0_ffn_expert_w3, L0_ffn_expert_b3)
        project(K, "b0", "combine", gat_weights=(L1_gnn_W, L1_gnn_att_src, L1_gnn_att_dst))
        attention(K, L1_gnn_bias)
        project(K, "b1", None, gate=(L1_ffn_Wg, L1_ffn_bg))
        experts(K, "e1", E1, L1_ffn_W1, L1_ffn_b1, H1, ACT.Gelu, None, None, L1_ffn_W2, L1_ffn_b2)
        finish(K, out)


def setup(K, x, src, dst):
    nc = K.nc
    with ExitStack() as stack:
        sb, pb, sem = K.tools(stack, "s")
        zero = sb("zero", [P, DIM])
        vdump = sb("vdump", [P, 2])
        dload = sb("dload", [EROWS, ECOLS], I32)
        dflt = sb("dflt", [EROWS, ECOLS])
        rng = sb("rng", [EROWS, 2, GPR])
        padf = sb("padf", [P, SE // P])
        padi = sb("padi", [P, SE // P], I32)
        made = sem("made")
        loaded = sem("loaded")
        dst_in = sem("dst_in")
        ready = sem("ready")
        stored = sem("stored")
        with nc.Block() as block:
            @block.gpsimd
            def _(gp):
                for n, (t, pat) in enumerate(((K.iota, [[1, 512]]), (K.pid, [[1, 1]]))):
                    nc.gpsimd.iota(t[:, :], pattern=pat, base=0, channel_multiplier=n,
                                   allow_small_or_imprecise_dtypes=True).then_inc(made, 1)
                nc.gpsimd.memset(K.ident[:, :], 0.0).then_inc(made, 1)
                nc.gpsimd.memset(K.ones[:, :], 1.0).then_inc(made, 1)
                gp.wait_ge(made, 4)
                nc.gpsimd.affine_select(out=K.ident[:, :], in_=K.ident[:, :], compare_op=ALU.not_equal, fill=1.0,
                                        base=0, pattern=[[-1, P]], channel_multiplier=1).then_inc(made, 1)
                nc.gpsimd.affine_select(out=K.tri[:, :], in_=K.ones[:, :], compare_op=ALU.is_gt, fill=0.0,
                                        base=0, pattern=[[1, P]], channel_multiplier=-1).then_inc(made, 1)

            @block.vector
            def _(v):
                ch = Chain(v, ready)
                ch.mark(nc.vector.memset(K.X[:, TILES - 1, :], 0.0))
                ch.mark(nc.vector.memset(zero[:, :], 0.0))
                ch.mark(nc.vector.memset(padf[:, :], -1.0))
                ch.mark(nc.vector.memset(padi[:, :], 0))
                ch.mark(nc.vector.memset(K.dstI[:, TILES - 1:TILES], 0))
                ch.mark(nc.vector.memset(K.srcI[:, TILES - 1:TILES], 0))
                ch.mark(nc.vector.memset(K.eps[:, :], EPS))
                ch.mark(nc.vector.memset(K.onesf[:, :], 1.0))
                ch.mark(nc.vector.memset(K.valids[:, :, :], 1.0))
                ch.mark(nc.vector.memset(K.dump[:, :, :], 0.0))
                v.wait_ge(made, 6)
                ch.link(nc.vector.tensor_scalar(K.valid[:, :], K.pid[:, :], float(TAIL), None, ALU.is_lt))
                ch.link(nc.vector.tensor_scalar(K.vneg[:, :], K.valid[:, :], -1.0, HUGE, ALU.add, ALU.mult))
                for k in range(2):
                    ch.link(nc.vector.tensor_scalar(vdump[:, k:k + 1], K.valid[:, :], -1.0, -1.0, ALU.add, ALU.mult))
                    ch.link(nc.vector.scalar_tensor_tensor(K.dump[:, TILES - 1, k:k + 1], K.pid[:, :], float(DUMP + k * P),
                                                           vdump[:, k:k + 1], ALU.add, ALU.mult))
                ch.link(nc.vector.tensor_copy(K.valids[:, TILES - 1, :], K.valid[:, :]))
                v.wait_ge(dst_in, 16)
                ch.link(nc.vector.tensor_copy(dflt[:, :], dload[:, :]))
                gv = dflt[:, :].rearrange("p (g e) -> p g e", e=GRAN)
                ch.mark(nc.vector.tensor_reduce(rng[:, 0, :], gv, AX.X, ALU.min))
                ch.mark(nc.vector.tensor_reduce(rng[:, 1, :], gv, AX.X, ALU.max))
                assert ch.n == 20

            @block.sync
            def _(sp):
                sp.dma_start(dload[:, :], dst.rearrange("(p e) -> p e", p=EROWS)).then_inc(dst_in, 16)
                full = (TILES - 1) * P
                for g in range(6):
                    sp.dma_start(K.X[:, 8 * g:8 * g + 8, :],
                                 x[8 * g * P:8 * (g + 1) * P, :].rearrange("(t p) d -> p t d", p=P)).then_inc(loaded, 16)
                sp.wait_ge(ready, 6)
                sp.dma_start(K.X[0:TAIL, TILES - 1, :], x[full:NODES, :]).then_inc(loaded, 16)
                for t, s in ((K.dstI, dst), (K.srcI, src)):
                    sp.dma_start(t[:, 0:TILES - 1], s[0:full].rearrange("(t p) -> p t", p=P),
                                 allow_slow_non_contiguous=True).then_inc(loaded, 16)
                    sp.dma_start(t[0:TAIL, TILES - 1:TILES], s[full:NODES].rearrange("(p o) -> p o", o=1)).then_inc(loaded, 16)
                sp.wait_ge(loaded, 16 * 11)

            @block.scalar
            def _(act):
                act.dma_start(K.SRCP[0:EDGES].rearrange("(p e) -> p e", p=EROWS),
                              src.rearrange("(p e) -> p e", p=EROWS)).then_inc(stored, 16)
                act.wait_ge(ready, 6)
                act.dma_start(K.SRCP[EDGES:EDGES + SE].rearrange("(p e) -> p e", p=P), padi[:, :]).then_inc(stored, 16)
                act.dma_start(K.DSTP[EDGES:EDGES + SE].rearrange("(p e) -> p e", p=P), padf[:, :]).then_inc(stored, 16)
                for k in range(2):
                    a = k * NODEROWS + NODES
                    act.dma_start(K.YS[a:(k + 1) * NODEROWS, :], zero[0:NODEROWS - NODES, :]).then_inc(stored, 16)
                act.wait_ge(ready, 18)
                act.dma_start(K.DSTP[0:EDGES].rearrange("(p e) -> p e", p=EROWS), dflt[:, :]).then_inc(stored, 16)
                act.wait_ge(ready, 20)
                for k in range(2):
                    act.dma_start(K.GR[k, :].rearrange("(p g) -> p g", p=EROWS), rng[:, k, :]).then_inc(stored, 16)
                act.wait_ge(stored, 16 * 8)


def edge_ranges(K):
    nc = K.nc
    with ExitStack() as stack:
        sb, pb, sem = K.tools(stack, "er")
        lo = sb("lo", [TILES, NGRAN])
        hi = sb("hi", [TILES, NGRAN])
        idx = sb("idx", [TILES, NGRAN])
        first = sb("first", [TILES, 1])
        last = sb("last", [TILES, 1])
        span = sb("span", [TILES, 2])
        cnt = sb("cnt", [TILES, 1])
        cmp = sb("cmp", [TILES, MAXSTEPS])
        row = sb("row", [1, TILES, 2])
        inc = sb("inc", [1, TILES])
        ranges_in = sem("ranges_in")
        index_made = sem("index_made")
        step = sem("step")
        span_out = sem("span_out")
        row_in = sem("row_in")
        with nc.Block() as block:
            @block.sync
            def _(sp):
                sp.dma_start(lo[:, :], K.GR[0:1, :].rearrange("o g -> (o g)").partition_broadcast(TILES)).then_inc(ranges_in, 16)
                sp.dma_start(hi[:, :], K.GR[1:2, :].rearrange("o g -> (o g)").partition_broadcast(TILES)).then_inc(ranges_in, 16)
                sp.wait_ge(step, 13)
                sp.dma_start(K.RT[:, :], span[:, :]).then_inc(span_out, 16)
                sp.wait_ge(span_out, 16)
                sp.dma_start(row[0:1, :, :], K.RT.rearrange("(o t) k -> o t k", o=1)).then_inc(row_in, 16)
                sp.wait_ge(row_in, 16)

            @block.gpsimd
            def _(gp):
                nc.gpsimd.iota(idx[:, :], pattern=[[1, NGRAN]], base=0, channel_multiplier=0,
                               allow_small_or_imprecise_dtypes=True).then_inc(index_made, 1)

            @block.vector
            def _(v):
                ch = Chain(v, step)
                v.wait_ge(ranges_in, 32)
                v.wait_ge(index_made, 1)
                ch.link(nc.vector.tensor_scalar(first[:, :], K.pid[0:TILES, :], float(P), None, ALU.mult))
                ch.link(nc.vector.tensor_scalar(last[:, :], first[:, :], float(P - 1), None, ALU.add))
                ch.link(nc.vector.tensor_scalar(hi[:, :], hi[:, :], first[:, 0:1], None, ALU.is_ge))
                ch.link(nc.vector.scalar_tensor_tensor(hi[:, :], lo[:, :], last[:, 0:1], hi[:, :], ALU.is_le, ALU.mult))
                ch.link(nc.vector.tensor_scalar(lo[:, :], hi[:, :], -2.0 * NGRAN, 2.0 * NGRAN, ALU.mult, ALU.add))
                ch.link(nc.vector.tensor_tensor(lo[:, :], lo[:, :], idx[:, :], ALU.add))
                ch.link(nc.vector.scalar_tensor_tensor(hi[:, :], idx[:, :], 1.0, hi[:, :], ALU.add, ALU.mult))
                ch.link(nc.vector.tensor_reduce(span[:, 0:1], lo[:, :], AX.X, ALU.min))
                ch.link(nc.vector.tensor_reduce(cnt[:, :], hi[:, :], AX.X, ALU.max))
                ch.link(nc.vector.tensor_scalar(span[:, 0:1], span[:, 0:1], float(NGRAN - 1), None, ALU.min))
                ch.link(nc.vector.tensor_scalar(cnt[:, :], cnt[:, :], span[:, 0:1], 1.0, ALU.subtract, ALU.max))
                ch.link(nc.vector.tensor_scalar(cmp[:, :], K.iota[0:TILES, 0:MAXSTEPS], float(SEG), cnt[:, 0:1],
                                                ALU.mult, ALU.is_lt))
                ch.link(nc.vector.tensor_reduce(span[:, 1:2], cmp[:, :], AX.X, ALU.add))
                assert ch.n == 13
                v.wait_ge(row_in, 16)
                ch.link(nc.vector.tensor_tensor_scan(inc[0:1, :], K.onesf[0:1, 0:TILES], row[0:1, :, 1], 0.0, ALU.mult, ALU.add))
                ch.mark(nc.vector.tensor_scalar(K.ET[0:1, :, 0], row[0:1, :, 0], float(GRAN), None, ALU.mult))
                ch.mark(nc.vector.tensor_copy(K.ET[0:1, :, 1], row[0:1, :, 1]))
                ch.mark(nc.vector.tensor_tensor(K.ET[0:1, :, 2], inc[0:1, :], row[0:1, :, 1], ALU.subtract))


def project(K, tag, pre, gat_weights=None, router=None, gate=None):
    nc = K.nc
    with ExitStack() as stack:
        sb, pb, sem = K.tools(stack, tag)
        routed = not gat_weights
        NC = DIM + 8 if gat_weights else (E0 if router else E1)
        stats = sb("stats", [P, BODY, 6])
        mv = sb("mv", [P, BODY, 2])
        std = sb("std", [P, BODY, 1])
        rstd = sb("rstd", [P, BODY, 1])
        yg = sb("yg", [P, BODY, DIM])
        yT = sb("yT", [P, BODY, KC, P])
        og = sb("og", [P, BODY, NC])
        w = sb("w", [P, KC, R0 if router else NC])
        if gat_weights:
            att = sb("att", [P, 2, DIM])
            prod = sb("prod", [P, 2, DIM])
        else:
            bias = sb("bias", [P, NC])
            E = NC
            Y = sb("Y", [P, TILES, WIDE])
            token = sb("token", [P, TILES])
            lg = sb("lg", [P, BODY, E])
            p = sb("p", [P, BODY, E])
            c = [sb(f"c{k}", [P, BODY, E]) for k in range(2)]
            M = [sb(f"M{k}", [P, BODY, E]) for k in range(2)]
            r = sb("r", [P, BODY, 1])
            rev = sb("rev", [P, E])
            region = sb("region", [P, E])
            Mb = sb("Mb", [P, BODY, E], BF16)
            before = sb("before", [P, E], BF16)
            here = sb("here", [P, E])
            rank = sb("rank", [P, BODY, E])
            pos = sb("pos", [P, BODY, 2])
            pr = pb("pr", [P, 512])
        if router:
            w2 = sb("w2", [P, NC])
            rb1 = sb("rb1", [P, 1])
            rhT = sb("rhT", [P, BODY, P])
            pR = [pb(f"pR{n}", [P, 512]) for n in range(2)]
        if pre == "attn0":
            rows = sb("rows", [P, BODY, DIM + 4])
            left = sb("left", [P, BODY, 4])
            z = sb("z", [P, BODY, 4])
            z1 = sb("z1", [P, BODY, 1])
            mix = sb("mix", [P, BODY, DIM])
            tmp = sb("tmp", [P, BODY, CH])
        if pre == "combine":
            rows = sb("rows", [P, 2, BODY, DIM])
        pT = [pb(f"pT{n}", [P, 512]) for n in range(2)]
        pO = [pb(f"pO{n}", [P, 512]) for n in range(2)]

        w_in = sem("w_in")
        w_ready = sem("w_ready")
        gathered = [sem(f"gathered{j}", indirect=True) for j in range(BODY)] if pre == "attn0" else None
        rows_in = sem("rows_in")
        rows_used = sem("rows_used")
        chain = sem("chain")
        exps_done = sem("exps_done")
        z_ready = sem("z_ready")
        stats_ready = sem("stats_ready")
        std_ready = sem("std_ready")
        y_ready = sem("y_ready")
        y_kept = sem("y_kept")
        pT_ready = sem("pT_ready")
        yT_ready = sem("yT_ready")
        pR_ready = sem("pR_ready")
        rh_ready = sem("rh_ready")
        pO_ready = sem("pO_ready")
        o_ready = sem("o_ready")
        stored = sem("stored")
        gate_sem = sem("passed")
        og_free = sem("og_free")
        token_made = sem("token_made")
        consts = sem("consts")
        exp_in = sem("exp_in")
        exp_out = sem("exp_out")
        masks = sem("masks")
        ranks = sem("ranks")
        slots_ready = sem("slots_ready")
        moved = sem("moved")
        sent = [sem(f"sent{k}", indirect=True) for k in range(2)] if routed else None
        count_in = sem("count_in")
        lifts = (rows_used, o_ready, pT_ready, y_kept, pO_ready, yT_ready, rh_ready, og_free)

        if routed:
            cnt = sb("cnt", [P, E])
            kt = sb("kt", [P, MAXT])
            cmp = sb("cmp", [P, E, MAXT])
            nt = sb("nt", [P, E])
            end = sb("end", [P, E])
            skip = sb("skip", [P, E])
            tj = sb("tj", [P, NT])
            cj = sb("cj", [P, NT, E])
            te = sb("te", [P, NT, 4])
            half = sb("half", [P, 1])
            c2 = sb("c2", [P, NT])

        def tables(ch):
            V = nc.vector
            v = ch.eng
            WT = K.WT
            v.sem_inc(count_in, 1)
            V.tensor_tensor(WT[:, :, 1:2], WT[:, :, 1:2], WT[:, :, 0:1], ALU.subtract).then_inc(exp_in, 1)
            ch.mark(V.tensor_scalar(kt[:, :], K.iota[:, 0:MAXT], float(MT), None, ALU.mult))
            ch.mark(V.tensor_scalar(tj[:, :], K.iota[:, 0:NT], float(MT), None, ALU.mult))
            v.wait_ge(ranks, TRIPS + 1)
            ch.link(V.tensor_copy(cnt[:, :], pr[:, 0:E]))
            ch.mark(V.tensor_tensor(K.PADS[:, 0:E], cnt[:, :], region[:, :], ALU.add))
            ch.link(V.tensor_tensor(cmp[:, :, :], cnt[:, :].rearrange("p (e o) -> p e o", o=1).to_broadcast([P, E, MAXT]),
                                    kt[:, :].rearrange("p (o k) -> p o k", o=1).to_broadcast([P, E, MAXT]), ALU.is_gt))
            ch.link(V.tensor_reduce(nt[:, :].rearrange("p (e o) -> p e o", o=1), cmp[:, :, :], AX.X, ALU.add))
            ch.mark(V.tensor_scalar(skip[:, :], nt[:, :], -float(MT), float(CAP), ALU.mult, ALU.add))
            ch.link(V.tensor_tensor_scan(end[:, :], K.onesf[:, 0:E], nt[:, :], 0.0, ALU.mult, ALU.add))
            ch.mark(V.tensor_scalar(c2[:, 1:NT], K.iota[:, 1:NT], 2.0, end[:, E - 1:E], ALU.mult, ALU.is_lt))
            ch.link(V.tensor_tensor(cj[:, :, :], end[:, :].rearrange("p (o e) -> p o e", o=1).to_broadcast([P, NT, E]),
                                    K.iota[:, 0:NT].rearrange("p (j o) -> p j o", o=1).to_broadcast([P, NT, E]), ALU.is_le))
            ch.mark(V.tensor_reduce(half[:, :], c2[:, 1:NT], AX.X, ALU.add))
            ch.link(V.tensor_reduce(te[:, :, 0:1], cj[:, :, :], AX.X, ALU.add))
            ch.mark(V.tensor_copy(K.LAST[:, :], half[:, :]))
            ch.link(V.tensor_tensor(cj[:, :, :], cj[:, :, :], skip[:, :].rearrange("p (o e) -> p o e", o=1).to_broadcast([P, NT, E]), ALU.mult))
            ch.mark(V.tensor_scalar(te[:, :, 0], te[:, :, 0], float(E - 1), None, ALU.min))
            ch.link(V.tensor_reduce(te[:, :, 1:2], cj[:, :, :], AX.X, ALU.add))
            ch.link(V.tensor_tensor(te[:, :, 1], te[:, :, 1], tj[:, :], ALU.add))
            ch.mark(V.tensor_scalar(te[:, :, 1], te[:, :, 1], float(E * CAP), None, ALU.min))
            ch.mark(V.memset(te[:, 0:2, 2:3], 1.0))
            ch.link(V.tensor_tensor(te[:, 2:NT, 2], te[:, 2:NT, 0], te[:, 0:NT - 2, 0], ALU.not_equal))
            for b in range(2):
                ch.mark(V.tensor_tensor_scan(te[:, b:NT:2, 3], K.onesf[:, 0:len(range(b, NT, 2))], te[:, b:NT:2, 2], 0.0, ALU.mult, ALU.add))
            ch.settle()
            ch.mark(V.tensor_copy(K.TE[:, :, :], te[:, :, :]))
            v.wait_ge(exp_out, TRIPS + 1 if router else 1)
            ch.link(V.tensor_scalar(WT[:, :, 0:1], WT[:, :, 1:2], 1.0, None, ALU.add))
            ch.link(V.reciprocal(WT[:, :, 0:1], WT[:, :, 0:1]))
            ch.mark(V.tensor_tensor(WT[:, :, 1:2], WT[:, :, 1:2], WT[:, :, 0:1], ALU.mult))

        n_w = 4 if gat_weights else (4 if router else 2)
        n_tables = (3 if tag == "a0" else 1) if gat_weights else 0

        def load_results(sp, i):
            at = [sp.snap(i * (BODY * P) + k * NODEROWS) for k in range(2)] if not isinstance(i, int) else [k * NODEROWS for k in range(2)]
            freed(sp, rows_used, i * BODY)
            for k in range(2):
                a = at[k] if not isinstance(i, int) else at[k]
                src = K.YS[bass.ds(a, BODY * P), :] if not isinstance(i, int) else K.YS[a:a + BODY * P, :]
                sp.dma_start(rows[:, k, :, :], src.rearrange("(t p) d -> p t d", p=P)).then_inc(rows_in, 16)

        def tiles(t, n):
            return slice(t, t + n) if isinstance(t, int) else bass.ds(t, n)

        with nc.Block() as block:
            @block.sync
            def _(sp):
                if gat_weights:
                    wd, first, second = gat_weights
                    for k in range(KC):
                        sp.dma_start(w[:, k, 0:DIM], wd[k * P:(k + 1) * P, :]).then_inc(w_in, 16)
                    for n, a in enumerate((first, second)):
                        sp.dma_start(att[:, n, :], a.rearrange("h c -> (h c)").partition_broadcast(P)).then_inc(w_in, 16)
                elif router:
                    r1, b1, r2, b2 = router
                    sp.dma_start(w[:, :, :], r1.rearrange("(k p) n -> p k n", p=P)).then_inc(w_in, 16)
                    sp.dma_start(rb1[:, :], b1.rearrange("(p o) -> p o", o=1)).then_inc(w_in, 16)
                    sp.dma_start(w2[:, :], r2).then_inc(w_in, 16)
                    sp.dma_start(bias[:, :], b2.partition_broadcast(P)).then_inc(w_in, 16)
                else:
                    wg, bg = gate
                    sp.dma_start(w[:, :, :], wg.rearrange("(k p) n -> p k n", p=P)).then_inc(w_in, 16)
                    sp.dma_start(bias[:, :], bg.partition_broadcast(P)).then_inc(w_in, 16)
                if gat_weights:
                    if pre == "combine":
                        load_results(sp, 0)
                    with sp.Fori(0, TRIPS) as i:
                        r0 = sp.snap(i * (BODY * P))
                        if pre == "combine":
                            with sp.If(i < TRIPS - 1):
                                load_results(sp, i + 1)
                        n_st = sp.snap((i + 1) * (32 if tag == "a0" else 16))
                        freed(sp, o_ready, i * BODY + BODY)
                        if tag == "a0":
                            sp.dma_start(K.T0[bass.ds(r0, BODY * P), :].rearrange("(t p) c -> p t c", p=P),
                                         og[:, :, 0:DIM + 4]).then_inc(stored, 16)
                            sp.dma_start(K.AL[bass.ds(r0, BODY * P), :].rearrange("(t p) c -> p t c", p=P),
                                         og[:, :, DIM + 4:DIM + 8]).then_inc(stored, 16)
                        else:
                            sp.dma_start(K.T1[bass.ds(r0, BODY * P), :].rearrange("(t p) c -> p t c", p=P),
                                         og[:, :, 0:DIM + 4]).then_inc(stored, 16)
                        sp.wait_ge(stored, n_st)
                        sp.sem_inc(og_free, 1)

            @block.gpsimd
            def _(gp):
                lift(gp, lifts)
                if routed:
                    nc.gpsimd.iota(token[:, :], pattern=[[P, TILES]], base=0, channel_multiplier=1,
                                   allow_small_or_imprecise_dtypes=True).then_inc(token_made, 1)

                def gather(i):
                    for j in range(BODY):
                        t = i * BODY + j
                        freed(gp, rows_used, max(0, t - BODY + 1))
                        gp.indirect_dma_start(rows[:, j, :], None, K.T0,
                                              bass.IndirectOffsetOnAxis(ap=K.dstI[:, t:t + 1], axis=0)).then_inc(gathered[j], 16)
                        gp.indirect_dma_start(left[:, j, :], None, K.AL,
                                              bass.IndirectOffsetOnAxis(ap=K.srcI[:, t:t + 1], axis=0)).then_inc(gathered[j], 16)

                def scatter(i, k):
                    gp.wait_ge(slots_ready, i + 1)
                    freed(gp, y_kept, (i + 1) * BODY)
                    if k == 1:
                        gp.wait_ge(moved, i + 1)
                    for t in range(i * BODY, (i + 1) * BODY):
                        gp.indirect_dma_start(K.XS, bass.IndirectOffsetOnAxis(ap=K.POS[:, t, k:k + 1], axis=0),
                                              Y[:, t, :], None).then_inc(sent[k], 16)

                late = 1 if pre == "attn0" else 0
                for i in range(TRIPS + 2):
                    if pre == "attn0" and i < TRIPS:
                        gather(i)
                    if routed and 0 <= i - late < TRIPS:
                        scatter(i - late, 0)
                    if routed and 0 <= i - late - 1 < TRIPS:
                        scatter(i - late - 1, 1)
                if routed:
                    for k in range(2):
                        gp.wait_ge(sent[k], 16 * TILES)

            @block.vector
            def _(v):
                if gat_weights:
                    ch = Chain(v, w_ready)
                    v.wait_ge(w_in, 16 * n_w)
                    for k in range(KC):
                        ch.link(nc.vector.tensor_tensor(prod[:, :, :], att[:, :, :],
                                                        w[:, k:k + 1, 0:DIM].to_broadcast([P, 2, DIM]), ALU.mult))
                        ch.link(nc.vector.tensor_reduce(w[:, k, DIM:DIM + 8],
                                                        prod[:, :, :].rearrange("p n (h c) -> p (n h) c", h=HEADS),
                                                        AX.X, ALU.add))
                if routed:
                    v.wait_ge(token_made, 1)
                    nc.vector.tensor_copy(Y[:, :, DIM], token[:, :]).then_inc(consts, 1)
                    nc.vector.tensor_scalar(rev[:, :], K.iota[:, 0:E], -1.0, float(E), ALU.mult, ALU.add).then_inc(consts, 1)
                    nc.vector.tensor_scalar(region[:, :], K.iota[:, 0:E], float(CAP), None, ALU.mult).then_inc(consts, 1)
                    nc.vector.memset(before[:, :], 0.0).then_inc(consts, 1)
                    v.wait_ge(consts, 4)

                def trip(i, per):
                    t0 = i * BODY
                    ch = Chain(v, chain, i * per)
                    if pre == "attn0":
                        for j in range(BODY):
                            v.wait_ge(gathered[j], i * 32 + 32)
                        ch.link(nc.vector.tensor_tensor(z[:, :, :], left[:, :, :], rows[:, :, DIM:DIM + 4], ALU.add))
                        ch.link(nc.vector.scalar_tensor_tensor(z[:, :, :], z[:, :, :], 0.01, z[:, :, :], ALU.mult, ALU.max))
                        ch.link(nc.vector.tensor_reduce(z1[:, :, :], z[:, :, :], AX.X, ALU.max))
                        nc.vector.tensor_tensor(z[:, :, :], z[:, :, :], z1[:, :, :].to_broadcast([P, BODY, 4]),
                                                ALU.subtract).then_inc(z_ready, 1)
                        v.wait_ge(exps_done, i + 1)
                        ch.link(nc.vector.tensor_reduce(z1[:, :, :], z[:, :, :], AX.X, ALU.add))
                        ch.link(nc.vector.reciprocal(z1[:, :, :], z1[:, :, :]))
                        ch.link(nc.vector.tensor_tensor(z[:, :, :], z[:, :, :], z1[:, :, :].to_broadcast([P, BODY, 4]), ALU.mult))
                        for j in range(BODY):
                            ch.mark(nc.vector.tensor_tensor(
                                mix[:, j, :].rearrange("p (h c) -> p h c", h=HEADS),
                                rows[:, j, 0:DIM].rearrange("p (h c) -> p h c", h=HEADS),
                                z[:, j, :].rearrange("p (h o) -> p h o", o=1).to_broadcast([P, HEADS, CH]), ALU.mult))
                        ch.settle()
                        for j in range(BODY):
                            ch.mark(nc.vector.tensor_reduce(
                                tmp[:, j, :].rearrange("p (c o) -> p c o", o=1),
                                mix[:, j, :].rearrange("p (h c) -> p c h", h=HEADS), AX.X, ALU.add))
                        ch.settle()
                        for j in range(BODY):
                            Xt = K.X[:, tiles(t0 + j, 1), :].rearrange("p o (h c) -> p (o h) c", h=HEADS)
                            nc.vector.tensor_tensor(Xt, Xt, tmp[:, j:j + 1, :].to_broadcast([P, HEADS, CH]),
                                                    ALU.add).then_inc(rows_used, 1)
                        freed(v, rows_used, i * BODY + BODY)
                        v.sem_inc(gate_sem, 1)
                    if pre == "combine":
                        v.wait_ge(rows_in, i * 32 + 32)
                        for j in range(BODY):
                            Xt = K.X[:, tiles(t0 + j, 1), :].rearrange("p o d -> p (o d)")
                            Wt = K.WT[:, tiles(t0 + j, 1), :].rearrange("p o d -> p (o d)")
                            ch.mark(nc.vector.scalar_tensor_tensor(Xt, rows[:, 0, j, :], Wt[:, 0:1], Xt, ALU.mult, ALU.add))
                        ch.settle()
                        for j in range(BODY):
                            Xt = K.X[:, tiles(t0 + j, 1), :].rearrange("p o d -> p (o d)")
                            Wt = K.WT[:, tiles(t0 + j, 1), :].rearrange("p o d -> p (o d)")
                            nc.vector.scalar_tensor_tensor(Xt, rows[:, 1, j, :], Wt[:, 1:2], Xt,
                                                           ALU.mult, ALU.add).then_inc(rows_used, 1)
                        freed(v, rows_used, i * BODY + BODY)
                        v.sem_inc(gate_sem, 1)
                    for j in range(BODY):
                        ch.mark(nc.vector.bn_stats(stats[:, j, :], K.X[:, tiles(t0 + j, 1), :].rearrange("p o d -> p (o d)")))
                    ch.settle()
                    v.sem_inc(gate_sem, 1)
                    for j in range(BODY):
                        last = nc.vector.bn_aggr(mv[:, j, :], stats[:, j, :])
                    last.then_inc(stats_ready, 1)
                    v.wait_ge(std_ready, i + 1)
                    ch.link(nc.vector.reciprocal(rstd[:, :, :], std[:, :, :]))
                    freed(v, pT_ready, i * BODY)
                    if not gat_weights:
                        freed(v, y_kept, i * BODY)
                    for j in range(BODY):
                        nc.vector.tensor_scalar(yg[:, j, :], K.X[:, tiles(t0 + j, 1), :].rearrange("p o d -> p (o d)"),
                                                mv[:, j, 0:1], rstd[:, j, :], ALU.subtract, ALU.mult).then_inc(y_ready, 1)
                    if not gat_weights:
                        for j in range(BODY):
                            freed(v, pO_ready, i * BODY + j + 1)
                            nc.vector.tensor_tensor(lg[:, j, :],
                                                    pO[j % 2][:, 0:NC], bias[:, :], ALU.add).then_inc(o_ready, 1)
                    if routed:
                        freed(v, o_ready, (i + 1) * BODY)
                        place(ch, i, t0)
                    return ch.n

                def place(ch, i, t0):
                    V = nc.vector
                    te = [P, BODY, E]

                    def of_expert(ap):
                        return ap[:, :].rearrange("p (o e) -> p o e", o=1).to_broadcast(te)

                    val = lg
                    if router:
                        ch.link(V.tensor_reduce(r[:, :, :], lg[:, :, :], AX.X, ALU.max))
                        V.tensor_tensor(p[:, :, :], lg[:, :, :], r[:, :, :].to_broadcast(te), ALU.subtract).then_inc(exp_in, 1)
                        v.wait_ge(exp_out, i + 1)
                        ch.link(V.tensor_reduce(r[:, :, :], p[:, :, :], AX.X, ALU.add))
                        ch.link(V.reciprocal(r[:, :, :], r[:, :, :]))
                        ch.link(V.tensor_tensor(p[:, :, :], p[:, :, :], r[:, :, :].to_broadcast(te), ALU.mult))
                        val = p
                    for k in range(2):
                        top = K.WT[:, tiles(t0, BODY), k:k + 1]
                        ch.link(V.tensor_reduce(top, val[:, :, :], AX.X, ALU.max))
                        ch.link(V.tensor_tensor(c[0][:, :, :], val[:, :, :], top.to_broadcast(te), ALU.is_equal))
                        ch.link(V.tensor_tensor(c[0][:, :, :], c[0][:, :, :], of_expert(rev), ALU.mult))
                        ch.link(V.tensor_reduce(r[:, :, :], c[0][:, :, :], AX.X, ALU.max))
                        ch.link(V.tensor_tensor(M[k][:, :, :], c[0][:, :, :], r[:, :, :].to_broadcast(te), ALU.is_equal))
                        if k == 0:
                            ch.link(V.scalar_tensor_tensor(val[:, :, :], M[0][:, :, :], -HUGE, val[:, :, :], ALU.mult, ALU.add))
                    for k in range(2):
                        ch.mark(V.tensor_tensor(M[k][:, :, :], M[k][:, :, :], K.valids[:, tiles(t0, BODY), :].to_broadcast(te), ALU.mult))
                    ch.settle()
                    V.tensor_tensor(Mb[:, :, :], M[0][:, :, :], M[1][:, :, :], ALU.add).then_inc(masks, 1)
                    v.wait_ge(ranks, i + 1)
                    ch.link(V.tensor_tensor(rank[:, :, :], pr[:, 0:BODY * E].rearrange("p (t e) -> p t e", e=E), of_expert(region), ALU.add))
                    ch.mark(V.tensor_reduce(here[:, :].rearrange("p (e o) -> p e o", o=1), Mb[:, :, :].rearrange("p t e -> p e t"), AX.X, ALU.add))
                    for k in range(2):
                        ch.mark(V.tensor_tensor(c[k][:, :, :], M[k][:, :, :], rank[:, :, :], ALU.mult))
                    ch.settle()
                    ch.mark(V.tensor_tensor(before[:, :], before[:, :], here[:, :], ALU.add))
                    for k in range(2):
                        ch.mark(V.tensor_reduce(pos[:, :, k:k + 1], c[k][:, :, :], AX.X, ALU.add))
                    ch.settle()
                    ch.link(V.tensor_tensor(pos[:, :, :], pos[:, :, :], K.dump[:, tiles(t0, BODY), :], ALU.add))
                    if not isinstance(i, int):
                        move(i - 1, t0 - BODY)
                    V.tensor_copy(K.POS[:, tiles(t0, BODY), :], pos[:, :, :]).then_inc(slots_ready, 1)

                def move(i, t0):
                    v.wait_ge(sent[0], i * (16 * BODY) + 16 * BODY)
                    nc.vector.tensor_scalar(Y[:, tiles(t0, BODY), DIM:DIM + 1].rearrange("p t o -> p (t o)"), token[:, tiles(t0, BODY)],
                                            float(NODEROWS), None, ALU.add).then_inc(moved, 1)

                per = trip(0, 0)
                with v.Fori(1, TRIPS) as i:
                    assert trip(i, per) == per
                if routed:
                    move(TRIPS - 1, (TRIPS - 1) * BODY)
                    tables(Chain(v, chain, TRIPS * per))

            @block.scalar
            def _(act):
                with act.Fori(0, TRIPS) as i:
                    t0 = i * BODY
                    if pre == "attn0":
                        act.wait_ge(z_ready, i + 1)
                        nc.scalar.activation(z[:, :, :], z[:, :, :], ACT.Exp).then_inc(exps_done, 1)
                    act.wait_ge(stats_ready, i + 1)
                    nc.scalar.activation(std[:, :, :], mv[:, :, 1:2], ACT.Sqrt, bias=K.eps[:, 0:1]).then_inc(std_ready, 1)

                    def take(j):
                        if gat_weights:
                            freed(act, pO_ready, i * BODY + j + 1)
                            if j == 0:
                                freed(act, og_free, i)
                            if tag != "a0":
                                nc.scalar.activation(K.AD[:, bass.ds(t0 + j, 1), :].rearrange("p o d -> p (o d)"),
                                                     pO[j % 2][:, DIM:DIM + 8], ACT.Copy)
                            nc.scalar.activation(og[:, j, :], pO[j % 2][:, 0:NC], ACT.Copy).then_inc(o_ready, 1)

                    def hidden(j):
                        act.wait_ge(pR_ready, i * BODY + j + 1)
                        nc.scalar.activation(rhT[:, j, :], pR[j % 2][:, 0:P], ACT.Relu, bias=rb1[:, 0:1]).then_inc(rh_ready, 1)

                    freed(act, pO_ready, i * BODY)
                    for j in range(BODY):
                        freed(act, pT_ready, i * BODY + j + 1)
                        nc.scalar.activation(yT[:, j, :, :].rearrange("p k m -> p (k m)"), pT[j % 2][:, 0:KC * P],
                                             ACT.Copy).then_inc(yT_ready, 1)
                        if not gat_weights:
                            nc.scalar.activation(Y[:, bass.ds(t0 + j, 1), 0:DIM].rearrange("p o d -> p (o d)"), yg[:, j, :],
                                                 ACT.Copy).then_inc(y_kept, 1)
                        if router:
                            if j:
                                hidden(j - 1)
                        elif j:
                            take(j - 1)
                    if router:
                        hidden(BODY - 1)
                        act.wait_ge(exp_in, i + 1)
                        nc.scalar.activation(p[:, :, :], p[:, :, :], ACT.Exp).then_inc(exp_out, 1)
                    else:
                        take(BODY - 1)
                if routed:
                    act.wait_ge(exp_in, TRIPS + 1 if router else 1)
                    nc.scalar.activation(K.WT[:, :, 1:2], K.WT[:, :, 1:2], ACT.Exp).then_inc(exp_out, 1)

            @block.tensor
            def _(pe):
                with pe.Fori(0, TRIPS) as i:
                    def transpose(j):
                        pe.wait_ge(y_ready, i * BODY + j + 1)
                        freed(pe, yT_ready, i * BODY + max(0, j - 1))
                        for k in range(KC):
                            last = nc.tensor.transpose(pT[j % 2][:, k * P:(k + 1) * P], yg[:, j, k * P:(k + 1) * P], K.ident[:, :])
                        last.then_inc(pT_ready, 1)

                    def multiply(j):
                        freed(pe, yT_ready, i * BODY + j + 1)
                        if router:
                            freed(pe, rh_ready, i * BODY + max(0, j - 1))
                            for k in range(KC):
                                last = nc.tensor.matmul(pR[j % 2][:, 0:P], w[:, k, :], yT[:, j, k, :], start=(k == 0), stop=(k == KC - 1))
                            last.then_inc(pR_ready, 1)
                        else:
                            freed(pe, o_ready, i * BODY + max(0, j - 1))
                            for k in range(KC):
                                last = nc.tensor.matmul(pO[j % 2][:, 0:NC], yT[:, j, k, :], w[:, k, :], start=(k == 0), stop=(k == KC - 1))
                            last.then_inc(pO_ready, 1)

                    def second(j):
                        freed(pe, rh_ready, i * BODY + j + 1)
                        freed(pe, o_ready, i * BODY + max(0, j - 1))
                        nc.tensor.matmul(pO[j % 2][:, 0:NC], rhT[:, j, :], w2[:, :], start=True, stop=True).then_inc(pO_ready, 1)

                    if gat_weights:
                        pe.wait_ge(w_ready, 2 * KC)
                    else:
                        pe.wait_ge(w_in, 16 * n_w)
                    for j in range(BODY + 2):
                        if j < BODY:
                            transpose(j)
                        if 1 <= j <= BODY:
                            multiply(j - 1)
                        if router and j >= 2:
                            second(j - 2)
                    if routed:
                        pe.wait_ge(masks, i + 1)
                        nc.tensor.matmul(pr[:, 0:BODY * E], K.tri[:, :], Mb[:, :, :].rearrange("p t e -> p (t e)"), start=True, stop=False)
                        for j in range(BODY - 1):
                            n = BODY - 1 - j
                            nc.tensor.matmul(pr[:, (j + 1) * E:BODY * E].rearrange("p (t e) -> p t e", e=E), K.ones[:, :],
                                             Mb[:, j:j + 1, :].to_broadcast([P, n, E]), start=False, stop=False)
                        nc.tensor.matmul(pr[:, 0:BODY * E].rearrange("p (t e) -> p t e", e=E), K.ones[:, :],
                                         before[:, :].rearrange("p (o e) -> p o e", o=1).to_broadcast([P, BODY, E]),
                                         start=False, stop=True).then_inc(ranks, 1)
                if routed:
                    pe.wait_ge(count_in, 1)
                    nc.tensor.matmul(pr[:, 0:E], K.ones[:, :], before[:, :], start=True, stop=True).then_inc(ranks, 1)


def experts(K, tag, E, wa, ba, H, func, wm, bm, wl, bl):
    nc = K.nc
    HC = H // P
    units = HC + (H // P if wm is not None else 0)
    with ExitStack() as stack:
        sb, pb, sem = K.tools(stack, tag)
        WA = [sb(f"WA{b}", [P, KC, H]) for b in range(2)]
        WL = [sb(f"WL{b}", [P, HC, DIM]) for b in range(2)]
        WM = [sb(f"WM{b}", [P, HC, H]) for b in range(2)] if wm is not None else None
        BA = sb("BA", [P, E * HC])
        BM = sb("BM", [P, E * HC]) if wm is not None else None
        BL = sb("BL", [P, E, DIM])
        pad = sb("pad", [P, E + 1, SUB, WIDE])
        xs = [sb(f"xs{b}", [P, SUB, WIDE]) for b in range(2)]
        to_f = [sb(f"to_f{b}", [P, SUB]) for b in range(2)]
        to = [sb(f"to{b}", [P, SUB], I32) for b in range(2)]
        xT = [sb(f"xT{b}", [P, KC, MT]) for b in range(2)]
        hT = [sb(f"hT{b}", [P, HC, MT]) for b in range(2)]
        mT = [sb(f"mT{b}", [P, HC, MT]) for b in range(2)] if wm is not None else None
        ob = [sb(f"ob{b}", [P, SUB, DIM]) for b in range(2)]
        pX = [pb(f"pX{b}", [P, KC, MT]) for b in range(2)]
        pH = [pb(f"pH{n}", [P, 512]) for n in range(4)]
        pO = [pb(f"pO{n}", [P, 512]) for n in range(2)]

        pad_made = sem("pad_made")
        padded = sem("padded")
        biases_in = sem("biases_in")
        wa_in = [sem(f"wa_in{b}") for b in range(2)]
        wm_in = [sem(f"wm_in{b}") for b in range(2)]
        wl_in = [sem(f"wl_in{b}") for b in range(2)]
        x_in = [sem(f"x_in{b}") for b in range(2)]
        pX_ready = [sem(f"pX_ready{b}") for b in range(2)]
        xT_ready = sem("xT_ready")
        pH_ready = sem("pH_ready")
        h_ready = sem("h_ready")
        tile_done = [sem(f"tile_done{b}") for b in range(2)]
        half_ready = sem("half_ready")
        o_ready = sem("o_ready")
        sent = [sem(f"sent{b}", indirect=True) for b in range(2)]
        passed = sem("passed")
        ob_free = [sem(f"ob_free{b}") for b in range(2)]
        lifts = (xT_ready, pH_ready, h_ready, o_ready, *pX_ready, *tile_done, *ob_free)
        n_b = 3 if wm is not None else 2

        def field(eng, j, c, top):
            at = slice(j, j + 1) if isinstance(j, int) else bass.ds(j, 1)
            return eng.value_load(K.TE[0:1, at, c:c + 1].rearrange("o a b -> o (a b)"), min_val=0, max_val=top)

        def last_pair(eng):
            return eng.value_load(K.LAST[0:1, 0:1], min_val=0, max_val=(NT - 1) // 2 - 1)

        with nc.Block() as block:
            @block.gpsimd
            def _(gp):
                lift(gp, lifts)
                nc.gpsimd.iota(pad[:, :, :, DIM].rearrange("p e s -> p (e s)"), pattern=[[P, (E + 1) * SUB]], base=YDUMP,
                               channel_multiplier=1, allow_small_or_imprecise_dtypes=True).then_inc(pad_made, 1)
                with gp.Fori(0, gp.snap(last_pair(gp) + 1)) as i:
                    for b in range(2):
                        freed(gp, o_ready, (i * 2 + b + 1) * SUB)
                        gp.sem_inc(passed, 1)
                        for s in range(SUB):
                            gp.indirect_dma_start(K.YS, bass.IndirectOffsetOnAxis(ap=to[b][:, s:s + 1], axis=0),
                                                  ob[b][:, s, :], None).then_inc(sent[b], 16)
                        if b == 1:
                            gp.wait_ge(sent[0], i * (16 * SUB) + 16 * SUB)
                            gp.sem_inc(ob_free[0], 1)
                            gp.wait_ge(sent[1], i * (16 * SUB) + 16 * SUB)
                            gp.sem_inc(ob_free[1], 1)

            @block.sync
            def _(sp):
                sp.dma_start(BA[:, :], ba.rearrange("e (c p) -> p (e c)", p=P), allow_slow_non_contiguous=True).then_inc(biases_in, 16)
                sp.dma_start(BL[:, :, :].rearrange("p e d -> p (e d)"), bl.rearrange("e d -> (e d)").partition_broadcast(P)).then_inc(biases_in, 16)
                if wm is not None:
                    sp.dma_start(BM[:, :], bm.rearrange("e (c p) -> p (e c)", p=P), allow_slow_non_contiguous=True).then_inc(biases_in, 16)
                wa_r = wa.rearrange("e k h -> (e k) h")
                wl_r = wl.rearrange("e h d -> (e h) d")
                wm_r = wm.rearrange("e h d -> (e h) d") if wm is not None else None

                def load(b, to, in_sem, src, row, rows):
                    sp.dma_start(to[b][:, :, :], src[bass.ds(row, rows), :].rearrange("(k p) h -> p k h", p=P)).then_inc(in_sem[b], 16)

                def rows(i, b):
                    r0 = field(sp, i * 2 + b, 1, BLANK)
                    if not isinstance(i, int) or i > 0:
                        freed(sp, pX_ready[b], i)
                        freed(sp, xT_ready, i * 2 + b - 1)
                    sp.dma_start(xs[b][:, :, :], K.XS[bass.ds(r0, MT), :].rearrange("(s p) d -> p s d", p=P)).then_inc(x_in[b], 16)

                def weights(i, b, ahead):
                    e = field(sp, i * 2 + b, 0, E - 1)
                    ra = sp.snap(e * DIM)
                    rl = sp.snap(e * H)
                    if isinstance(i, int):
                        load(b, WA, wa_in, wa_r, ra, DIM)
                        ahead()
                        if wm is not None:
                            load(b, WM, wm_in, wm_r, rl, H)
                        load(b, WL, wl_in, wl_r, rl, H)
                        return
                    before = sp.snap((i * 2 + b - 2) * units)
                    other = field(sp, i * 2 + b, 2, 1)
                    with sp.If(other > 0):
                        freed(sp, pH_ready, before + HC)
                        load(b, WA, wa_in, wa_r, ra, DIM)
                    ahead()
                    with sp.If(other > 0):
                        if wm is not None:
                            freed(sp, pH_ready, before + units)
                            load(b, WM, wm_in, wm_r, rl, H)
                        freed(sp, tile_done[b], i)
                        load(b, WL, wl_in, wl_r, rl, H)

                sp.wait_ge(pad_made, 2)
                for e in range(E):
                    r0 = sp.value_load(K.PADS[0:1, e:e + 1], min_val=0, max_val=BLANK - MT)
                    sp.dma_start(K.XS[bass.ds(r0, MT), :].rearrange("(s p) d -> p s d", p=P), pad[:, e, :, :]).then_inc(padded, 16)
                sp.dma_start(K.XS[E * CAP:E * CAP + MT, :].rearrange("(s p) d -> p s d", p=P), pad[:, E, :, :]).then_inc(padded, 16)
                sp.wait_ge(padded, 16 * (E + 1))
                last = last_pair(sp)
                rows(0, 0)
                weights(0, 0, lambda: rows(0, 1))
                weights(0, 1, lambda: rows(1, 0))

                def next_pair(i):
                    with sp.If(i < last):
                        rows(i + 1, 0)

                with sp.Fori(1, sp.snap(last + 1)) as i:
                    weights(i, 0, lambda: rows(i, 1))
                    weights(i, 1, lambda: next_pair(i))

            @block.tensor
            def _(pe):
                def transpose(i, b):
                    pe.wait_ge(x_in[b], i * 16 + 16)
                    if not isinstance(i, int):
                        freed(pe, xT_ready, i * 2 + b - 1)
                    for s in range(SUB):
                        for k in range(KC):
                            last = nc.tensor.transpose(pX[b][:, k, s * P:(s + 1) * P], xs[b][:, s, k * P:(k + 1) * P], K.ident[:, :])
                    last.then_inc(pX_ready[b], 1)

                def hidden(i, b, W, src, nk, u0):
                    for u in range(HC):
                        if u0 + u - 3 > HC or not u0:
                            freed(pe, h_ready, (i * 2 + b) * units + max(0, u0 + u - 3))
                        for k in range(nk):
                            last = nc.tensor.matmul(pH[(u0 + u) % 4][:, 0:MT], W[b][:, k, u * P:(u + 1) * P], src[b][:, k, :],
                                                    start=(k == 0), stop=(k == nk - 1))
                        last.then_inc(pH_ready, 1)

                loads = {}

                def first(i, b):
                    loads[b] = field(pe, i * 2 + b, 3, NT // 2)
                    freed(pe, xT_ready, i * 2 + b + 1)
                    pe.wait_ge(wa_in[b], loads[b] * 16)
                    hidden(i, b, WA, xT, KC, 0)

                def middle(i, b):
                    if wm is not None:
                        pe.wait_ge(wm_in[b], loads[b] * 16)
                        freed(pe, h_ready, (i * 2 + b) * units + HC)
                        hidden(i, b, WM, hT, HC, HC)

                def final(i, b):
                    act_in = mT if wm is not None else hT
                    pe.wait_ge(wl_in[b], loads[b] * 16)
                    freed(pe, h_ready, (i * 2 + b + 1) * units)
                    for s in range(SUB):
                        freed(pe, o_ready, (i * 2 + b) * SUB)
                        for k in range(HC):
                            last = nc.tensor.matmul(pO[s][:, 0:DIM], act_in[b][:, k, s * P:(s + 1) * P], WL[b][:, k, :],
                                                    start=(k == 0), stop=(k == HC - 1))
                        last.then_inc(half_ready if s == 0 else tile_done[b], 1)

                pe.wait_ge(biases_in, 16 * n_b)
                last = last_pair(pe)
                transpose(0, 0)
                first(0, 0)
                transpose(0, 1)
                middle(0, 0)
                with pe.Fori(0, last) as i:
                    first(i, 1)
                    transpose(i + 1, 0)
                    loads[0] = field(pe, i * 2, 3, NT // 2)
                    final(i, 0)
                    middle(i, 1)
                    first(i + 1, 0)
                    transpose(i + 1, 1)
                    final(i, 1)
                    middle(i + 1, 0)
                first(last, 1)
                loads[0] = field(pe, last * 2, 3, NT // 2)
                final(last, 0)
                middle(last, 1)
                final(last, 1)

            @block.scalar
            def _(act):
                act.wait_ge(biases_in, 16 * n_b)
                with act.Fori(0, act.snap(last_pair(act) + 1)) as i:
                    for b in range(2):
                        e = field(act, i * 2 + b, 0, E - 1)
                        freed(act, tile_done[b], i)
                        for u in range(units):
                            freed(act, pH_ready, (i * 2 + b) * units + u + 1)
                            dst, bias, c = (hT, BA, u) if u < HC else (mT, BM, u - HC)
                            nc.scalar.activation(dst[b][:, c, :], pH[u % 4][:, 0:MT], func,
                                                 bias=bias[:, bass.ds(e * HC + c, 1)]).then_inc(h_ready, 1)

            @block.vector
            def _(v):
                def x_out(i, b):
                    freed(v, pX_ready[b], i + 1)
                    if not isinstance(i, int):
                        freed(v, pH_ready, (i * 2 + b - 2) * units + HC)
                        freed(v, o_ready, (i * 2 + b - 1) * SUB)
                    nc.vector.tensor_copy(to_f[b][:, :], xs[b][:, :, DIM])
                    nc.vector.tensor_copy(xT[b][:, :, :], pX[b][:, :, :]).then_inc(xT_ready, 1)

                def o_out(i, b):
                    e = field(v, i * 2 + b, 0, E - 1)
                    freed(v, ob_free[b], i)
                    freed(v, xT_ready, i * 2 + b + 1)
                    nc.vector.tensor_copy(to[b][:, :], to_f[b][:, :])
                    for s in range(SUB):
                        if s == 0:
                            v.wait_ge(half_ready, i * 2 + b + 1)
                        else:
                            freed(v, tile_done[b], i + 1)
                        nc.vector.tensor_tensor(ob[b][:, s, :], pO[s][:, 0:DIM],
                                                BL[:, bass.ds(e, 1), :].rearrange("p o d -> p (o d)"), ALU.add).then_inc(o_ready, 1)

                for e in range(E + 1):
                    last = nc.vector.memset(pad[:, e, :, 0:DIM], 0.0)
                last.then_inc(pad_made, 1)
                v.wait_ge(biases_in, 16 * n_b)
                last = last_pair(v)
                x_out(0, 0)
                x_out(0, 1)
                with v.Fori(0, last) as i:
                    o_out(i, 0)
                    x_out(i + 1, 0)
                    o_out(i, 1)
                    x_out(i + 1, 1)
                o_out(last, 0)
                o_out(last, 1)


def attention(K, bias_in):
    nc = K.nc
    J = range(len(CHUNKS))
    with ExitStack() as stack:
        sb, pb, sem = K.tools(stack, "at")
        gm = sb("gm", [P, HEADS])
        gt = sb("gt", [P, HEADS])
        adm = sb("adm", [P, TILES, 8])
        exs = sb("exs", [P, TILES, HEADS])
        pm = sem("pm")
        gm_ready = sem("gm_ready")
        gm_all = sem("gm_all")
        self_z = sem("self_z")
        with nc.Block() as block:
            @block.vector
            def _(v):
                V = nc.vector
                ch = Chain(v, pm)
                AS, ADs = K.AD[:, :, 0:4], K.AD[:, :, 4:8]
                ch.mark(V.tensor_reduce(gm[:, :].rearrange("p (h o) -> p h o", o=1),
                                        K.AD[:, 0:TILES - 1, 0:4].rearrange("p t h -> p h t"), AX.X, ALU.max))
                ch.link(V.tensor_scalar(gt[:, :], K.AD[:, TILES - 1, 0:4], K.vneg[:, 0:1], None, ALU.add))
                V.tensor_tensor(gm[:, :], gm[:, :], gt[:, :], ALU.max).then_inc(gm_ready, 1)
                v.wait_ge(gm_all, 1)
                ch.link(V.tensor_copy(adm[:, :, 0:4], ADs))
                ch.link(V.tensor_tensor(adm[:, :, 4:8], ADs, gt[:, :].rearrange("p (o h) -> p o h", o=1).to_broadcast([P, TILES, HEADS]), ALU.add))
                ch.link(V.scalar_tensor_tensor(adm[:, :, 4:8], adm[:, :, 4:8], 0.2, adm[:, :, 4:8], ALU.mult, ALU.max))
                ch.link(V.tensor_tensor(exs[:, :, :], AS, ADs, ALU.add))
                ch.link(V.scalar_tensor_tensor(exs[:, :, :], exs[:, :, :], 0.2, exs[:, :, :], ALU.mult, ALU.max))
                ch.link(V.tensor_tensor(exs[:, :, :], exs[:, :, :], adm[:, :, 4:8], ALU.subtract))
                V.tensor_scalar(exs[:, :, :], exs[:, :, :], 0.0, None, ALU.min).then_inc(self_z, 1)

            @block.gpsimd
            def _(gp):
                gp.wait_ge(gm_ready, 1)
                nc.gpsimd.partition_all_reduce(gt[:, :], gm[:, :], P, bass.bass_isa.ReduceOp.max).then_inc(gm_all, 1)

            @block.scalar
            def _(act):
                act.wait_ge(self_z, 1)
                nc.scalar.activation(exs[:, :, :], exs[:, :, :], ACT.Exp)

        idx = [sb(f"idx{j}", [P, CHUNKS[j]], I32) for j in J]
        dcol = [sb(f"dcol{j}", [P, CHUNKS[j]]) for j in J]
        drow = [sb(f"drow{j}", [P, CHUNKS[j] * P]) for j in J]
        G = [sb(f"G{j}", [P, CHUNKS[j], DIM + 4]) for j in J]
        OH = [sb(f"OH{j}", [P, CHUNKS[j], P]) for j in J]
        OT = [sb(f"OT{j}", [P, CHUNKS[j], P]) for j in J]
        Z = [sb(f"Z{j}", [P, CHUNKS[j], HEADS]) for j in J]
        own = sb("own", [P, DIM + 4])
        cur = sb("cur", [P, 8])
        TI = sb("TI", [P, P])
        TP = sb("TP", [P, 1])
        ACC = sb("ACC", [P, DIM + 4])
        bias = sb("bias", [P, DIM])
        res = sb("res", [P, DIM])
        rec = sb("rec", [P, HEADS])
        pAd = [pb(f"pAd{j}", [P, 512]) for j in J]
        pAgg = pb("pAgg", [P, 512])

        bias_ld = sem("bias_ld")
        init = sem("init")
        src_in = [sem(f"src_in{j}") for j in J]
        dst_in = [sem(f"dst_in{j}") for j in J]
        gathered = [sem(f"gathered{j}", indirect=True) for j in J]
        onehots = [sem(f"onehots{j}") for j in J]
        agg_done = [sem(f"agg_done{j}") for j in J]
        own_in = sem("own_in")
        own_used = sem("own_used")
        cur_ready = sem("cur_ready")
        ad_ready = sem("ad_ready")
        scored = [sem(f"scored{j}") for j in J]
        ex_ready = sem("ex_ready")
        msg_ready = sem("msg_ready")
        acc_done = sem("acc_done")
        chain = sem("chain")
        passed = sem("passed")
        NJ = len(CHUNKS)
        lifts = (own_used, acc_done, *scored, *onehots, *agg_done)
        START, STEP, END = 3, 3 * NJ, 5

        def tile_steps(eng, t):
            at = slice(t, t + 1) if isinstance(t, int) else bass.ds(t, 1)
            n = eng.value_load(K.ET[0:1, at, 1:2].rearrange("o a b -> o (a b)"), min_val=1, max_val=MAXSTEPS)
            s0 = eng.value_load(K.ET[0:1, at, 2:3].rearrange("o a b -> o (a b)"), min_val=0, max_val=TILES * MAXSTEPS)
            return n, s0

        with nc.Block() as block:
            @block.sync
            def _(sp):
                sp.dma_start(bias[:, :], bias_in.partition_broadcast(P)).then_inc(bias_ld, 16)
                with sp.Fori(0, TILES) as t:
                    n, s0 = tile_steps(sp, t)
                    base = sp.value_load(K.ET[0:1, bass.ds(t, 1), 0:1].rearrange("o a b -> o (a b)"), min_val=0, max_val=EDGES - GRAN)
                    r0 = sp.snap(t * P)
                    freed(sp, own_used, t)
                    sp.dma_start(own[:, :], K.T1[bass.ds(r0, P), :]).then_inc(own_in, 16)
                    with sp.Fori(0, n) as g:
                        s = sp.snap(s0 + g)
                        e0 = nc.s_assert_within(sp.snap(base + g * SE), 0, EDGES, skip_runtime_bounds_check_because=
                                                "a step begins before its tile's last edge, and SE edges of padding follow the last")
                        at = [sp.snap(e0 + OFFS[j]) for j in J]
                        for j in J:
                            ne = CHUNKS[j] * P
                            freed(sp, scored[j], s)
                            sp.dma_start(idx[j][:, :], K.SRCP[bass.ds(at[j], ne)].rearrange("(p c) -> p c", p=P)).then_inc(src_in[j], 16)
                            freed(sp, onehots[j], s)
                            sp.dma_start(dcol[j][:, :], K.DSTP[bass.ds(at[j], ne)].rearrange("(p c) -> p c", p=P)).then_inc(dst_in[j], 16)
                            sp.dma_start(drow[j][:, :], K.DSTP[bass.ds(at[j], ne)].partition_broadcast(P)).then_inc(dst_in[j], 16)

            @block.gpsimd
            def _(gp):
                lift(gp, lifts)
                n, s0 = tile_steps(gp, TILES - 1)
                with gp.Fori(0, gp.snap(s0 + n)) as s:
                    for j in J:
                        gp.wait_ge(src_in[j], s * 16 + 16)
                        freed(gp, agg_done[j], s)
                        gp.sem_inc(passed, 1)
                        for c in range(CHUNKS[j]):
                            gp.indirect_dma_start(G[j][:, c, :], None, K.T1,
                                                  bass.IndirectOffsetOnAxis(ap=idx[j][:, c:c + 1], axis=0)).then_inc(gathered[j], 16)

            @block.vector
            def _(v):
                V = nc.vector

                def one_hots(s, j):
                    c = CHUNKS[j]
                    v.wait_ge(dst_in[j], s * 32 + 32)
                    freed(v, agg_done[j], s)
                    V.tensor_tensor(OH[j][:, :, :], dcol[j][:, :].rearrange("p (c o) -> p c o", o=1).to_broadcast([P, c, P]),
                                    TI[:, :].rearrange("p (o n) -> p o n", o=1).to_broadcast([P, c, P]), ALU.is_equal)
                    V.tensor_scalar(OT[j][:, :, :], drow[j][:, :].rearrange("n (p c) -> n c p", c=c), TP[:, 0:1], None,
                                    ALU.is_equal).then_inc(onehots[j], 1)

                def scores(ch, s, j):
                    c = CHUNKS[j]
                    v.wait_ge(gathered[j], s * (16 * c) + 16 * c)
                    v.wait_ge(ad_ready, s * NJ + j + 1)
                    ad = pAd[j][:, 0:8 * c].rearrange("p (c k) -> p c k", k=8)
                    ch.link(V.tensor_tensor(Z[j][:, :, :], G[j][:, :, DIM:DIM + 4], ad[:, :, 0:4], ALU.add))
                    ch.link(V.scalar_tensor_tensor(Z[j][:, :, :], Z[j][:, :, :], 0.2, Z[j][:, :, :], ALU.mult, ALU.max))
                    ch.link(V.tensor_tensor(Z[j][:, :, :], Z[j][:, :, :], ad[:, :, 4:8], ALU.subtract))
                    V.tensor_scalar(Z[j][:, :, :], Z[j][:, :, :], 0.0, None, ALU.min).then_inc(scored[j], 1)

                def weigh(s, j):
                    c = CHUNKS[j]
                    v.wait_ge(ex_ready, s * NJ + j + 1)
                    rows = G[j][:, :, 0:DIM].rearrange("p c (h k) -> p c h k", h=HEADS)
                    ex = G[j][:, :, DIM:DIM + 4].rearrange("p c (h o) -> p c h o", o=1).to_broadcast([P, c, HEADS, CH])
                    V.tensor_tensor(rows, rows, ex, ALU.mult).then_inc(msg_ready, 1)

                def first_group(ch, s):
                    one_hots(s, 0)
                    one_hots(s, 1)
                    scores(ch, s, 0)
                    weigh(s, 0)

                def other_groups(ch, s):
                    one_hots(s, 2)
                    scores(ch, s, 1)
                    weigh(s, 1)
                    scores(ch, s, 2)
                    weigh(s, 2)

                def absorb(s):
                    freed(v, agg_done[NJ - 1], s)
                    V.tensor_tensor(ACC[:, :], ACC[:, :], pAgg[:, 0:DIM + 4], ALU.add).then_inc(acc_done, 1)
                    freed(v, acc_done, s)

                def finalize(ch, t):
                    ch.link(V.tensor_scalar(rec[:, :], ACC[:, DIM:DIM + 4], 1e-30, None, ALU.add))
                    ch.link(V.reciprocal(rec[:, :], rec[:, :]))
                    ch.link(V.tensor_tensor(res[:, :].rearrange("p (h k) -> p h k", h=HEADS),
                                            ACC[:, 0:DIM].rearrange("p (h k) -> p h k", h=HEADS),
                                            rec[:, :].rearrange("p (h o) -> p h o", o=1).to_broadcast([P, HEADS, CH]), ALU.mult))
                    ch.link(V.tensor_tensor(res[:, :], res[:, :], bias[:, :], ALU.add))
                    Xt = K.X[:, bass.ds(t, 1), :].rearrange("p o d -> p (o d)")
                    ch.mark(V.scalar_tensor_tensor(Xt, res[:, :], 0.0, Xt, ALU.max, ALU.add))

                def tile(t, before):
                    n, s0 = tile_steps(v, t)
                    ch = Chain(v, chain, t * START + before * END + s0 * STEP)
                    ch.mark(V.tensor_scalar(TI[:, :], TI[:, :], float(P), None, ALU.add))
                    ch.mark(V.tensor_scalar(TP[:, :], TP[:, :], float(P), None, ALU.add))
                    V.tensor_copy(cur[:, :], adm[:, bass.ds(t, 1), :].rearrange("p o k -> p (o k)")).then_inc(cur_ready, 1)
                    ch.settle()
                    first_group(ch, s0)
                    if not isinstance(t, int):
                        absorb(s0)
                        finalize(ch, t - 1)
                    ex_t = exs[:, bass.ds(t, 1), :].rearrange("p o h -> p (o h)")
                    v.wait_ge(own_in, t * 16 + 16)
                    V.tensor_tensor(ACC[:, 0:DIM].rearrange("p (h k) -> p h k", h=HEADS),
                                    own[:, 0:DIM].rearrange("p (h k) -> p h k", h=HEADS),
                                    ex_t.rearrange("p (h o) -> p h o", o=1).to_broadcast([P, HEADS, CH]), ALU.mult).then_inc(own_used, 1)
                    ch.link(V.tensor_copy(ACC[:, DIM:DIM + 4], ex_t))
                    freed(v, own_used, t + 1)
                    other_groups(ch, s0)
                    assert ch.n == START + STEP + (0 if isinstance(t, int) else END)
                    with v.If(n > 1):
                        with v.Fori(1, n) as g:
                            s = v.snap(s0 + g)
                            cs = Chain(v, chain, (t + 1) * START + t * END + s * STEP)
                            first_group(cs, s)
                            absorb(s)
                            other_groups(cs, s)
                            assert cs.n == STEP

                V.tensor_scalar(TI[:, :], K.iota[:, 0:P], -float(P), None, ALU.add).then_inc(init, 1)
                V.tensor_scalar(TP[:, :], K.pid[:, :], -float(P), None, ALU.add).then_inc(init, 1)
                v.wait_ge(init, 2)
                v.wait_ge(bias_ld, 16)
                tile(0, 0)
                with v.Fori(1, TILES) as t:
                    tile(t, t - 1)
                n, s0 = tile_steps(v, TILES - 1)
                s = v.snap(s0 + n)
                absorb(s)
                ch = Chain(v, chain, TILES * START + (TILES - 1) * END + s * STEP)
                finalize(ch, TILES - 1)

            @block.scalar
            def _(act):
                n, s0 = tile_steps(act, TILES - 1)
                with act.Fori(0, act.snap(s0 + n)) as s:
                    for j in J:
                        freed(act, scored[j], s + 1)
                        nc.scalar.activation(G[j][:, :, DIM:DIM + 4], Z[j][:, :, :], ACT.Exp).then_inc(ex_ready, 1)

            @block.tensor
            def _(pe):
                def destinations(s, j):
                    freed(pe, onehots[j], s + 1)
                    freed(pe, scored[j], s)
                    for c in range(CHUNKS[j]):
                        last = nc.tensor.matmul(pAd[j][:, 8 * c:8 * c + 8], OT[j][:, c, :], cur[:, :], start=True, stop=True)
                    last.then_inc(ad_ready, 1)

                def aggregate(s, j):
                    pe.wait_ge(msg_ready, s * NJ + j + 1)
                    for c in range(CHUNKS[j]):
                        last = nc.tensor.matmul(pAgg[:, 0:DIM + 4], OH[j][:, c, :], G[j][:, c, :],
                                                start=(j == 0 and c == 0), stop=(j == NJ - 1 and c == CHUNKS[j] - 1))
                    last.then_inc(agg_done[j], 1)

                with pe.Fori(0, TILES) as t:
                    n, s0 = tile_steps(pe, t)
                    pe.wait_ge(cur_ready, t + 1)
                    pe.sem_inc(passed, 1)
                    with pe.Fori(0, n) as g:
                        s = pe.snap(s0 + g)
                        destinations(s, 0)
                        destinations(s, 1)
                        freed(pe, acc_done, s)
                        aggregate(s, 0)
                        destinations(s, 2)
                        aggregate(s, 1)
                        aggregate(s, 2)


def finish(K, out):
    nc = K.nc
    with ExitStack() as stack:
        sb, pb, sem = K.tools(stack, "f")
        rows = [sb(f"rows{k}", [P, BODY, DIM]) for k in range(4)]
        rows_in = [sem(f"rows_in{b}") for b in range(2)]
        half = sem("half")
        done = sem("done")
        stored = sem("stored")
        with nc.Block() as block:
            @block.scalar
            def _(act):
                for i in range(TRIPS):
                    b = i % 2
                    if i >= 2:
                        act.wait_ge(done, (i - 1) * BODY)
                    for k in range(2):
                        a = k * NODEROWS + i * BODY * P
                        act.dma_start(rows[2 * b + k][:, :, :],
                                      K.YS[a:a + BODY * P, :].rearrange("(t p) d -> p t d", p=P)).then_inc(rows_in[b], 16)

            @block.vector
            def _(v):
                for i in range(TRIPS):
                    b = i % 2
                    v.wait_ge(rows_in[b], 32 * (i // 2 + 1))
                    for k in range(2):
                        if k:
                            v.wait_ge(half, (i + 1) * BODY)
                        for j in range(BODY):
                            t = i * BODY + j
                            nc.vector.scalar_tensor_tensor(K.X[:, t, :], rows[2 * b + k][:, j, :], K.WT[:, t, k:k + 1], K.X[:, t, :],
                                                           ALU.mult, ALU.add).then_inc(done if k else half, 1)

            @block.sync
            def _(sp):
                for i in range(TRIPS):
                    a, b = i * BODY, min((i + 1) * BODY, TILES - 1)
                    sp.wait_ge(done, (i + 1) * BODY)
                    sp.dma_start(out[a * P:b * P, :].rearrange("(t p) d -> p t d", p=P), K.X[:, a:b, :]).then_inc(stored, 16)
                sp.dma_start(out[(TILES - 1) * P:NODES, :], K.X[0:TAIL, TILES - 1, :]).then_inc(stored, 16)
                sp.wait_ge(stored, 16 * (TRIPS + 1))


_INS = ['x', 'src', 'dst', 'L0_gnn_weight', 'L0_gnn_attn_l', 'L0_gnn_attn_r', 'L0_ffn_router_w1', 'L0_ffn_router_b1',
        'L0_ffn_router_w2', 'L0_ffn_router_b2', 'L0_ffn_expert_w1', 'L0_ffn_expert_b1', 'L0_ffn_expert_w2',
        'L0_ffn_expert_b2', 'L0_ffn_expert_w3', 'L0_ffn_expert_b3', 'L1_gnn_W', 'L1_gnn_att_src', 'L1_gnn_att_dst',
        'L1_gnn_bias', 'L1_ffn_Wg', 'L1_ffn_bg', 'L1_ffn_W1', 'L1_ffn_b1', 'L1_ffn_W2', 'L1_ffn_b2']


def kernel(**inputs):
    import numpy as _np
    import concourse.bacc as _bacc
    from concourse import mybir as _mybir
    from concourse.bass_utils import run_bass_kernel_spmd as _run

    nc = _bacc.Bacc("TRN2", target_bir_lowering=False, num_devices=1)
    arrays, args = {}, {}
    for name in _INS:
        a = _np.ascontiguousarray(inputs[name])
        arrays[f"in_{name}_dram"] = a
        args[name] = nc.dram_tensor(f"in_{name}_dram", a.shape, _mybir.dt.from_np(a.dtype), kind="ExternalInput").ap()
    out = nc.dram_tensor("out_dram", (NODES, DIM), _mybir.dt.float32, kind="ExternalOutput").ap()
    gnn_moe(nc, out, **args)
    r = _run(nc, [arrays], core_ids=[0])
    return r.results[0]["out_dram"]
```

```python
import concourse.bass as bass
from concourse import mybir
from contextlib import ExitStack

F32 = mybir.dt.float32
I32 = mybir.dt.int32
F32R = mybir.dt.float32r
BF16 = mybir.dt.bfloat16
ALU = mybir.AluOpType
ACT = mybir.ActivationFunctionType
AX = mybir.AxisListType

P = 128
NODES, DIM = 6250, 256
EDGES = 100000
HEADS, CH = 4, 64
TILES = -(-NODES // P)
TAIL = NODES - (TILES - 1) * P
BODY = 7
TRIPS = TILES // BODY
assert TRIPS * BODY == TILES
KC = DIM // P
EPS = 1e-5

MT = 256
SUB = MT // P
E0, H0, R0 = 6, 256, 128
E1, H1 = 8, 1024
WIDE = DIM + 1
NODEROWS = TILES * P
MAXT = -(-NODES // MT)
CAP = (MAXT + 1) * MT
NT = (2 * NODES) // MT + E1 + 2
BLANK = max(E0, E1) * CAP
DUMP = BLANK + MT
YDUMP = 2 * NODEROWS

CHUNKS = (6, 6, 5)
OFFS = (0, 6 * P, 12 * P)
SE = sum(CHUNKS) * P
GRAN = 32
NGRAN = EDGES // GRAN
EROWS = 125
ECOLS = EDGES // EROWS
GPR = ECOLS // GRAN
SEG = SE // GRAN
MAXSTEPS = -(-NGRAN // SEG)
HUGE = 1.0e30


class Shared:
    pass


def lift(eng, sems):
    for s in sems:
        eng.sem_inc(s, 1)


def freed(eng, sem, n):
    eng.wait_ge(sem, n + 1)


class Chain:

    def __init__(self, eng, sem, base=0):
        self.eng, self.sem, self.base, self.n = eng, sem, base, 0

    def mark(self, ins):
        self.n += 1
        ins.then_inc(self.sem, 1)

    def settle(self):
        self.eng.wait_ge(self.sem, self.base + self.n)

    def link(self, ins):
        self.mark(ins)
        self.settle()


def gnn_moe(nc, out, x, src, dst, L0_gnn_weight, L0_gnn_attn_l, L0_gnn_attn_r, L0_ffn_router_w1, L0_ffn_router_b1, L0_ffn_router_w2, L0_ffn_router_b2, L0_ffn_expert_w1, L0_ffn_expert_b1, L0_ffn_expert_w2, L0_ffn_expert_b2, L0_ffn_expert_w3, L0_ffn_expert_b3, L1_gnn_W, L1_gnn_att_src, L1_gnn_att_dst, L1_gnn_bias, L1_ffn_Wg, L1_ffn_bg, L1_ffn_W1, L1_ffn_b1, L1_ffn_W2, L1_ffn_b2):
    with ExitStack() as whole:
        K = Shared()
        K.nc = nc

        def tools(stack, tag):
            def sb(name, shape, dt=F32):
                return stack.enter_context(nc.sbuf_tensor(f"{tag}_{name}", shape, dt))

            def pb(name, shape, dt=F32):
                return stack.enter_context(nc.psum_tensor(f"{tag}_{name}", shape, dt))

            used = []
            bank = K.banks[K.phase % 2]
            K.phase += 1
            K.last_used, K.used = K.used, used

            def sem(name, software=False):
                if software:
                    return whole.enter_context(nc.semaphore(f"{tag}_{name}"))
                if len(used) == len(bank):
                    bank.append(whole.enter_context(nc.semaphore(f"phase{(K.phase - 1) % 2}_{len(bank)}")))
                used.append(bank[len(used)])
                return used[-1]

            return sb, pb, sem

        def clear_last(eng):
            for s in K.last_used:
                eng.sem_clear(s)

        K.banks, K.phase, K.used = ([], []), 0, []
        K.clear_last = clear_last
        K.tools = tools
        sb, pb, sem = tools(whole, "g")

        def dram(name, shape, dt=F32):
            return nc.dram_tensor(name, shape, dt, kind="Internal").ap()

        K.T0 = dram("xt_ar", [TILES * P, DIM + 4])
        K.AL = dram("al", [TILES * P, 4])
        K.T1 = dram("h_as", [TILES * P, DIM + 4])
        K.XS = dram("slot_rows", [DUMP + 2 * P, WIDE])
        K.YS = dram("expert_out", [YDUMP + (max(E0, E1) + 1) * MT, DIM])
        K.SRCP = dram("src_padded", [EDGES + SE], I32)
        K.DSTP = dram("dst_padded", [EDGES + SE])
        K.GR = dram("granule_range", [2, NGRAN])
        K.RT = dram("tile_range", [TILES, 2])

        K.X = sb("x", [P, TILES, DIM])
        K.ident = sb("ident", [P, P])
        K.iota = sb("iota", [P, 512])
        K.pid = sb("pid", [P, 1])
        K.valid = sb("valid", [P, 1])
        K.valids = sb("valids", [P, TILES, 1])
        K.dump = sb("dump", [P, TILES, 2])
        K.vneg = sb("vneg", [P, 1])
        K.eps = sb("eps", [P, 1])
        K.tri = sb("tri", [P, P], BF16)
        K.ones = sb("ones", [P, P], BF16)
        K.onesf = sb("onesf", [P, max(TILES, NT)])
        K.POS = sb("slot_of", [P, TILES, 2], I32)
        K.WT = sb("weight_of", [P, TILES, 2])
        K.TE = sb("slot_tiles", [P, NT, 6], I32)
        K.PADS = sb("pads", [P, E1], I32)
        K.LAST = sb("last_pair", [P, 1], I32)
        K.ET = sb("edge_steps", [1, TILES, 3], I32)
        K.AD = sb("as_ad", [P, TILES, 8])

        K.dstI = sb("dst_first", [P, TILES], I32)
        K.srcI = sb("src_first", [P, TILES], I32)

        setup(K, src, dst)
        project(K, "a0", "load", x=x, gat_weights=(L0_gnn_weight, L0_gnn_attn_r, L0_gnn_attn_l))
        project(K, "a1", "attn0", router=(L0_ffn_router_w1, L0_ffn_router_b1, L0_ffn_router_w2, L0_ffn_router_b2))
        experts(K, "e0", E0, L0_ffn_expert_w1, L0_ffn_expert_b1, H0, ACT.Relu,
                L0_ffn_expert_w2, L0_ffn_expert_b2, L0_ffn_expert_w3, L0_ffn_expert_b3)
        project(K, "b0", "combine", gat_weights=(L1_gnn_W, L1_gnn_att_src, L1_gnn_att_dst))
        attention(K, L1_gnn_bias)
        project(K, "b1", None, gate=(L1_ffn_Wg, L1_ffn_bg))
        experts(K, "e1", E1, L1_ffn_W1, L1_ffn_b1, H1, ACT.Gelu, None, None, L1_ffn_W2, L1_ffn_b2)
        finish(K, out)


def setup(K, src, dst):
    nc = K.nc
    with ExitStack() as stack:
        sb, pb, sem = K.tools(stack, "s")
        zero = sb("zero", [P, DIM])
        vdump = sb("vdump", [P, 2])
        dload = sb("dload", [EROWS, ECOLS], I32)
        dflt = sb("dflt", [EROWS, ECOLS])
        rng = sb("rng", [EROWS, 2, GPR])
        padf = sb("padf", [P, SE // P])
        padi = sb("padi", [P, SE // P], I32)
        made = sem("made")
        loaded = sem("loaded")
        dst_in = sem("dst_in")
        ready = sem("ready")
        stored = sem("stored")
        with nc.Block() as block:
            @block.gpsimd
            def _(gp):
                for n, (t, pat) in enumerate(((K.iota, [[1, 512]]), (K.pid, [[1, 1]]))):
                    nc.gpsimd.iota(t[:, :], pattern=pat, base=0, channel_multiplier=n,
                                   allow_small_or_imprecise_dtypes=True).then_inc(made, 1)
                nc.gpsimd.memset(K.ident[:, :], 0.0).then_inc(made, 1)
                nc.gpsimd.memset(K.ones[:, :], 1.0).then_inc(made, 1)
                gp.wait_ge(made, 4)
                nc.gpsimd.affine_select(out=K.ident[:, :], in_=K.ident[:, :], compare_op=ALU.not_equal, fill=1.0,
                                        base=0, pattern=[[-1, P]], channel_multiplier=1).then_inc(made, 1)
                nc.gpsimd.affine_select(out=K.tri[:, :], in_=K.ones[:, :], compare_op=ALU.is_gt, fill=0.0,
                                        base=0, pattern=[[1, P]], channel_multiplier=-1).then_inc(made, 1)

            @block.vector
            def _(v):
                ch = Chain(v, ready)
                ch.mark(nc.vector.memset(K.X[:, TILES - 1, :], 0.0))
                ch.mark(nc.vector.memset(zero[:, :], 0.0))
                ch.mark(nc.vector.memset(padf[:, :], -1.0))
                ch.mark(nc.vector.memset(padi[:, :], 0))
                ch.mark(nc.vector.memset(K.dstI[:, TILES - 1:TILES], 0))
                ch.mark(nc.vector.memset(K.srcI[:, TILES - 1:TILES], 0))
                ch.mark(nc.vector.memset(K.eps[:, :], EPS))
                ch.mark(nc.vector.memset(K.onesf[:, :], 1.0))
                ch.mark(nc.vector.memset(K.valids[:, :, :], 1.0))
                ch.mark(nc.vector.memset(K.dump[:, :, :], 0.0))
                v.wait_ge(made, 6)
                ch.link(nc.vector.tensor_scalar(K.valid[:, :], K.pid[:, :], float(TAIL), None, ALU.is_lt))
                ch.link(nc.vector.tensor_scalar(K.vneg[:, :], K.valid[:, :], -1.0, HUGE, ALU.add, ALU.mult))
                for k in range(2):
                    ch.link(nc.vector.tensor_scalar(vdump[:, k:k + 1], K.valid[:, :], -1.0, -1.0, ALU.add, ALU.mult))
                    ch.link(nc.vector.scalar_tensor_tensor(K.dump[:, TILES - 1, k:k + 1], K.pid[:, :], float(DUMP + k * P),
                                                           vdump[:, k:k + 1], ALU.add, ALU.mult))
                ch.link(nc.vector.tensor_copy(K.valids[:, TILES - 1, :], K.valid[:, :]))
                v.wait_ge(dst_in, 16)
                ch.link(nc.vector.tensor_copy(dflt[:, :], dload[:, :]))
                gv = dflt[:, :].rearrange("p (g e) -> p g e", e=GRAN)
                ch.mark(nc.vector.tensor_reduce(rng[:, 0, :], gv, AX.X, ALU.min))
                ch.mark(nc.vector.tensor_reduce(rng[:, 1, :], gv, AX.X, ALU.max))
                assert ch.n == 20

            @block.sync
            def _(sp):
                sp.dma_start(dload[:, :], dst.rearrange("(p e) -> p e", p=EROWS)).then_inc(dst_in, 16)
                full = (TILES - 1) * P
                sp.wait_ge(ready, 6)
                for t, s in ((K.dstI, dst), (K.srcI, src)):
                    sp.dma_start(t[:, 0:TILES - 1], s[0:full].rearrange("(t p) -> p t", p=P),
                                 allow_slow_non_contiguous=True).then_inc(loaded, 16)
                    sp.dma_start(t[0:TAIL, TILES - 1:TILES], s[full:NODES].rearrange("(p o) -> p o", o=1)).then_inc(loaded, 16)
                sp.wait_ge(loaded, 16 * 4)
                K.clear_last(sp)

            @block.scalar
            def _(act):
                act.dma_start(K.SRCP[0:EDGES].rearrange("(p e) -> p e", p=EROWS),
                              src.rearrange("(p e) -> p e", p=EROWS)).then_inc(stored, 16)
                act.wait_ge(ready, 6)
                act.dma_start(K.SRCP[EDGES:EDGES + SE].rearrange("(p e) -> p e", p=P), padi[:, :]).then_inc(stored, 16)
                act.dma_start(K.DSTP[EDGES:EDGES + SE].rearrange("(p e) -> p e", p=P), padf[:, :]).then_inc(stored, 16)
                for k in range(2):
                    a = k * NODEROWS + NODES
                    act.dma_start(K.YS[a:(k + 1) * NODEROWS, :], zero[0:NODEROWS - NODES, :]).then_inc(stored, 16)
                act.wait_ge(ready, 18)
                act.dma_start(K.DSTP[0:EDGES].rearrange("(p e) -> p e", p=EROWS), dflt[:, :]).then_inc(stored, 16)
                act.wait_ge(ready, 20)
                for k in range(2):
                    act.dma_start(K.GR[k, :].rearrange("(p g) -> p g", p=EROWS), rng[:, k, :]).then_inc(stored, 16)
                act.wait_ge(stored, 16 * 8)


class EdgeRanges:

    def __init__(self, K, sb, sem):
        self.K = K
        self.lo = sb("lo", [TILES, NGRAN])
        self.hi = sb("hi", [TILES, NGRAN])
        self.idx = sb("idx", [TILES, NGRAN])
        self.first = sb("first", [TILES, 1])
        self.last = sb("last", [TILES, 1])
        self.span = sb("span", [TILES, 2])
        self.cnt = sb("cnt", [TILES, 1])
        self.cmp = sb("cmp", [TILES, MAXSTEPS])
        self.row = sb("row", [1, TILES, 2])
        self.inc = sb("inc", [1, TILES])
        self.ranges_in = sem("ranges_in", software=True)
        self.index_made = sem("index_made")
        self.step = sem("step")
        self.span_out = sem("span_out", software=True)
        self.row_in = sem("row_in", software=True)

    def load(self, gp):
        K = self.K
        gp.dma_start(self.lo[:, :], K.GR[0:1, :].rearrange("o g -> (o g)").partition_broadcast(TILES)).then_inc(self.ranges_in, 16)
        gp.dma_start(self.hi[:, :], K.GR[1:2, :].rearrange("o g -> (o g)").partition_broadcast(TILES)).then_inc(self.ranges_in, 16)
        K.nc.gpsimd.iota(self.idx[:, :], pattern=[[1, NGRAN]], base=0, channel_multiplier=0,
                         allow_small_or_imprecise_dtypes=True).then_inc(self.index_made, 1)

    def turn(self, gp):
        K = self.K
        gp.wait_ge(self.step, 13)
        gp.dma_start(K.RT[:, :], self.span[:, :]).then_inc(self.span_out, 16)
        gp.wait_ge(self.span_out, 16)
        gp.dma_start(self.row[0:1, :, :], K.RT.rearrange("(o t) k -> o t k", o=1)).then_inc(self.row_in, 16)
        gp.wait_ge(self.row_in, 16)

    def spans(self, v):
        nc, K = self.K.nc, self.K
        lo, hi, idx, first, last, span, cnt, cmp = self.lo, self.hi, self.idx, self.first, self.last, self.span, self.cnt, self.cmp
        ch = Chain(v, self.step)
        v.wait_ge(self.ranges_in, 32)
        v.wait_ge(self.index_made, 1)
        ch.link(nc.vector.tensor_scalar(first[:, :], K.pid[0:TILES, :], float(P), None, ALU.mult))
        ch.link(nc.vector.tensor_scalar(last[:, :], first[:, :], float(P - 1), None, ALU.add))
        ch.link(nc.vector.tensor_scalar(hi[:, :], hi[:, :], first[:, 0:1], None, ALU.is_ge))
        ch.link(nc.vector.scalar_tensor_tensor(hi[:, :], lo[:, :], last[:, 0:1], hi[:, :], ALU.is_le, ALU.mult))
        ch.link(nc.vector.tensor_scalar(lo[:, :], hi[:, :], -2.0 * NGRAN, 2.0 * NGRAN, ALU.mult, ALU.add))
        ch.link(nc.vector.tensor_tensor(lo[:, :], lo[:, :], idx[:, :], ALU.add))
        ch.link(nc.vector.scalar_tensor_tensor(hi[:, :], idx[:, :], 1.0, hi[:, :], ALU.add, ALU.mult))
        ch.link(nc.vector.tensor_reduce(span[:, 0:1], lo[:, :], AX.X, ALU.min))
        ch.link(nc.vector.tensor_reduce(cnt[:, :], hi[:, :], AX.X, ALU.max))
        ch.link(nc.vector.tensor_scalar(span[:, 0:1], span[:, 0:1], float(NGRAN - 1), None, ALU.min))
        ch.link(nc.vector.tensor_scalar(cnt[:, :], cnt[:, :], span[:, 0:1], 1.0, ALU.subtract, ALU.max))
        ch.link(nc.vector.tensor_scalar(cmp[:, :], K.iota[0:TILES, 0:MAXSTEPS], float(SEG), cnt[:, 0:1],
                                        ALU.mult, ALU.is_lt))
        ch.link(nc.vector.tensor_reduce(span[:, 1:2], cmp[:, :], AX.X, ALU.add))
        assert ch.n == 13

    def table(self, v):
        nc, K = self.K.nc, self.K
        row, inc = self.row, self.inc
        ch = Chain(v, self.step, 13)
        v.wait_ge(self.row_in, 16)
        ch.link(nc.vector.tensor_tensor_scan(inc[0:1, :], K.onesf[0:1, 0:TILES], row[0:1, :, 1], 0.0, ALU.mult, ALU.add))
        ch.mark(nc.vector.tensor_scalar(K.ET[0:1, :, 0], row[0:1, :, 0], float(GRAN), None, ALU.mult))
        ch.mark(nc.vector.tensor_copy(K.ET[0:1, :, 1], row[0:1, :, 1]))
        ch.mark(nc.vector.tensor_tensor(K.ET[0:1, :, 2], inc[0:1, :], row[0:1, :, 1], ALU.subtract))


def project(K, tag, pre, x=None, gat_weights=None, router=None, gate=None):
    nc = K.nc
    with ExitStack() as stack:
        sb, pb, sem = K.tools(stack, tag)
        routed = not gat_weights
        if pre == "load":
            edges = EdgeRanges(K, sb, sem)
            x_in = sem("x_in", software=True)
        NC = DIM + 8 if gat_weights else (E0 if router else E1)
        stats = sb("stats", [P, BODY, 6])
        mv = sb("mv", [P, BODY, 2])
        std = sb("std", [P, BODY, 1])
        rstd = sb("rstd", [P, BODY, 1])
        yg = sb("yg", [P, BODY, DIM])
        yT = sb("yT", [P, BODY, KC, P])
        og = sb("og", [P, 2 * BODY, NC]) if gat_weights else None
        w = sb("w", [P, KC, R0 if router else NC])
        if gat_weights:
            att = sb("att", [P, 2, DIM])
            prod = sb("prod", [P, 2, DIM])
        else:
            bias = sb("bias", [P, NC])
            E = NC
            Y = sb("Y", [P, TILES, WIDE])
            token = sb("token", [P, TILES])
            pad = sb("pad", [P, 2, SUB, WIDE])
            lg = sb("lg", [P, BODY, E])
            p = sb("p", [P, BODY, E])
            c = [sb(f"c{k}", [P, BODY, E]) for k in range(2)]
            M = [sb(f"M{k}", [P, BODY, E]) for k in range(2)]
            r = sb("r", [P, BODY, 1])
            rev = sb("rev", [P, E])
            region = sb("region", [P, E])
            Mb = sb("Mb", [P, BODY, E], BF16)
            before = sb("before", [P, E], BF16)
            here = sb("here", [P, E])
            rank = sb("rank", [P, BODY, E])
            pos = sb("pos", [P, BODY, 2])
            pr = pb("pr", [P, 512])
        if router:
            w2 = sb("w2", [P, NC])
            rb1 = sb("rb1", [P, 1])
            rhT = sb("rhT", [P, BODY, P])
            pR = [pb(f"pR{n}", [P, 512]) for n in range(2)]
        if pre == "attn0":
            rows = sb("rows", [P, BODY, DIM + 4])
            left = sb("left", [P, BODY, 4])
            z = sb("z", [P, BODY, 4])
            z1 = sb("z1", [P, BODY, 1])
            mix = sb("mix", [P, BODY, DIM])
            tmp = sb("tmp", [P, BODY, CH])
        if pre == "combine":
            rows = sb("rows", [P, 2, BODY, DIM])
        pT = [pb(f"pT{n}", [P, 512]) for n in range(2)]
        pO = [pb(f"pO{n}", [P, 512]) for n in range(2)]

        w_in = sem("w_in")
        w_ready = sem("w_ready")
        gathered = [sem(f"gathered{j}", software=True) for j in range(BODY)] if pre == "attn0" else None
        rows_in = sem("rows_in")
        rows_used = sem("rows_used")
        rstd_ready = sem("rstd_ready")
        place_chain = sem("place_chain")
        chain = sem("chain")
        exps_done = sem("exps_done")
        z_ready = sem("z_ready")
        stats_ready = sem("stats_ready")
        std_ready = sem("std_ready")
        y_ready = sem("y_ready")
        y_kept = sem("y_kept")
        pT_ready = sem("pT_ready")
        yT_ready = sem("yT_ready")
        pR_ready = sem("pR_ready")
        rh_ready = sem("rh_ready")
        pO_ready = sem("pO_ready")
        o_ready = sem("o_ready")
        stored = sem("stored")
        passed = sem("passed")
        og_free = sem("og_free")
        token_made = sem("token_made")
        consts = sem("consts")
        exp_in = sem("exp_in")
        exp_out = sem("exp_out")
        masks = sem("masks")
        ranks = sem("ranks")
        slots_ready = sem("slots_ready")
        moved = sem("moved")
        sent = [sem(f"sent{k}", software=True) for k in range(2)] if routed else None
        count_in = sem("count_in")
        pad_made = sem("pad_made")
        ends_ready = sem("ends_ready")
        padded = sem("padded")
        lifts = (rows_used, o_ready, pT_ready, y_kept, pO_ready, yT_ready, rh_ready, og_free)

        if routed:
            cnt = sb("cnt", [P, E])
            kt = sb("kt", [P, MAXT])
            cmp = sb("cmp", [P, E, MAXT])
            nt = sb("nt", [P, E])
            end = sb("end", [P, E])
            skip = sb("skip", [P, E])
            tj = sb("tj", [P, NT])
            cj = sb("cj", [P, NT, E])
            te = sb("te", [P, NT, 6])
            half = sb("half", [P, 1])
            c2 = sb("c2", [P, NT])
            ended = sb("ended", [P, E])
            final = sb("final", [P, 1])

        def tables(ch):
            V = nc.vector
            v = ch.eng
            WT = K.WT
            v.sem_inc(count_in, 1)
            V.tensor_tensor(WT[:, :, 1:2], WT[:, :, 1:2], WT[:, :, 0:1], ALU.subtract).then_inc(exp_in, 1)
            ch.mark(V.tensor_scalar(kt[:, :], K.iota[:, 0:MAXT], float(MT), None, ALU.mult))
            ch.mark(V.tensor_scalar(tj[:, :], K.iota[:, 0:NT], float(MT), None, ALU.mult))
            v.wait_ge(ranks, TRIPS + 1)
            ch.link(V.tensor_copy(cnt[:, :], pr[:, 0:E]))
            V.tensor_tensor(K.PADS[:, 0:E], cnt[:, :], region[:, :], ALU.add).then_inc(ends_ready, 1)
            ch.link(V.tensor_tensor(cmp[:, :, :], cnt[:, :].rearrange("p (e o) -> p e o", o=1).to_broadcast([P, E, MAXT]),
                                    kt[:, :].rearrange("p (o k) -> p o k", o=1).to_broadcast([P, E, MAXT]), ALU.is_gt))
            ch.link(V.tensor_reduce(nt[:, :].rearrange("p (e o) -> p e o", o=1), cmp[:, :, :], AX.X, ALU.add))
            ch.mark(V.tensor_scalar(skip[:, :], nt[:, :], -float(MT), float(CAP), ALU.mult, ALU.add))
            ch.link(V.tensor_tensor_scan(end[:, :], K.onesf[:, 0:E], nt[:, :], 0.0, ALU.mult, ALU.add))
            ch.mark(V.tensor_scalar(c2[:, 1:NT], K.iota[:, 1:NT], 2.0, end[:, E - 1:E], ALU.mult, ALU.is_lt))
            ch.mark(V.tensor_scalar(ended[:, :], end[:, :], end[:, E - 1:E], None, ALU.is_lt))
            ch.link(V.tensor_tensor(cj[:, :, :], end[:, :].rearrange("p (o e) -> p o e", o=1).to_broadcast([P, NT, E]),
                                    K.iota[:, 0:NT].rearrange("p (j o) -> p j o", o=1).to_broadcast([P, NT, E]), ALU.is_le))
            ch.mark(V.tensor_reduce(half[:, :], c2[:, 1:NT], AX.X, ALU.add))
            ch.mark(V.tensor_reduce(final[:, :], ended[:, :], AX.X, ALU.add))
            ch.link(V.tensor_reduce(te[:, :, 0:1], cj[:, :, :], AX.X, ALU.add))
            ch.mark(V.tensor_copy(K.LAST[:, :], half[:, :]))
            ch.link(V.tensor_tensor(cj[:, :, :], cj[:, :, :], skip[:, :].rearrange("p (o e) -> p o e", o=1).to_broadcast([P, NT, E]), ALU.mult))
            ch.mark(V.tensor_scalar(te[:, :, 0], te[:, :, 0], final[:, 0:1], None, ALU.min))
            ch.link(V.tensor_reduce(te[:, :, 1:2], cj[:, :, :], AX.X, ALU.add))
            ch.link(V.tensor_tensor(te[:, :, 1], te[:, :, 1], tj[:, :], ALU.add))
            ch.mark(V.tensor_scalar(te[:, :, 1], te[:, :, 1], float(E * CAP), None, ALU.min))
            for n, at in ((2, 2), (1, 4)):
                ch.mark(V.memset(te[:, 0:n, at:at + 1], 1.0))
                ch.mark(V.tensor_tensor(te[:, n:NT, at], te[:, n:NT, 0], te[:, 0:NT - n, 0], ALU.not_equal))
            ch.settle()
            for at, less in ((2, -1.0), (4, 0.0)):
                ch.mark(V.tensor_tensor_scan(te[:, :, at + 1], K.onesf[:, 0:NT], te[:, :, at], less, ALU.mult, ALU.add))
            ch.settle()
            ch.mark(V.tensor_copy(K.TE[:, :, :], te[:, :, :]))
            v.wait_ge(exp_out, TRIPS + 1 if router else 1)
            ch.link(V.tensor_scalar(WT[:, :, 0:1], WT[:, :, 1:2], 1.0, None, ALU.add))
            ch.link(V.reciprocal(WT[:, :, 0:1], WT[:, :, 0:1]))
            ch.mark(V.tensor_tensor(WT[:, :, 1:2], WT[:, :, 1:2], WT[:, :, 0:1], ALU.mult))

        n_w = 4 if gat_weights else (4 if router else 2)

        def load_results(sp, i):
            freed(sp, rows_used, i * BODY)
            for k in range(2):
                a = i * (BODY * P) + k * NODEROWS
                at = slice(a, a + BODY * P) if isinstance(i, int) else bass.ds(sp.snap(a), BODY * P)
                sp.dma_start(rows[:, k, :, :], K.YS[at, :].rearrange("(t p) d -> p t d", p=P)).then_inc(rows_in, 16)

        def tiles(t, n):
            return slice(t, t + n) if isinstance(t, int) else bass.ds(t, n)

        with nc.Block() as block:
            @block.sync
            def _(sp):
                if gat_weights:
                    wd, first, second = gat_weights
                    for k in range(KC):
                        sp.dma_start(w[:, k, 0:DIM], wd[k * P:(k + 1) * P, :]).then_inc(w_in, 16)
                    for n, a in enumerate((first, second)):
                        sp.dma_start(att[:, n, :], a.rearrange("h c -> (h c)").partition_broadcast(P)).then_inc(w_in, 16)
                elif router:
                    r1, b1, r2, b2 = router
                    sp.dma_start(w[:, :, :], r1.rearrange("(k p) n -> p k n", p=P)).then_inc(w_in, 16)
                    sp.dma_start(rb1[:, :], b1.rearrange("(p o) -> p o", o=1)).then_inc(w_in, 16)
                    sp.dma_start(w2[:, :], r2).then_inc(w_in, 16)
                    sp.dma_start(bias[:, :], b2.partition_broadcast(P)).then_inc(w_in, 16)
                else:
                    wg, bg = gate
                    sp.dma_start(w[:, :, :], wg.rearrange("(k p) n -> p k n", p=P)).then_inc(w_in, 16)
                    sp.dma_start(bias[:, :], bg.partition_broadcast(P)).then_inc(w_in, 16)
                if routed:
                    sp.wait_ge(pad_made, 2)
                    sp.wait_ge(ends_ready, 1)
                    ends = [sp.value_load(K.PADS[0:1, e:e + 1], min_val=0, max_val=BLANK - MT) for e in range(E)]
                    for e, r0 in enumerate([*ends, E * CAP]):
                        at = slice(r0, r0 + MT) if e == E else bass.ds(r0, MT)
                        sp.dma_start(K.XS[at, :].rearrange("(s p) d -> p s d", p=P), pad[:, e % 2, :, :]).then_inc(padded, 16)
                    sp.wait_ge(padded, 16 * (E + 1))
                if gat_weights:
                    if pre == "combine":
                        load_results(sp, 0)
                        load_results(sp, 1)
                    with sp.Fori(0, TRIPS) as i:
                        r0 = sp.snap(i * (BODY * P))
                        if pre == "combine":
                            with sp.If(i < TRIPS - 2):
                                load_results(sp, i + 2)
                        half = sp.snap((i % 2) * BODY)
                        n_st = sp.snap((i + 1) * (32 if pre == "load" else 16))
                        freed(sp, o_ready, i * BODY + BODY)
                        if pre == "load":
                            sp.dma_start(K.T0[bass.ds(r0, BODY * P), :].rearrange("(t p) c -> p t c", p=P),
                                         og[:, bass.ds(half, BODY), 0:DIM + 4]).then_inc(stored, 16)
                            sp.dma_start(K.AL[bass.ds(r0, BODY * P), :].rearrange("(t p) c -> p t c", p=P),
                                         og[:, bass.ds(half, BODY), DIM + 4:DIM + 8]).then_inc(stored, 16)
                        else:
                            sp.dma_start(K.T1[bass.ds(r0, BODY * P), :].rearrange("(t p) c -> p t c", p=P),
                                         og[:, bass.ds(half, BODY), 0:DIM + 4]).then_inc(stored, 16)
                        sp.wait_ge(stored, n_st)
                        sp.sem_inc(passed, 1)
                        with sp.If(i < TRIPS - 1):
                            sp.wait_ge(o_ready, sp.snap(i * BODY + (BODY + 2)))
                            sp.sem_inc(og_free, 1)
                K.clear_last(sp)

            @block.gpsimd
            def _(gp):
                lift(gp, lifts)
                if routed:
                    nc.gpsimd.iota(token[:, :], pattern=[[P, TILES]], base=0, channel_multiplier=1,
                                   allow_small_or_imprecise_dtypes=True).then_inc(token_made, 1)
                    nc.gpsimd.iota(pad[:, :, :, DIM].rearrange("p e s -> p (e s)"), pattern=[[P, 2 * SUB]], base=YDUMP,
                                   channel_multiplier=1, allow_small_or_imprecise_dtypes=True).then_inc(pad_made, 1)

                def gather(i):
                    for j in range(BODY):
                        t = i * BODY + j
                        freed(gp, rows_used, max(0, t - BODY + 1))
                        gp.indirect_dma_start(rows[:, j, :], None, K.T0,
                                              bass.IndirectOffsetOnAxis(ap=K.dstI[:, t:t + 1], axis=0)).then_inc(gathered[j], 16)
                        gp.indirect_dma_start(left[:, j, :], None, K.AL,
                                              bass.IndirectOffsetOnAxis(ap=K.srcI[:, t:t + 1], axis=0)).then_inc(gathered[j], 16)

                def scatter(i, k):
                    gp.wait_ge(slots_ready, i + 1)
                    freed(gp, y_kept, (i + 1) * BODY)
                    if k == 1:
                        gp.wait_ge(moved, i + 1)
                    for t in range(i * BODY, (i + 1) * BODY):
                        gp.indirect_dma_start(K.XS, bass.IndirectOffsetOnAxis(ap=K.POS[:, t, k:k + 1], axis=0),
                                              Y[:, t, :], None).then_inc(sent[k], 16)

                if pre == "load":
                    def load(i, to, rows):
                        gp.dma_start(to, rows.rearrange("(t p) d -> p t d", p=P)).then_inc(x_in, 16)
                        gp.wait_ge(x_in, i * 16 + 16)

                    load(0, K.X[:, 0:BODY, :], x[0:BODY * P, :])
                    edges.load(gp)
                    with gp.Fori(1, TRIPS - 1) as i:
                        load(i, K.X[:, bass.ds(i * BODY, BODY), :], x[bass.ds(gp.snap(i * (BODY * P)), BODY * P), :])
                    full = (TILES - 1) * P
                    load(TRIPS - 1, K.X[:, (TRIPS - 1) * BODY:TILES - 1, :], x[(TRIPS - 1) * BODY * P:full, :])
                    gp.dma_start(K.X[0:TAIL, TILES - 1, :], x[full:NODES, :]).then_inc(x_in, 16)
                    edges.turn(gp)

                late = 2 if pre == "attn0" else 0
                for i in range(TRIPS + late + 1):
                    if pre == "attn0" and i < TRIPS:
                        gather(i)
                    if routed and 0 <= i - late < TRIPS:
                        scatter(i - late, 0)
                    if routed and 0 <= i - late - 1 < TRIPS:
                        scatter(i - late - 1, 1)
                if routed:
                    for k in range(2):
                        gp.wait_ge(sent[k], 16 * TILES)

            @block.vector
            def _(v):
                if gat_weights:
                    ch = Chain(v, w_ready)
                    v.wait_ge(w_in, 16 * n_w)
                    for k in range(KC):
                        ch.link(nc.vector.tensor_tensor(prod[:, :, :], att[:, :, :],
                                                        w[:, k:k + 1, 0:DIM].to_broadcast([P, 2, DIM]), ALU.mult))
                        ch.link(nc.vector.tensor_reduce(w[:, k, DIM:DIM + 8],
                                                        prod[:, :, :].rearrange("p n (h c) -> p (n h) c", h=HEADS),
                                                        AX.X, ALU.add))
                if routed:
                    for e in range(2):
                        last = nc.vector.memset(pad[:, e, :, 0:DIM], 0.0)
                    last.then_inc(pad_made, 1)
                    v.wait_ge(token_made, 1)
                    nc.vector.tensor_copy(Y[:, :, DIM], token[:, :]).then_inc(consts, 1)
                    nc.vector.tensor_scalar(rev[:, :], K.iota[:, 0:E], -1.0, float(E), ALU.mult, ALU.add).then_inc(consts, 1)
                    nc.vector.tensor_scalar(region[:, :], K.iota[:, 0:E], float(CAP), None, ALU.mult).then_inc(consts, 1)
                    nc.vector.memset(before[:, :], 0.0).then_inc(consts, 1)
                    v.wait_ge(consts, 4)

                def update(i):
                    t0 = i * BODY
                    per = {None: 0, "load": 0, "attn0": 6 + 2 * BODY, "combine": BODY}[pre] + BODY
                    ch = Chain(v, chain, i * per)
                    if pre == "load":
                        v.wait_ge(x_in, i * 16 + (32 if isinstance(i, int) and i == TRIPS - 1 else 16))
                        v.sem_inc(passed, 1)
                    if pre == "attn0":
                        for j in range(BODY):
                            v.wait_ge(gathered[j], i * 32 + 32)
                        ch.link(nc.vector.tensor_tensor(z[:, :, :], left[:, :, :], rows[:, :, DIM:DIM + 4], ALU.add))
                        ch.link(nc.vector.scalar_tensor_tensor(z[:, :, :], z[:, :, :], 0.01, z[:, :, :], ALU.mult, ALU.max))
                        ch.link(nc.vector.tensor_reduce(z1[:, :, :], z[:, :, :], AX.X, ALU.max))
                        nc.vector.tensor_tensor(z[:, :, :], z[:, :, :], z1[:, :, :].to_broadcast([P, BODY, 4]),
                                                ALU.subtract).then_inc(z_ready, 1)
                        v.wait_ge(exps_done, i + 1)
                        ch.link(nc.vector.tensor_reduce(z1[:, :, :], z[:, :, :], AX.X, ALU.add))
                        ch.link(nc.vector.reciprocal(z1[:, :, :], z1[:, :, :]))
                        ch.link(nc.vector.tensor_tensor(z[:, :, :], z[:, :, :], z1[:, :, :].to_broadcast([P, BODY, 4]), ALU.mult))
                        for j in range(BODY):
                            ch.mark(nc.vector.tensor_tensor(
                                mix[:, j, :].rearrange("p (h c) -> p h c", h=HEADS),
                                rows[:, j, 0:DIM].rearrange("p (h c) -> p h c", h=HEADS),
                                z[:, j, :].rearrange("p (h o) -> p h o", o=1).to_broadcast([P, HEADS, CH]), ALU.mult))
                        ch.settle()
                        for j in range(BODY):
                            ch.mark(nc.vector.tensor_reduce(
                                tmp[:, j, :].rearrange("p (c o) -> p c o", o=1),
                                mix[:, j, :].rearrange("p (h c) -> p c h", h=HEADS), AX.X, ALU.add))
                        ch.settle()
                        for j in range(BODY):
                            Xt = K.X[:, tiles(t0 + j, 1), :].rearrange("p o (h c) -> p (o h) c", h=HEADS)
                            nc.vector.tensor_tensor(Xt, Xt, tmp[:, j:j + 1, :].to_broadcast([P, HEADS, CH]),
                                                    ALU.add).then_inc(rows_used, 1)
                        freed(v, rows_used, i * BODY + BODY)
                        v.sem_inc(passed, 1)
                    if pre == "combine":
                        v.wait_ge(rows_in, i * 32 + 32)
                        for j in range(BODY):
                            Xt = K.X[:, tiles(t0 + j, 1), :].rearrange("p o d -> p (o d)")
                            Wt = K.WT[:, tiles(t0 + j, 1), :].rearrange("p o d -> p (o d)")
                            ch.mark(nc.vector.scalar_tensor_tensor(Xt, rows[:, 0, j, :], Wt[:, 0:1], Xt, ALU.mult, ALU.add))
                        ch.settle()
                        for j in range(BODY):
                            Xt = K.X[:, tiles(t0 + j, 1), :].rearrange("p o d -> p (o d)")
                            Wt = K.WT[:, tiles(t0 + j, 1), :].rearrange("p o d -> p (o d)")
                            nc.vector.scalar_tensor_tensor(Xt, rows[:, 1, j, :], Wt[:, 1:2], Xt,
                                                           ALU.mult, ALU.add).then_inc(rows_used, 1)
                        freed(v, rows_used, i * BODY + BODY)
                        v.sem_inc(passed, 1)
                    for j in range(BODY):
                        ch.mark(nc.vector.bn_stats(stats[:, j, :], K.X[:, tiles(t0 + j, 1), :].rearrange("p o d -> p (o d)")))
                    ch.settle()
                    v.sem_inc(passed, 1)
                    for j in range(BODY):
                        last = nc.vector.bn_aggr(mv[:, j, :], stats[:, j, :])
                    last.then_inc(stats_ready, 1)
                    assert ch.n == per

                def norm(i):
                    t0 = i * BODY
                    v.wait_ge(std_ready, i + 1)
                    nc.vector.reciprocal(rstd[:, :, :], std[:, :, :]).then_inc(rstd_ready, 1)
                    v.wait_ge(rstd_ready, i + 1)
                    freed(v, pT_ready, i * BODY)
                    if routed:
                        freed(v, y_kept, i * BODY)
                    for j in range(BODY):
                        nc.vector.tensor_scalar(yg[:, j, :], K.X[:, tiles(t0 + j, 1), :].rearrange("p o d -> p (o d)"),
                                                mv[:, j, 0:1], rstd[:, j, :], ALU.subtract, ALU.mult).then_inc(y_ready, 1)

                placing = 21 + (4 if router else 0)

                def place(i):
                    V = nc.vector
                    t0 = i * BODY
                    ch = Chain(v, place_chain, i * placing)
                    freed(v, pO_ready, i + 1)
                    V.tensor_tensor(lg[:, :, :], pO[0][:, 0:BODY * E].rearrange("p (t e) -> p t e", e=E),
                                    bias[:, :].rearrange("p (o e) -> p o e", o=1).to_broadcast([P, BODY, E]), ALU.add).then_inc(o_ready, 1)
                    freed(v, o_ready, i + 1)
                    te = [P, BODY, E]

                    def of_expert(ap):
                        return ap[:, :].rearrange("p (o e) -> p o e", o=1).to_broadcast(te)

                    val = lg
                    if router:
                        ch.link(V.tensor_reduce(r[:, :, :], lg[:, :, :], AX.X, ALU.max))
                        V.tensor_tensor(p[:, :, :], lg[:, :, :], r[:, :, :].to_broadcast(te), ALU.subtract).then_inc(exp_in, 1)
                        v.wait_ge(exp_out, i + 1)
                        ch.link(V.tensor_reduce(r[:, :, :], p[:, :, :], AX.X, ALU.add))
                        ch.link(V.reciprocal(r[:, :, :], r[:, :, :]))
                        ch.link(V.tensor_tensor(p[:, :, :], p[:, :, :], r[:, :, :].to_broadcast(te), ALU.mult))
                        val = p
                    for k in range(2):
                        top = K.WT[:, tiles(t0, BODY), k:k + 1]
                        ch.link(V.tensor_reduce(top, val[:, :, :], AX.X, ALU.max))
                        ch.link(V.tensor_tensor(c[0][:, :, :], val[:, :, :], top.to_broadcast(te), ALU.is_equal))
                        ch.link(V.tensor_tensor(c[0][:, :, :], c[0][:, :, :], of_expert(rev), ALU.mult))
                        ch.link(V.tensor_reduce(r[:, :, :], c[0][:, :, :], AX.X, ALU.max))
                        ch.link(V.tensor_tensor(M[k][:, :, :], c[0][:, :, :], r[:, :, :].to_broadcast(te), ALU.is_equal))
                        if k == 0:
                            ch.link(V.scalar_tensor_tensor(val[:, :, :], M[0][:, :, :], -HUGE, val[:, :, :], ALU.mult, ALU.add))
                    for k in range(2):
                        ch.mark(V.tensor_tensor(M[k][:, :, :], M[k][:, :, :], K.valids[:, tiles(t0, BODY), :].to_broadcast(te), ALU.mult))
                    ch.settle()
                    V.tensor_tensor(Mb[:, :, :], M[0][:, :, :], M[1][:, :, :], ALU.add).then_inc(masks, 1)
                    v.wait_ge(ranks, i + 1)
                    ch.link(V.tensor_tensor(rank[:, :, :], pr[:, 0:BODY * E].rearrange("p (t e) -> p t e", e=E), of_expert(region), ALU.add))
                    ch.mark(V.tensor_reduce(here[:, :].rearrange("p (e o) -> p e o", o=1), Mb[:, :, :].rearrange("p t e -> p e t"), AX.X, ALU.add))
                    for k in range(2):
                        ch.mark(V.tensor_tensor(c[k][:, :, :], M[k][:, :, :], rank[:, :, :], ALU.mult))
                    ch.settle()
                    ch.mark(V.tensor_tensor(before[:, :], before[:, :], here[:, :], ALU.add))
                    for k in range(2):
                        ch.mark(V.tensor_reduce(pos[:, :, k:k + 1], c[k][:, :, :], AX.X, ALU.add))
                    ch.settle()
                    ch.link(V.tensor_tensor(pos[:, :, :], pos[:, :, :], K.dump[:, tiles(t0, BODY), :], ALU.add))
                    assert ch.n == placing, ch.n
                    if not isinstance(i, int) or i > 0:
                        move(i - 1, t0 - BODY)
                    V.tensor_copy(K.POS[:, tiles(t0, BODY), :], pos[:, :, :]).then_inc(slots_ready, 1)

                def move(i, t0):
                    v.wait_ge(sent[0], i * (16 * BODY) + 16 * BODY)
                    nc.vector.tensor_scalar(Y[:, tiles(t0, BODY), DIM:DIM + 1].rearrange("p t o -> p (t o)"), token[:, tiles(t0, BODY)],
                                            float(NODEROWS), None, ALU.add).then_inc(moved, 1)

                def trip(i):
                    if not isinstance(i, int) or i + 1 < TRIPS:
                        norm(i + 1)
                    if routed:
                        place(i)
                    if not isinstance(i, int) or i + 2 < TRIPS:
                        update(i + 2)

                update(0)
                norm(0)
                update(1)
                trip(0)
                if pre == "load":
                    edges.spans(v)
                with v.Fori(1, TRIPS - 3) as i:
                    trip(i)
                trip(TRIPS - 3)
                trip(TRIPS - 2)
                trip(TRIPS - 1)
                if pre == "load":
                    edges.table(v)
                if routed:
                    tables(Chain(v, place_chain, TRIPS * placing))
                    move(TRIPS - 1, (TRIPS - 1) * BODY)

            @block.scalar
            def _(act):
                def deviations(i):
                    if pre == "attn0":
                        act.wait_ge(z_ready, i + 1)
                        nc.scalar.activation(z[:, :, :], z[:, :, :], ACT.Exp).then_inc(exps_done, 1)
                    act.wait_ge(stats_ready, i + 1)
                    nc.scalar.activation(std[:, :, :], mv[:, :, 1:2], ACT.Sqrt, bias=K.eps[:, 0:1]).then_inc(std_ready, 1)

                deviations(0)
                with act.Fori(0, TRIPS) as i:
                    t0 = i * BODY
                    half = act.snap((i % 2) * BODY) if gat_weights else None

                    def take(j):
                        if gat_weights:
                            if j == 0:
                                with act.If(i > 1):
                                    act.wait_ge(og_free, i)
                                    act.sem_inc(passed, 1)
                            freed(act, pO_ready, i * BODY + j + 1)
                            if pre != "load":
                                nc.scalar.activation(K.AD[:, bass.ds(t0 + j, 1), :].rearrange("p o d -> p (o d)"),
                                                     pO[j % 2][:, DIM:DIM + 8], ACT.Copy)
                            nc.scalar.activation(og[:, bass.ds(half + j, 1), :].rearrange("p o d -> p (o d)"), pO[j % 2][:, 0:NC], ACT.Copy).then_inc(o_ready, 1)

                    def hidden(j):
                        act.wait_ge(pR_ready, i * BODY + j + 1)
                        nc.scalar.activation(rhT[:, j, :], pR[j % 2][:, 0:P], ACT.Relu, bias=rb1[:, 0:1]).then_inc(rh_ready, 1)

                    freed(act, pO_ready, i if routed else i * BODY)
                    for j in range(BODY):
                        freed(act, pT_ready, i * BODY + j + 1)
                        nc.scalar.activation(yT[:, j, :, :].rearrange("p k m -> p (k m)"), pT[j % 2][:, 0:KC * P],
                                             ACT.Copy).then_inc(yT_ready, 1)
                        if not gat_weights:
                            nc.scalar.activation(Y[:, bass.ds(t0 + j, 1), 0:DIM].rearrange("p o d -> p (o d)"), yg[:, j, :],
                                                 ACT.Copy).then_inc(y_kept, 1)
                        if router:
                            if j:
                                hidden(j - 1)
                        elif j and gat_weights:
                            take(j - 1)
                        if j == BODY - 2:
                            with act.If(i < TRIPS - 1):
                                deviations(i + 1)
                    if router:
                        hidden(BODY - 1)
                        act.wait_ge(exp_in, i + 1)
                        nc.scalar.activation(p[:, :, :], p[:, :, :], ACT.Exp).then_inc(exp_out, 1)
                    elif gat_weights:
                        take(BODY - 1)
                if routed:
                    act.wait_ge(exp_in, TRIPS + 1 if router else 1)
                    nc.scalar.activation(K.WT[:, :, 1:2], K.WT[:, :, 1:2], ACT.Exp).then_inc(exp_out, 1)

            @block.tensor
            def _(pe):
                def transpose(i, j):
                    pe.wait_ge(y_ready, i * BODY + j + 1)
                    freed(pe, yT_ready, i * BODY + max(0, j - 1))
                    for k in range(KC):
                        last = nc.tensor.transpose(pT[j % 2][:, k * P:(k + 1) * P], yg[:, j, k * P:(k + 1) * P], K.ident[:, :])
                    last.then_inc(pT_ready, 1)

                def outputs(i, j, left, right, n):
                    if gat_weights:
                        freed(pe, o_ready, i * BODY + max(0, j - 1))
                    elif j == 0:
                        freed(pe, o_ready, i)
                    out = pO[j % 2][:, 0:NC] if gat_weights else pO[0][:, j * NC:(j + 1) * NC]
                    for k in range(n):
                        last = nc.tensor.matmul(out, left(k), right(k), start=(k == 0), stop=(k == n - 1))
                    if gat_weights or j == BODY - 1:
                        last.then_inc(pO_ready, 1)

                def multiply(i, j):
                    freed(pe, yT_ready, i * BODY + j + 1)
                    if router:
                        freed(pe, rh_ready, i * BODY + max(0, j - 1))
                        for k in range(KC):
                            last = nc.tensor.matmul(pR[j % 2][:, 0:P], w[:, k, :], yT[:, j, k, :], start=(k == 0), stop=(k == KC - 1))
                        last.then_inc(pR_ready, 1)
                    else:
                        outputs(i, j, lambda k: yT[:, j, k, :], lambda k: w[:, k, :], KC)

                def second(i, j):
                    freed(pe, rh_ready, i * BODY + j + 1)
                    outputs(i, j, lambda k: rhT[:, j, :], lambda k: w2[:, :], 1)

                def count(i):
                    pe.wait_ge(masks, i + 1)
                    nc.tensor.matmul(pr[:, 0:BODY * E], K.tri[:, :], Mb[:, :, :].rearrange("p t e -> p (t e)"), start=True, stop=False)
                    for j in range(BODY - 1):
                        n = BODY - 1 - j
                        nc.tensor.matmul(pr[:, (j + 1) * E:BODY * E].rearrange("p (t e) -> p t e", e=E), K.ones[:, :],
                                         Mb[:, j:j + 1, :].to_broadcast([P, n, E]), start=False, stop=False)
                    nc.tensor.matmul(pr[:, 0:BODY * E].rearrange("p (t e) -> p t e", e=E), K.ones[:, :],
                                     before[:, :].rearrange("p (o e) -> p o e", o=1).to_broadcast([P, BODY, E]),
                                     start=False, stop=True).then_inc(ranks, 1)

                def trip(i):
                    for j in range(BODY + 2):
                        if j < BODY:
                            transpose(i, j)
                        if 1 <= j <= BODY:
                            multiply(i, j - 1)
                        if router and j >= 2:
                            second(i, j - 2)
                        if routed and j == 2 and not isinstance(i, int):
                            count(i - 1)

                if gat_weights:
                    pe.wait_ge(w_ready, 2 * KC)
                else:
                    pe.wait_ge(w_in, 16 * n_w)
                trip(0)
                with pe.Fori(1, TRIPS) as i:
                    trip(i)
                if routed:
                    count(TRIPS - 1)
                if routed:
                    pe.wait_ge(count_in, 1)
                    nc.tensor.matmul(pr[:, 0:E], K.ones[:, :], before[:, :], start=True, stop=True).then_inc(ranks, 1)


def experts(K, tag, E, wa, ba, H, func, wm, bm, wl, bl):
    nc = K.nc
    HC = H // P
    units = HC + (H // P if wm is not None else 0)
    with ExitStack() as stack:
        sb, pb, sem = K.tools(stack, tag)
        parted = wm is None

        def parts(name, shape):
            return [sb(f"{name}_{part}", shape, F32R) for part in ("high", "low")] if parted else [sb(name, shape)]

        WA = [parts(f"WA{b}", [P, KC, H]) for b in range(2)]
        WL = [parts(f"WL{b}", [P, HC, DIM]) for b in range(2)]
        WM = [parts(f"WM{b}", [P, HC, H]) for b in range(2)] if wm is not None else None
        rawA = sb("rawA", [P, KC, H])
        rawL = sb("rawL", [P, HC, DIM])
        rawB = sb("rawB", [P, DIM])
        rawM = sb("rawM", [P, HC, H]) if wm is not None else None
        BA = sb("BA", [P, E * HC])
        BM = sb("BM", [P, E * HC]) if wm is not None else None
        BL = [sb(f"BL{b}", [P, DIM]) for b in range(2)]
        xs = [sb(f"xs{b}", [P, SUB, WIDE]) for b in range(2)]
        to_f = [sb(f"to_f{b}", [P, SUB]) for b in range(2)]
        to = [sb(f"to{b}", [P, SUB], I32) for b in range(2)]
        xT = parts("xT", [P, KC, MT])
        full = [sb(f"full{n}", [P, MT]) for n in range(4 if parted else 0)]
        hT = [parts(f"hT{b}", [P, HC, MT]) for b in range(2)]
        mT = [parts(f"mT{b}", [P, HC, MT]) for b in range(2)] if wm is not None else None
        ob = [sb(f"ob{b}", [P, SUB, DIM]) for b in range(2)]
        pX = [pb(f"pX{b}", [P, KC, MT]) for b in range(2)]
        pH = [pb(f"pH{n}", [P, 512]) for n in range(4)]
        pO = [pb(f"pO{n}", [P, 512]) for n in range(2)]

        biases_in = sem("biases_in")
        wa_in = sem("wa_in")
        wm_in = sem("wm_in")
        wl_in = sem("wl_in")
        wa_split = sem("wa_split")
        wm_split = sem("wm_split")
        wl_split = sem("wl_split")
        x_high = sem("x_high")
        wa_high = sem("wa_high")
        wl_high = sem("wl_high")
        x_in = [sem(f"x_in{b}") for b in range(2)]
        pX_ready = [sem(f"pX_ready{b}") for b in range(2)]
        xT_ready = sem("xT_ready")
        to_ready = sem("to_ready")
        pH_ready = sem("pH_ready")
        h_ready = sem("h_ready")
        l_ready = sem("l_ready") if parted else h_ready
        tile_done = [sem(f"tile_done{b}") for b in range(2)]
        half_ready = sem("half_ready")
        o_ready = sem("o_ready")
        sent = [sem(f"sent{b}", software=True) for b in range(2)]
        passed = sem("passed")
        ob_free = [sem(f"ob_free{b}") for b in range(2)]
        lifts = (xT_ready, to_ready, pH_ready, h_ready, wa_split, wm_split, wl_split, o_ready, *pX_ready, *tile_done, *ob_free) + ((l_ready,) if parted else ())
        n_b = 2 if wm is not None else 1

        def field(eng, j, c, top):
            at = slice(j, j + 1) if isinstance(j, int) else bass.ds(j, 1)
            return eng.value_load(K.TE[0:1, at, c:c + 1].rearrange("o a b -> o (a b)"), min_val=0, max_val=top)

        def last_pair(eng):
            return eng.value_load(K.LAST[0:1, 0:1], min_val=0, max_val=(NT - 1) // 2 - 1)

        with nc.Block() as block:
            @block.gpsimd
            def _(gp):
                lift(gp, lifts)

                def split_last(i, b):
                    before = field(gp, i * 2 + b, 3, NT)
                    gp.wait_ge(wl_in, field(gp, i * 2 + b, 5, NT) * 32)
                    freed(gp, tile_done[b], i)
                    gp.sem_inc(passed, 1)
                    nc.gpsimd.tensor_copy(BL[b][:, :], rawB[:, :])
                    if not parted:
                        nc.gpsimd.tensor_copy(WL[b][0][:, :, :], rawL[:, :, :]).then_inc(wl_split, 1)
                        return
                    nc.gpsimd.tensor_copy(WL[b][0][:, :, :], rawL[:, :, :]).then_inc(wl_high, 1)
                    gp.wait_ge(wl_high, before + 1)
                    nc.gpsimd.tensor_tensor(WL[b][1][:, :, :], rawL[:, :, :], WL[b][0][:, :, :], ALU.subtract).then_inc(wl_split, 1)

                split_last(0, 0)
                split_last(0, 1)
                with gp.Fori(0, gp.snap(last_pair(gp) + 1)) as i:
                    for b in range(2):
                        freed(gp, o_ready, (i * 2 + b + 1) * SUB)
                        gp.sem_inc(passed, 1)
                        for s in range(SUB):
                            gp.indirect_dma_start(K.YS, bass.IndirectOffsetOnAxis(ap=to[b][:, s:s + 1], axis=0),
                                                  ob[b][:, s, :], None).then_inc(sent[b], 16)
                        with gp.If(field(gp, i * 2 + b + 2, 2, 1) > 0):
                            split_last(i + 1, b)
                        if b == 1:
                            for c in range(2):
                                gp.wait_ge(sent[c], i * (16 * SUB) + 16 * SUB)
                                gp.sem_inc(ob_free[c], 1)

            @block.sync
            def _(sp):
                sp.dma_start(BA[:, :], ba.rearrange("e (c p) -> p (e c)", p=P), allow_slow_non_contiguous=True).then_inc(biases_in, 16)
                if wm is not None:
                    sp.dma_start(BM[:, :], bm.rearrange("e (c p) -> p (e c)", p=P), allow_slow_non_contiguous=True).then_inc(biases_in, 16)
                wa_r = wa.rearrange("e k h -> (e k) h")
                wl_r = wl.rearrange("e h d -> (e h) d")
                wm_r = wm.rearrange("e h d -> (e h) d") if wm is not None else None

                bl_r = bl.rearrange("e d -> (e d)")

                def load(to, in_sem, src, row, rows):
                    sp.dma_start(to[:, :, :], src[bass.ds(row, rows), :].rearrange("(k p) h -> p k h", p=P)).then_inc(in_sem, 16)

                def rows(i, b):
                    r0 = field(sp, i * 2 + b, 1, BLANK)
                    if not isinstance(i, int) or i > 0:
                        freed(sp, pX_ready[b], i)
                        freed(sp, to_ready, i * 2 + b - 1)
                    sp.dma_start(xs[b][:, :, :], K.XS[bass.ds(r0, MT), :].rearrange("(s p) d -> p s d", p=P)).then_inc(x_in[b], 16)

                def weights(i, b):
                    e = field(sp, i * 2 + b, 0, E - 1)
                    before = field(sp, i * 2 + b, 3, NT)
                    ra = sp.snap(e * DIM)
                    rl = sp.snap(e * H)
                    with sp.If(field(sp, i * 2 + b, 4, 1) > 0):
                        freed(sp, wa_split, before)
                        load(rawA, wa_in, wa_r, ra, DIM)
                        if wm is not None:
                            freed(sp, wm_split, before)
                            load(rawM, wm_in, wm_r, rl, H)
                        freed(sp, wl_split, before)
                        load(rawL, wl_in, wl_r, rl, H)
                        sp.dma_start(rawB[:, :], bl_r[bass.ds(ra, DIM)].partition_broadcast(P)).then_inc(wl_in, 16)

                weights(0, 0)
                last = last_pair(sp)
                rows(0, 0)
                rows(0, 1)
                weights(0, 1)
                with sp.Fori(1, sp.snap(last + 1)) as i:
                    for b in range(2):
                        rows(i, b)
                        weights(i, b)
                K.clear_last(sp)

            @block.tensor
            def _(pe):
                def transpose(i, b):
                    pe.wait_ge(x_in[b], i * 16 + 16)
                    if not isinstance(i, int):
                        freed(pe, xT_ready, i * 2 + b - 1)
                    for s in range(SUB):
                        for k in range(KC):
                            last = nc.tensor.transpose(pX[b][:, k, s * P:(s + 1) * P], xs[b][:, s, k * P:(k + 1) * P], K.ident[:, :])
                    last.then_inc(pX_ready[b], 1)

                def product(out, left, right, start, stop):
                    if not parted:
                        return nc.tensor.matmul(out, left[0], right[0], start=start, stop=stop)
                    nc.tensor.matmul(out, left[0], right[0], start=start, stop=False)
                    nc.tensor.matmul(out, left[0], right[1], start=False, stop=False)
                    return nc.tensor.matmul(out, left[1], right[0], start=False, stop=stop)

                def hidden(i, b, W, src, nk, u0):
                    for u in range(HC):
                        if u0 + u - 3 > HC or not u0:
                            freed(pe, h_ready, (i * 2 + b) * units + max(0, u0 + u - 3))
                        for k in range(nk):
                            last = product(pH[(u0 + u) % 4][:, 0:MT], [w[:, k, u * P:(u + 1) * P] for w in W[b]],
                                           [a[:, k, :] for a in src], k == 0, k == nk - 1)
                        last.then_inc(pH_ready, 1)

                loads = {}

                def first(i, b):
                    loads[b] = field(pe, i * 2 + b, 3, NT)
                    freed(pe, xT_ready, i * 2 + b + 1)
                    freed(pe, wa_split, loads[b] + 1)
                    hidden(i, b, WA, xT, KC, 0)

                def middle(i, b):
                    if wm is not None:
                        freed(pe, wm_split, loads[b] + 1)
                        freed(pe, l_ready, (i * 2 + b) * units + HC)
                        hidden(i, b, WM, hT[b], HC, HC)

                def final(i, b):
                    act_in = mT if wm is not None else hT
                    freed(pe, wl_split, loads[b] + 1)
                    freed(pe, l_ready, (i * 2 + b + 1) * units)
                    for s in range(SUB):
                        freed(pe, o_ready, (i * 2 + b) * SUB)
                        for k in range(HC):
                            last = product(pO[s][:, 0:DIM], [a[:, k, s * P:(s + 1) * P] for a in act_in[b]],
                                           [w[:, k, :] for w in WL[b]], k == 0, k == HC - 1)
                        last.then_inc(half_ready if s == 0 else tile_done[b], 1)

                pe.wait_ge(biases_in, 16 * n_b)
                last = last_pair(pe)
                transpose(0, 0)
                first(0, 0)
                transpose(0, 1)
                middle(0, 0)
                with pe.Fori(0, last) as i:
                    first(i, 1)
                    transpose(i + 1, 0)
                    loads[0] = field(pe, i * 2, 3, NT)
                    final(i, 0)
                    middle(i, 1)
                    first(i + 1, 0)
                    transpose(i + 1, 1)
                    final(i, 1)
                    middle(i + 1, 0)
                first(last, 1)
                loads[0] = field(pe, last * 2, 3, NT)
                final(last, 0)
                middle(last, 1)
                final(last, 1)

            @block.scalar
            def _(act):
                act.wait_ge(biases_in, 16 * n_b)
                with act.Fori(0, act.snap(last_pair(act) + 1)) as i:
                    for b in range(2):
                        e = field(act, i * 2 + b, 0, E - 1)
                        freed(act, tile_done[b], i)
                        for u in range(units):
                            freed(act, pH_ready, (i * 2 + b) * units + u + 1)
                            dst, bias, c = (hT, BA, u) if u < HC else (mT, BM, u - HC)
                            at = bias[:, bass.ds(e * HC + c, 1)]
                            if parted:
                                freed(act, l_ready, (i * 2 + b) * units + max(0, u - 3))
                                nc.scalar.activation(full[u % 4][:, :], pH[u % 4][:, 0:MT], func, bias=at)
                            nc.scalar.activation(dst[b][0][:, c, :], pH[u % 4][:, 0:MT], func, bias=at).then_inc(h_ready, 1)

            @block.vector
            def _(v):
                V = nc.vector

                def x_out(i, b):
                    freed(v, pX_ready[b], i + 1)
                    if not isinstance(i, int) or b:
                        freed(v, pH_ready, (i * 2 + b - 1) * units + HC)
                    V.tensor_copy(xT[0][:, :, :], pX[b][:, :, :]).then_inc(x_high if parted else xT_ready, 1)
                    if not parted:
                        return
                    v.wait_ge(x_high, i * 2 + b + 1)
                    V.tensor_tensor(xT[1][:, :, :], pX[b][:, :, :], xT[0][:, :, :], ALU.subtract).then_inc(xT_ready, 1)

                def split_others(i, b, u, before):
                    if not parted:
                        V.tensor_copy(WA[b][0][:, :, :], rawA[:, :, :]).then_inc(wa_split, 1)
                        V.tensor_copy(WM[b][0][:, :, :], rawM[:, :, :]).then_inc(wm_split, 1)
                        return lambda: None
                    raw, high, lower = (t[:, :, :].rearrange("p k h -> p (k h)") for t in (rawA, *WA[b]))
                    size = KC * H // HC
                    at = slice(u * size, (u + 1) * size)
                    V.tensor_copy(high[:, at], raw[:, at]).then_inc(wa_high, 1)

                    def rest():
                        v.wait_ge(wa_high, before * HC + (u + 1))
                        ins = V.tensor_tensor(lower[:, at], raw[:, at], high[:, at], ALU.subtract)
                        if u == HC - 1:
                            ins.then_inc(wa_split, 1)
                    return rest

                def low(i, b, following):
                    i2, b2 = (i, 1) if b == 0 else (i + 1, 0)
                    if following:
                        before = field(v, i2 * 2 + b2, 3, NT)
                        loads = field(v, i2 * 2 + b2, 5, NT)
                        v.wait_ge(wa_in, loads * 16)
                        if wm is not None:
                            v.wait_ge(wm_in, loads * 16)
                        if not isinstance(i2, int):
                            freed(v, pH_ready, (i2 * 2 + b2 - 1) * units)
                    for u in range(HC if parted else 1):
                        if following:
                            rest = split_others(i2, b2, u, before)
                        if parted:
                            freed(v, h_ready, (i * 2 + b) * units + u + 1)
                            V.tensor_tensor(hT[b][1][:, u, :], full[u % 4][:, :], hT[b][0][:, u, :], ALU.subtract).then_inc(l_ready, 1)
                        if following:
                            rest()

                def low_any(i, b):
                    other = field(v, i * 2 + b + 1, 2, 1)
                    with v.If(other > 0):
                        low(i, b, True)
                    if parted:
                        with v.If(other < 1):
                            low(i, b, False)

                def keep_to(i, b):
                    if not isinstance(i, int):
                        freed(v, o_ready, (i * 2 + b - 1) * SUB)
                    V.tensor_copy(to_f[b][:, :], xs[b][:, :, DIM]).then_inc(to_ready, 1)

                def o_out(i, b):
                    freed(v, ob_free[b], i)
                    freed(v, to_ready, i * 2 + b + 1)
                    V.tensor_copy(to[b][:, :], to_f[b][:, :])
                    for s in range(SUB):
                        if s == 0:
                            v.wait_ge(half_ready, i * 2 + b + 1)
                        else:
                            freed(v, tile_done[b], i + 1)
                        V.tensor_tensor(ob[b][:, s, :], pO[s][:, 0:DIM], BL[b][:, :], ALU.add).then_inc(o_ready, 1)

                last = last_pair(v)
                v.wait_ge(wa_in, 16)
                if wm is not None:
                    v.wait_ge(wm_in, 16)
                for u in range(HC if parted else 1):
                    split_others(0, 0, u, 0)()
                x_out(0, 0)
                keep_to(0, 0)
                low(0, 0, True)
                x_out(0, 1)
                keep_to(0, 1)
                with v.Fori(0, last) as i:
                    for b in range(2):
                        low_any(i + b, 1 - b)
                        x_out(i + 1, b)
                        o_out(i, b)
                        keep_to(i + 1, b)
                low_any(last, 1)
                o_out(last, 0)
                o_out(last, 1)


def attention(K, bias_in):
    nc = K.nc
    J = range(len(CHUNKS))
    with ExitStack() as stack:
        sb, pb, sem = K.tools(stack, "at")
        gm = sb("gm", [P, HEADS])
        gt = sb("gt", [P, HEADS])
        adm = sb("adm", [P, TILES, 8])
        exs = sb("exs", [P, TILES, HEADS])
        pm = sem("pm")
        gm_ready = sem("gm_ready")
        gm_all = sem("gm_all")
        self_z = sem("self_z")
        with nc.Block() as block:
            @block.vector
            def _(v):
                V = nc.vector
                ch = Chain(v, pm)
                AS, ADs = K.AD[:, :, 0:4], K.AD[:, :, 4:8]
                ch.mark(V.tensor_reduce(gm[:, :].rearrange("p (h o) -> p h o", o=1),
                                        K.AD[:, 0:TILES - 1, 0:4].rearrange("p t h -> p h t"), AX.X, ALU.max))
                ch.link(V.tensor_scalar(gt[:, :], K.AD[:, TILES - 1, 0:4], K.vneg[:, 0:1], None, ALU.add))
                V.tensor_tensor(gm[:, :], gm[:, :], gt[:, :], ALU.max).then_inc(gm_ready, 1)
                v.wait_ge(gm_all, 1)
                ch.link(V.tensor_copy(adm[:, :, 0:4], ADs))
                ch.link(V.tensor_tensor(adm[:, :, 4:8], ADs, gt[:, :].rearrange("p (o h) -> p o h", o=1).to_broadcast([P, TILES, HEADS]), ALU.add))
                ch.link(V.scalar_tensor_tensor(adm[:, :, 4:8], adm[:, :, 4:8], 0.2, adm[:, :, 4:8], ALU.mult, ALU.max))
                ch.link(V.tensor_tensor(exs[:, :, :], AS, ADs, ALU.add))
                ch.link(V.scalar_tensor_tensor(exs[:, :, :], exs[:, :, :], 0.2, exs[:, :, :], ALU.mult, ALU.max))
                ch.link(V.tensor_tensor(exs[:, :, :], exs[:, :, :], adm[:, :, 4:8], ALU.subtract))
                V.tensor_scalar(exs[:, :, :], exs[:, :, :], 0.0, None, ALU.min).then_inc(self_z, 1)

            @block.gpsimd
            def _(gp):
                gp.wait_ge(gm_ready, 1)
                nc.gpsimd.partition_all_reduce(gt[:, :], gm[:, :], P, bass.bass_isa.ReduceOp.max).then_inc(gm_all, 1)

            @block.scalar
            def _(act):
                act.wait_ge(self_z, 1)
                nc.scalar.activation(exs[:, :, :], exs[:, :, :], ACT.Exp)

        idx = [sb(f"idx{j}", [P, CHUNKS[j]], I32) for j in J]
        dcol = [sb(f"dcol{j}", [P, CHUNKS[j]]) for j in J]
        drow = [sb(f"drow{j}", [P, CHUNKS[j] * P]) for j in J]
        G = [sb(f"G{j}", [P, CHUNKS[j], DIM + 4]) for j in J]
        OH = [sb(f"OH{j}", [P, CHUNKS[j], P]) for j in J]
        OT = [sb(f"OT{j}", [P, CHUNKS[j], P]) for j in J]
        Z = [sb(f"Z{j}", [P, CHUNKS[j], HEADS]) for j in J]
        own = sb("own", [P, DIM + 4])
        cur = sb("cur", [P, 8])
        TI = sb("TI", [P, P])
        TP = sb("TP", [P, 1])
        ACC = sb("ACC", [P, DIM + 4])
        bias = sb("bias", [P, DIM])
        res = sb("res", [P, DIM])
        rec = sb("rec", [P, HEADS])
        pAd = [pb(f"pAd{j}", [P, 512]) for j in J]
        pAgg = pb("pAgg", [P, 512])

        bias_ld = sem("bias_ld")
        init = sem("init")
        src_in = [sem(f"src_in{j}") for j in J]
        dst_in = [sem(f"dst_in{j}") for j in J]
        gathered = [sem(f"gathered{j}", software=True) for j in J]
        onehots = [sem(f"onehots{j}") for j in J]
        agg_done = [sem(f"agg_done{j}") for j in J]
        own_in = sem("own_in")
        own_used = sem("own_used")
        cur_ready = sem("cur_ready")
        ad_ready = sem("ad_ready")
        scored = [sem(f"scored{j}") for j in J]
        ex_ready = sem("ex_ready")
        msg_ready = sem("msg_ready")
        acc_done = sem("acc_done")
        chain = sem("chain")
        passed = sem("passed")
        NJ = len(CHUNKS)
        lifts = (own_used, acc_done, *scored, *onehots, *agg_done)
        START, STEP, END = 3, 3 * NJ, 5

        def tile_steps(eng, t):
            at = slice(t, t + 1) if isinstance(t, int) else bass.ds(t, 1)
            n = eng.value_load(K.ET[0:1, at, 1:2].rearrange("o a b -> o (a b)"), min_val=1, max_val=MAXSTEPS)
            s0 = eng.value_load(K.ET[0:1, at, 2:3].rearrange("o a b -> o (a b)"), min_val=0, max_val=TILES * MAXSTEPS)
            return n, s0

        with nc.Block() as block:
            @block.sync
            def _(sp):
                sp.dma_start(bias[:, :], bias_in.partition_broadcast(P)).then_inc(bias_ld, 16)
                with sp.Fori(0, TILES) as t:
                    n, s0 = tile_steps(sp, t)
                    base = sp.value_load(K.ET[0:1, bass.ds(t, 1), 0:1].rearrange("o a b -> o (a b)"), min_val=0, max_val=EDGES - GRAN)
                    r0 = sp.snap(t * P)
                    freed(sp, own_used, t)
                    sp.dma_start(own[:, :], K.T1[bass.ds(r0, P), :]).then_inc(own_in, 16)
                    with sp.Fori(0, n) as g:
                        s = sp.snap(s0 + g)
                        e0 = nc.s_assert_within(sp.snap(base + g * SE), 0, EDGES, skip_runtime_bounds_check_because=
                                                "a step begins before its tile's last edge, and SE edges of padding follow the last")
                        at = [sp.snap(e0 + OFFS[j]) for j in J]
                        for j in J:
                            ne = CHUNKS[j] * P
                            freed(sp, scored[j], s)
                            sp.dma_start(idx[j][:, :], K.SRCP[bass.ds(at[j], ne)].rearrange("(p c) -> p c", p=P)).then_inc(src_in[j], 16)
                            freed(sp, onehots[j], s)
                            sp.dma_start(dcol[j][:, :], K.DSTP[bass.ds(at[j], ne)].rearrange("(p c) -> p c", p=P)).then_inc(dst_in[j], 16)
                            sp.dma_start(drow[j][:, :], K.DSTP[bass.ds(at[j], ne)].partition_broadcast(P)).then_inc(dst_in[j], 16)
                K.clear_last(sp)

            @block.gpsimd
            def _(gp):
                lift(gp, lifts)
                n, s0 = tile_steps(gp, TILES - 1)
                with gp.Fori(0, gp.snap(s0 + n)) as s:
                    for j in J:
                        gp.wait_ge(src_in[j], s * 16 + 16)
                        freed(gp, agg_done[j], s)
                        gp.sem_inc(passed, 1)
                        for c in range(CHUNKS[j]):
                            gp.indirect_dma_start(G[j][:, c, :], None, K.T1,
                                                  bass.IndirectOffsetOnAxis(ap=idx[j][:, c:c + 1], axis=0)).then_inc(gathered[j], 16)

            @block.vector
            def _(v):
                V = nc.vector

                def one_hots(s, j):
                    c = CHUNKS[j]
                    v.wait_ge(dst_in[j], s * 32 + 32)
                    freed(v, agg_done[j], s)
                    V.tensor_tensor(OH[j][:, :, :], dcol[j][:, :].rearrange("p (c o) -> p c o", o=1).to_broadcast([P, c, P]),
                                    TI[:, :].rearrange("p (o n) -> p o n", o=1).to_broadcast([P, c, P]), ALU.is_equal)
                    V.tensor_scalar(OT[j][:, :, :], drow[j][:, :].rearrange("n (p c) -> n c p", c=c), TP[:, 0:1], None,
                                    ALU.is_equal).then_inc(onehots[j], 1)

                def scores(ch, s, j):
                    c = CHUNKS[j]
                    v.wait_ge(gathered[j], s * (16 * c) + 16 * c)
                    v.wait_ge(ad_ready, s * NJ + j + 1)
                    ad = pAd[j][:, 0:8 * c].rearrange("p (c k) -> p c k", k=8)
                    ch.link(V.tensor_tensor(Z[j][:, :, :], G[j][:, :, DIM:DIM + 4], ad[:, :, 0:4], ALU.add))
                    ch.link(V.scalar_tensor_tensor(Z[j][:, :, :], Z[j][:, :, :], 0.2, Z[j][:, :, :], ALU.mult, ALU.max))
                    ch.link(V.tensor_tensor(Z[j][:, :, :], Z[j][:, :, :], ad[:, :, 4:8], ALU.subtract))
                    V.tensor_scalar(Z[j][:, :, :], Z[j][:, :, :], 0.0, None, ALU.min).then_inc(scored[j], 1)

                def weigh(s, j):
                    c = CHUNKS[j]
                    v.wait_ge(ex_ready, s * NJ + j + 1)
                    rows = G[j][:, :, 0:DIM].rearrange("p c (h k) -> p c h k", h=HEADS)
                    ex = G[j][:, :, DIM:DIM + 4].rearrange("p c (h o) -> p c h o", o=1).to_broadcast([P, c, HEADS, CH])
                    V.tensor_tensor(rows, rows, ex, ALU.mult).then_inc(msg_ready, 1)

                def first_group(ch, s):
                    one_hots(s, 0)
                    one_hots(s, 1)
                    scores(ch, s, 0)
                    weigh(s, 0)

                def other_groups(ch, s):
                    one_hots(s, 2)
                    scores(ch, s, 1)
                    weigh(s, 1)
                    scores(ch, s, 2)
                    weigh(s, 2)

                def absorb(s):
                    freed(v, agg_done[NJ - 1], s)
                    V.tensor_tensor(ACC[:, :], ACC[:, :], pAgg[:, 0:DIM + 4], ALU.add).then_inc(acc_done, 1)
                    freed(v, acc_done, s)

                def finalize(ch, t):
                    ch.link(V.tensor_scalar(rec[:, :], ACC[:, DIM:DIM + 4], 1e-30, None, ALU.add))
                    ch.link(V.reciprocal(rec[:, :], rec[:, :]))
                    ch.link(V.tensor_tensor(res[:, :].rearrange("p (h k) -> p h k", h=HEADS),
                                            ACC[:, 0:DIM].rearrange("p (h k) -> p h k", h=HEADS),
                                            rec[:, :].rearrange("p (h o) -> p h o", o=1).to_broadcast([P, HEADS, CH]), ALU.mult))
                    ch.link(V.tensor_tensor(res[:, :], res[:, :], bias[:, :], ALU.add))
                    Xt = K.X[:, bass.ds(t, 1), :].rearrange("p o d -> p (o d)")
                    ch.mark(V.scalar_tensor_tensor(Xt, res[:, :], 0.0, Xt, ALU.max, ALU.add))

                def tile(t, before):
                    n, s0 = tile_steps(v, t)
                    ch = Chain(v, chain, t * START + before * END + s0 * STEP)
                    ch.mark(V.tensor_scalar(TI[:, :], TI[:, :], float(P), None, ALU.add))
                    ch.mark(V.tensor_scalar(TP[:, :], TP[:, :], float(P), None, ALU.add))
                    V.tensor_copy(cur[:, :], adm[:, bass.ds(t, 1), :].rearrange("p o k -> p (o k)")).then_inc(cur_ready, 1)
                    ch.settle()
                    first_group(ch, s0)
                    if not isinstance(t, int):
                        absorb(s0)
                        finalize(ch, t - 1)
                    ex_t = exs[:, bass.ds(t, 1), :].rearrange("p o h -> p (o h)")
                    v.wait_ge(own_in, t * 16 + 16)
                    V.tensor_tensor(ACC[:, 0:DIM].rearrange("p (h k) -> p h k", h=HEADS),
                                    own[:, 0:DIM].rearrange("p (h k) -> p h k", h=HEADS),
                                    ex_t.rearrange("p (h o) -> p h o", o=1).to_broadcast([P, HEADS, CH]), ALU.mult).then_inc(own_used, 1)
                    ch.link(V.tensor_copy(ACC[:, DIM:DIM + 4], ex_t))
                    freed(v, own_used, t + 1)
                    other_groups(ch, s0)
                    assert ch.n == START + STEP + (0 if isinstance(t, int) else END)
                    with v.If(n > 1):
                        with v.Fori(1, n) as g:
                            s = v.snap(s0 + g)
                            cs = Chain(v, chain, (t + 1) * START + t * END + s * STEP)
                            first_group(cs, s)
                            absorb(s)
                            other_groups(cs, s)
                            assert cs.n == STEP

                V.tensor_scalar(TI[:, :], K.iota[:, 0:P], -float(P), None, ALU.add).then_inc(init, 1)
                V.tensor_scalar(TP[:, :], K.pid[:, :], -float(P), None, ALU.add).then_inc(init, 1)
                v.wait_ge(init, 2)
                v.wait_ge(bias_ld, 16)
                tile(0, 0)
                with v.Fori(1, TILES) as t:
                    tile(t, t - 1)
                n, s0 = tile_steps(v, TILES - 1)
                s = v.snap(s0 + n)
                absorb(s)
                ch = Chain(v, chain, TILES * START + (TILES - 1) * END + s * STEP)
                finalize(ch, TILES - 1)

            @block.scalar
            def _(act):
                n, s0 = tile_steps(act, TILES - 1)
                with act.Fori(0, act.snap(s0 + n)) as s:
                    for j in J:
                        freed(act, scored[j], s + 1)
                        nc.scalar.activation(G[j][:, :, DIM:DIM + 4], Z[j][:, :, :], ACT.Exp).then_inc(ex_ready, 1)

            @block.tensor
            def _(pe):
                def destinations(s, j):
                    freed(pe, onehots[j], s + 1)
                    freed(pe, scored[j], s)
                    for c in range(CHUNKS[j]):
                        last = nc.tensor.matmul(pAd[j][:, 8 * c:8 * c + 8], OT[j][:, c, :], cur[:, :], start=True, stop=True)
                    last.then_inc(ad_ready, 1)

                def aggregate(s, j):
                    pe.wait_ge(msg_ready, s * NJ + j + 1)
                    for c in range(CHUNKS[j]):
                        last = nc.tensor.matmul(pAgg[:, 0:DIM + 4], OH[j][:, c, :], G[j][:, c, :],
                                                start=(j == 0 and c == 0), stop=(j == NJ - 1 and c == CHUNKS[j] - 1))
                    last.then_inc(agg_done[j], 1)

                with pe.Fori(0, TILES) as t:
                    n, s0 = tile_steps(pe, t)
                    pe.wait_ge(cur_ready, t + 1)
                    pe.sem_inc(passed, 1)
                    with pe.Fori(0, n) as g:
                        s = pe.snap(s0 + g)
                        destinations(s, 0)
                        destinations(s, 1)
                        freed(pe, acc_done, s)
                        aggregate(s, 0)
                        destinations(s, 2)
                        aggregate(s, 1)
                        aggregate(s, 2)


def finish(K, out):
    nc = K.nc
    with ExitStack() as stack:
        sb, pb, sem = K.tools(stack, "f")
        rows = [sb(f"rows{k}", [P, BODY, DIM]) for k in range(4)]
        rows_in = [sem(f"rows_in{b}") for b in range(2)]
        half = sem("half")
        done = sem("done")
        stored = sem("stored")
        with nc.Block() as block:
            @block.scalar
            def _(act):
                for i in range(TRIPS):
                    b = i % 2
                    if i >= 2:
                        act.wait_ge(done, (i - 1) * BODY)
                    for k in range(2):
                        a = k * NODEROWS + i * BODY * P
                        act.dma_start(rows[2 * b + k][:, :, :],
                                      K.YS[a:a + BODY * P, :].rearrange("(t p) d -> p t d", p=P)).then_inc(rows_in[b], 16)

            @block.vector
            def _(v):
                for i in range(TRIPS):
                    b = i % 2
                    v.wait_ge(rows_in[b], 32 * (i // 2 + 1))
                    for k in range(2):
                        if k:
                            v.wait_ge(half, (i + 1) * BODY)
                        for j in range(BODY):
                            t = i * BODY + j
                            nc.vector.scalar_tensor_tensor(K.X[:, t, :], rows[2 * b + k][:, j, :], K.WT[:, t, k:k + 1], K.X[:, t, :],
                                                           ALU.mult, ALU.add).then_inc(done if k else half, 1)

            @block.sync
            def _(sp):
                for i in range(TRIPS):
                    a, b = i * BODY, min((i + 1) * BODY, TILES - 1)
                    sp.wait_ge(done, (i + 1) * BODY)
                    sp.dma_start(out[a * P:b * P, :].rearrange("(t p) d -> p t d", p=P), K.X[:, a:b, :]).then_inc(stored, 16)
                sp.dma_start(out[(TILES - 1) * P:NODES, :], K.X[0:TAIL, TILES - 1, :]).then_inc(stored, 16)
                sp.wait_ge(stored, 16 * (TRIPS + 1))
                K.clear_last(sp)


_INS = ['x', 'src', 'dst', 'L0_gnn_weight', 'L0_gnn_attn_l', 'L0_gnn_attn_r', 'L0_ffn_router_w1', 'L0_ffn_router_b1',
        'L0_ffn_router_w2', 'L0_ffn_router_b2', 'L0_ffn_expert_w1', 'L0_ffn_expert_b1', 'L0_ffn_expert_w2',
        'L0_ffn_expert_b2', 'L0_ffn_expert_w3', 'L0_ffn_expert_b3', 'L1_gnn_W', 'L1_gnn_att_src', 'L1_gnn_att_dst',
        'L1_gnn_bias', 'L1_ffn_Wg', 'L1_ffn_bg', 'L1_ffn_W1', 'L1_ffn_b1', 'L1_ffn_W2', 'L1_ffn_b2']


def kernel(**inputs):
    import numpy as _np
    import concourse.bacc as _bacc
    from concourse import mybir as _mybir
    from concourse.bass_utils import run_bass_kernel_spmd as _run

    nc = _bacc.Bacc("TRN2", target_bir_lowering=False, num_devices=1)
    arrays, args = {}, {}
    for name in _INS:
        a = _np.ascontiguousarray(inputs[name])
        arrays[f"in_{name}_dram"] = a
        args[name] = nc.dram_tensor(f"in_{name}_dram", a.shape, _mybir.dt.from_np(a.dtype), kind="ExternalInput").ap()
    out = nc.dram_tensor("out_dram", (NODES, DIM), _mybir.dt.float32, kind="ExternalOutput").ap()
    gnn_moe(nc, out, **args)
    r = _run(nc, [arrays], core_ids=[0])
    return r.results[0]["out_dram"]
```
